# Optimizing a Trainium2 kernel written in Bass

```python
import numpy as np
import jax
import jax.numpy as jnp

def _softmax(x, axis=-1):
    return jax.nn.softmax(x, axis=axis)

def _gelu(x):
    return jax.nn.gelu(x, approximate=True)

def _silu(x):
    return jax.nn.silu(x)

def _sigmoid(x):
    return jax.nn.sigmoid(x)

def _layernorm(x, axis=-1, eps=1e-05):
    m = jnp.mean(x, axis=axis, keepdims=True)
    v = jnp.var(x, axis=axis, keepdims=True)
    return (x - m) / jnp.sqrt(v + eps)

def _scatter_add(tgt, idx, src, axis=0):
    return tgt.at[idx].add(src)

def _segment_sum(src, seg, n):
    return jax.ops.segment_sum(src, seg, n)
kernel_name = 'mk_flamingo_gated_d2_seqx_r8_3bfabf'

def setup_inputs(seed: int=0):
    np.random.seed(seed)
    _w = jnp.asarray

    def _rec_inputs():
        import jax
        import jax.numpy as jnp
        _rk = jax.random.key(seed)
        x = 7.22e-05 + 1 * jax.random.normal(jax.random.fold_in(_rk, 1), (16, 128, 256), jnp.float32)
        _lenS = 128 - jax.random.randint(jax.random.fold_in(_rk, 7), (16,), 0, max(1, 128 // 4) + 1, jnp.int32)
        _lenS2 = 128 - jax.random.randint(jax.random.fold_in(_rk, 8), (16,), 0, max(1, 128 // 4) + 1, jnp.int32)
        _ctx_2048P = jax.random.normal(jax.random.fold_in(_rk, 11), (16, 16, 256), jnp.float32)
        _ctx_2048c = jax.random.dirichlet(jax.random.fold_in(_rk, 511), 0.3 * jnp.ones((16,), jnp.float32), (16, 128))
        _ctx_2048t = jnp.einsum('bsk,bkd->bsd', _ctx_2048c, _ctx_2048P)
        _ctx_2048t = _ctx_2048t * jax.lax.rsqrt(jnp.mean(jnp.square(_ctx_2048t)) + 1e-12) * 0.953939
        ctx_2048 = 4.13588e-05 + 0.999923 * (_ctx_2048t + 0.3 * jax.random.normal(jax.random.fold_in(_rk, 611), (16, 128, 256), jnp.float32))
        _g = jax.random.normal(jax.random.fold_in(_rk, 9001), (2, 2), jnp.float32)
        _g = jnp.sign(_g) * jnp.maximum(jnp.abs(_g), 1.0) + (_g == 0) * 1.0
        g_xattn = _g[0]
        g_ffn = _g[1]
        return (x, ctx_2048, g_xattn, g_ffn)
    x, ctx_2048, g_xattn, g_ffn = _rec_inputs()

    def _L0_xattn_setup():
        import jax, jax.numpy as jnp
        import numpy as np
        NUM_FEATURES = 128
        NUM_HEADS = 16
        HEAD_DIM = NUM_FEATURES // NUM_HEADS
        B, SQ, SKV = (4, 256, 256)

        def _split_heads(x):
            b, s, _ = x.shape
            return x.reshape(b, s, NUM_HEADS, HEAD_DIM).transpose(0, 2, 1, 3)
        key = jax.random.key(seed)
        ks = jax.random.split(key, 8)
        w_scale = 1.0 / np.sqrt(NUM_FEATURES)
        return {'query': jax.random.normal(ks[0], (B, NUM_FEATURES, SQ), dtype=jnp.float32), 'key': jax.random.normal(ks[1], (B, NUM_FEATURES, SKV), dtype=jnp.float32), 'value': jax.random.normal(ks[2], (B, NUM_FEATURES, SKV), dtype=jnp.float32), 'Wq': jax.random.normal(ks[3], (NUM_FEATURES, NUM_FEATURES), dtype=jnp.float32) * w_scale, 'bq': jnp.zeros((NUM_FEATURES,), dtype=jnp.float32), 'Wk': jax.random.normal(ks[4], (NUM_FEATURES, NUM_FEATURES), dtype=jnp.float32) * w_scale, 'bk': jnp.zeros((NUM_FEATURES,), dtype=jnp.float32), 'Wv': jax.random.normal(ks[5], (NUM_FEATURES, NUM_FEATURES), dtype=jnp.float32) * w_scale, 'bv': jnp.zeros((NUM_FEATURES,), dtype=jnp.float32), 'Wo': jax.random.normal(ks[6], (NUM_FEATURES, NUM_FEATURES), dtype=jnp.float32) * w_scale, 'bo': jnp.zeros((NUM_FEATURES,), dtype=jnp.float32)}
    _L0_xattn_all = _L0_xattn_setup()
    _L0_xattn_in = {k: v for k, v in _L0_xattn_all.items() if k in ('Wq', 'bq', 'Wk', 'bk', 'Wv', 'bv', 'Wo', 'bo')}
    del _L0_xattn_all

    def _L0_ffn_setup():
        import jax, jax.numpy as jnp
        import numpy as np
        from jax import lax
        B, S, H = (1, 256, 256)
        E, I, TOP_K = (64, 64, 8)
        SHARED_I = 64
        key = jax.random.key(seed)
        ks = jax.random.split(key, 8)
        sc = 0.02
        return {'hidden_states': jax.random.normal(ks[0], (B, S, H), jnp.float32), 'router_w': jax.random.normal(ks[1], (E, H), jnp.float32) * sc, 'gate_up_proj': jax.random.normal(ks[2], (E, 2 * I, H), jnp.float32) * sc, 'down_proj': jax.random.normal(ks[3], (E, H, I), jnp.float32) * sc, 'shared_gate_w': jax.random.normal(ks[4], (SHARED_I, H), jnp.float32) * sc, 'shared_up_w': jax.random.normal(ks[5], (SHARED_I, H), jnp.float32) * sc, 'shared_down_w': jax.random.normal(ks[6], (H, SHARED_I), jnp.float32) * sc, 'shared_expert_gate_w': jax.random.normal(ks[7], (1, H), jnp.float32) * sc}
    _L0_ffn_all = _L0_ffn_setup()
    _L0_ffn_in = {k: v for k, v in _L0_ffn_all.items() if k in ('router_w', 'gate_up_proj', 'down_proj', 'shared_gate_w', 'shared_up_w', 'shared_down_w', 'shared_expert_gate_w')}
    del _L0_ffn_all

    def _L1_xattn_setup():
        import jax, jax.numpy as jnp
        import numpy as np
        B, S, E, NH = (2, 128, 256, 16)
        DH = E // NH
        EPS = 1e-06

        def _mlstm_forward(q, k, v, Wi, bi, Wf, bf, ln_scale):
            b, s, e = q.shape
            nh = Wi.shape[1]
            dh = e // nh
            x = jnp.concatenate([q, k, v], axis=-1)
            ig = (x @ Wi + bi).transpose(0, 2, 1)[..., None]
            fg = (x @ Wf + bf).transpose(0, 2, 1)[..., None]
            split = lambda t: t.reshape(b, s, nh, dh).transpose(0, 2, 1, 3)
            qh, kh, vh = (split(q), split(k), split(v))
            log_f = jax.nn.log_sigmoid(fg)
            log_f_cum = jnp.concatenate([jnp.zeros((b, nh, 1, 1), q.dtype), jnp.cumsum(log_f, axis=2)], axis=2)
            fg_mat = log_f_cum - jnp.transpose(log_f_cum, (0, 1, 3, 2))
            ltr = jnp.tril(jnp.ones((s, s), dtype=bool))
            log_fg = jnp.where(ltr, fg_mat[:, :, 1:, 1:], -jnp.inf)
            log_D = log_fg + jnp.transpose(ig, (0, 1, 3, 2))
            max_log_D = jnp.max(log_D, axis=-1, keepdims=True)
            D = jnp.exp(log_D - max_log_D)
            qk = jnp.einsum('bhsd,bhtd->bhst', qh, kh) / jnp.sqrt(jnp.asarray(dh, q.dtype))
            C = qk * D
            normalizer = jnp.maximum(jnp.abs(C.sum(-1, keepdims=True)), jnp.exp(-max_log_D))
            Cn = C / (normalizer + EPS)
            h = jnp.einsum('bhst,bhtd->bhsd', Cn, vh)
            mu = h.mean(-1, keepdims=True)
            var = ((h - mu) ** 2).mean(-1, keepdims=True)
            hn = (h - mu) * jax.lax.rsqrt(var + EPS)
            hn = hn * ln_scale.reshape(1, nh, 1, dh)
            return hn.transpose(0, 2, 1, 3).reshape(b, s, e)
        key = jax.random.key(seed)
        ks = jax.random.split(key, 6)
        q = jax.random.normal(ks[0], (B, S, E), dtype=jnp.float32)
        k = jax.random.normal(ks[1], (B, S, E), dtype=jnp.float32)
        v = jax.random.normal(ks[2], (B, S, E), dtype=jnp.float32)
        Wi = jax.random.normal(ks[3], (3 * E, NH), dtype=jnp.float32) * 0.02
        bi = jax.random.normal(ks[4], (NH,), dtype=jnp.float32) * 0.1
        Wf = jax.random.normal(ks[5], (3 * E, NH), dtype=jnp.float32) * 0.02
        bf = jnp.linspace(3.0, 6.0, NH, dtype=jnp.float32)
        ln_scale = jnp.ones((E,), dtype=jnp.float32)
        return {'q': q, 'k': k, 'v': v, 'Wi': Wi, 'bi': bi, 'Wf': Wf, 'bf': bf, 'ln_scale': ln_scale}
    _L1_xattn_all = _L1_xattn_setup()
    _L1_xattn_in = {k: v for k, v in _L1_xattn_all.items() if k in ('Wi', 'bi', 'Wf', 'bf', 'ln_scale')}
    del _L1_xattn_all

    def _L1_ffn_setup():
        import jax, jax.numpy as jnp
        import numpy as np
        import math
        B, S, D = (2, 256, 256)
        H, HD = (16, 128)
        E, I = (4, 256)
        TOP_K = 2
        ROPE_THETA = 10000.0

        def _layernorm(x, w, b):
            mu = jnp.mean(x, axis=-1, keepdims=True)
            var = jnp.mean(jnp.square(x - mu), axis=-1, keepdims=True)
            return (x - mu) * jax.lax.rsqrt(var + 1e-05) * w + b

        def _rotate_half(x):
            x1, x2 = jnp.split(x, 2, axis=-1)
            return jnp.concatenate((-x2, x1), axis=-1)

        def _attention(h, wq, bq, wk, bk, wv, bv, wo, bo):
            b, s, _ = h.shape
            q = (h @ wq + bq).reshape(b, s, H, HD).transpose(0, 2, 1, 3)
            k = (h @ wk + bk).reshape(b, s, H, HD).transpose(0, 2, 1, 3)
            v = (h @ wv + bv).reshape(b, s, H, HD).transpose(0, 2, 1, 3)
            inv_freq = 1.0 / ROPE_THETA ** (jnp.arange(0, HD, 2, dtype=jnp.float32) / HD)
            freqs = jnp.arange(s, dtype=jnp.float32)[:, None] * inv_freq[None, :]
            emb = jnp.concatenate((freqs, freqs), axis=-1)
            cos = jnp.cos(emb)[None, None]
            sin = jnp.sin(emb)[None, None]
            q = q * cos + _rotate_half(q) * sin
            k = k * cos + _rotate_half(k) * sin
            scores = jnp.einsum('bhqd,bhkd->bhqk', q, k) / math.sqrt(HD)
            causal = jnp.tril(jnp.ones((s, s), bool))
            scores = jnp.where(causal[None, None], scores, jnp.finfo(jnp.float32).min)
            probs = jax.nn.softmax(scores.astype(jnp.float32), axis=-1).astype(q.dtype)
            out = jnp.einsum('bhqk,bhkd->bhqd', probs, v)
            out = out.transpose(0, 2, 1, 3).reshape(b, s, H * HD)
            return out @ wo + bo

        def _moe(h, w_gate, we1, be1, we2, be2):
            b, s, d = h.shape
            x = h.reshape(-1, d)
            t = x.shape[0]
            raw = jax.nn.softmax(x @ w_gate, axis=-1)
            top_vals, top_idx = jax.lax.top_k(raw, TOP_K)
            w = jax.nn.softmax(top_vals, axis=-1)
            comb = jnp.zeros((t, E), x.dtype).at[jnp.arange(t)[:, None], top_idx].add(w)
            hmid = jax.nn.gelu(jnp.einsum('td,edi->tei', x, we1) + be1[None], approximate=False)
            eout = jnp.einsum('tei,eid->ted', hmid, we2) + be2[None]
            out = jnp.einsum('te,ted->td', comb, eout)
            return out.reshape(b, s, d)
        key = jax.random.key(seed)
        ks = jax.random.split(key, 20)
        s = 0.02
        p = {'hidden_states': jax.random.normal(ks[0], (B, S, D), jnp.float32), 'wq': jax.random.normal(ks[1], (D, H * HD), jnp.float32) * s, 'bq': jnp.zeros((H * HD,), jnp.float32), 'wk': jax.random.normal(ks[2], (D, H * HD), jnp.float32) * s, 'bk': jnp.zeros((H * HD,), jnp.float32), 'wv': jax.random.normal(ks[3], (D, H * HD), jnp.float32) * s, 'bv': jnp.zeros((H * HD,), jnp.float32), 'wo': jax.random.normal(ks[4], (H * HD, D), jnp.float32) * s, 'bo': jnp.zeros((D,), jnp.float32), 'ln1_w': jnp.ones((D,), jnp.float32), 'ln1_b': jnp.zeros((D,), jnp.float32), 'ln2_w': jnp.ones((D,), jnp.float32), 'ln2_b': jnp.zeros((D,), jnp.float32), 'w_gate': jax.random.normal(ks[5], (D, E), jnp.float32) * s, 'we1': jax.random.normal(ks[6], (E, D, I), jnp.float32) * s, 'be1': jnp.zeros((E, I), jnp.float32), 'we2': jax.random.normal(ks[7], (E, I, D), jnp.float32) * s, 'be2': jnp.zeros((E, D), jnp.float32)}
        return p
    _L1_ffn_all = _L1_ffn_setup()
    _L1_ffn_in = {k: v for k, v in _L1_ffn_all.items() if k in ('wq', 'bq', 'wk', 'bk', 'wv', 'bv', 'wo', 'bo', 'ln1_w', 'ln1_b', 'ln2_w', 'ln2_b', 'w_gate', 'we1', 'be1', 'we2', 'be2')}
    del _L1_ffn_all
    return {'x': x, 'ctx_2048': ctx_2048, 'g_xattn': g_xattn, 'g_ffn': g_ffn, 'L0_xattn_Wq': _L0_xattn_in['Wq'], 'L0_xattn_bq': _L0_xattn_in['bq'], 'L0_xattn_Wk': _L0_xattn_in['Wk'], 'L0_xattn_bk': _L0_xattn_in['bk'], 'L0_xattn_Wv': _L0_xattn_in['Wv'], 'L0_xattn_bv': _L0_xattn_in['bv'], 'L0_xattn_Wo': _L0_xattn_in['Wo'], 'L0_xattn_bo': _L0_xattn_in['bo'], 'L0_ffn_router_w': _L0_ffn_in['router_w'], 'L0_ffn_gate_up_proj': _L0_ffn_in['gate_up_proj'], 'L0_ffn_down_proj': _L0_ffn_in['down_proj'], 'L0_ffn_shared_gate_w': _L0_ffn_in['shared_gate_w'], 'L0_ffn_shared_up_w': _L0_ffn_in['shared_up_w'], 'L0_ffn_shared_down_w': _L0_ffn_in['shared_down_w'], 'L0_ffn_shared_expert_gate_w': _L0_ffn_in['shared_expert_gate_w'], 'L1_xattn_Wi': _L1_xattn_in['Wi'], 'L1_xattn_bi': _L1_xattn_in['bi'], 'L1_xattn_Wf': _L1_xattn_in['Wf'], 'L1_xattn_bf': _L1_xattn_in['bf'], 'L1_xattn_ln_scale': _L1_xattn_in['ln_scale'], 'L1_ffn_wq': _L1_ffn_in['wq'], 'L1_ffn_bq': _L1_ffn_in['bq'], 'L1_ffn_wk': _L1_ffn_in['wk'], 'L1_ffn_bk': _L1_ffn_in['bk'], 'L1_ffn_wv': _L1_ffn_in['wv'], 'L1_ffn_bv': _L1_ffn_in['bv'], 'L1_ffn_wo': _L1_ffn_in['wo'], 'L1_ffn_bo': _L1_ffn_in['bo'], 'L1_ffn_ln1_w': _L1_ffn_in['ln1_w'], 'L1_ffn_ln1_b': _L1_ffn_in['ln1_b'], 'L1_ffn_ln2_w': _L1_ffn_in['ln2_w'], 'L1_ffn_ln2_b': _L1_ffn_in['ln2_b'], 'L1_ffn_w_gate': _L1_ffn_in['w_gate'], 'L1_ffn_we1': _L1_ffn_in['we1'], 'L1_ffn_be1': _L1_ffn_in['be1'], 'L1_ffn_we2': _L1_ffn_in['we2'], 'L1_ffn_be2': _L1_ffn_in['be2']}

def reference(x, ctx_2048, g_xattn, g_ffn, L0_xattn_Wq, L0_xattn_bq, L0_xattn_Wk, L0_xattn_bk, L0_xattn_Wv, L0_xattn_bv, L0_xattn_Wo, L0_xattn_bo, L0_ffn_router_w, L0_ffn_gate_up_proj, L0_ffn_down_proj, L0_ffn_shared_gate_w, L0_ffn_shared_up_w, L0_ffn_shared_down_w, L0_ffn_shared_expert_gate_w, L1_xattn_Wi, L1_xattn_bi, L1_xattn_Wf, L1_xattn_bf, L1_xattn_ln_scale, L1_ffn_wq, L1_ffn_bq, L1_ffn_wk, L1_ffn_bk, L1_ffn_wv, L1_ffn_bv, L1_ffn_wo, L1_ffn_bo, L1_ffn_ln1_w, L1_ffn_ln1_b, L1_ffn_ln2_w, L1_ffn_ln2_b, L1_ffn_w_gate, L1_ffn_we1, L1_ffn_be1, L1_ffn_we2, L1_ffn_be2):
    import jax
    import jax.numpy as jnp

    def _L0_xattn_ref(query, key, value, Wq, bq, Wk, bk, Wv, bv, Wo, bo):
        import jax, jax.numpy as jnp
        import numpy as np
        NUM_FEATURES = 128
        NUM_HEADS = 16
        HEAD_DIM = NUM_FEATURES // NUM_HEADS
        B, SQ, SKV = (4, 256, 256)

        def _split_heads(x):
            b, s, _ = x.shape
            return x.reshape(b, s, NUM_HEADS, HEAD_DIM).transpose(0, 2, 1, 3)
        q_in = query.transpose(0, 2, 1)
        k_in = key.transpose(0, 2, 1)
        v_in = value.transpose(0, 2, 1)
        q = _split_heads(jnp.einsum('bsf,of->bso', q_in, Wq) + bq)
        k = _split_heads(jnp.einsum('bsf,of->bso', k_in, Wk) + bk)
        v = _split_heads(jnp.einsum('bsf,of->bso', v_in, Wv) + bv)
        scale = 1.0 / jnp.sqrt(jnp.float32(NUM_FEATURES))
        scores = jnp.einsum('bhqd,bhkd->bhqk', q, k) * scale
        attn = jax.nn.softmax(scores, axis=-1)
        out = jnp.einsum('bhqk,bhkd->bhqd', attn, v)
        b = out.shape[0]
        out = out.transpose(0, 2, 1, 3).reshape(b, -1, NUM_FEATURES)
        out = jnp.einsum('bsf,of->bso', out, Wo) + bo
        return out.transpose(0, 2, 1)

    def _L0_ffn_ref(hidden_states, router_w, gate_up_proj, down_proj, shared_gate_w, shared_up_w, shared_down_w, shared_expert_gate_w):
        import jax, jax.numpy as jnp
        import numpy as np
        from jax import lax
        B, S, H = (1, 256, 256)
        E, I, TOP_K = (64, 64, 8)
        SHARED_I = 64
        b, s, h_dim = hidden_states.shape
        h = hidden_states.reshape(-1, h_dim)
        T = h.shape[0]
        shared = jnp.dot(jax.nn.silu(jnp.dot(h, shared_gate_w.T)) * jnp.dot(h, shared_up_w.T), shared_down_w.T)
        shared = jax.nn.sigmoid(jnp.dot(h, shared_expert_gate_w.T)) * shared
        logits = jnp.dot(h, router_w.T)
        probs = jax.nn.softmax(logits.astype(jnp.float32), axis=-1)
        top_vals, top_idx = lax.top_k(probs, TOP_K)
        top_vals = top_vals / jnp.sum(top_vals, axis=-1, keepdims=True)
        top_vals = top_vals.astype(h.dtype)
        comb = jnp.zeros((T, E), h.dtype).at[jnp.arange(T)[:, None], top_idx].add(top_vals)

        def body(acc, xs):
            wgu, wd, w_e = xs
            g, u = jnp.split(jnp.dot(h, wgu.T), 2, axis=-1)
            eo = jnp.dot(jax.nn.silu(g) * u, wd.T)
            return (acc + eo * w_e[:, None], None)
        expert_out, _ = lax.scan(body, jnp.zeros_like(h), (gate_up_proj, down_proj, comb.T))
        return (expert_out + shared).reshape(b, s, h_dim)

    def _L1_xattn_ref(q, k, v, Wi, bi, Wf, bf, ln_scale):
        import jax, jax.numpy as jnp
        import numpy as np
        B, S, E, NH = (2, 128, 256, 16)
        DH = E // NH
        EPS = 1e-06

        def _mlstm_forward(q, k, v, Wi, bi, Wf, bf, ln_scale):
            b, s, e = q.shape
            nh = Wi.shape[1]
            dh = e // nh
            x = jnp.concatenate([q, k, v], axis=-1)
            ig = (x @ Wi + bi).transpose(0, 2, 1)[..., None]
            fg = (x @ Wf + bf).transpose(0, 2, 1)[..., None]
            split = lambda t: t.reshape(b, s, nh, dh).transpose(0, 2, 1, 3)
            qh, kh, vh = (split(q), split(k), split(v))
            log_f = jax.nn.log_sigmoid(fg)
            log_f_cum = jnp.concatenate([jnp.zeros((b, nh, 1, 1), q.dtype), jnp.cumsum(log_f, axis=2)], axis=2)
            fg_mat = log_f_cum - jnp.transpose(log_f_cum, (0, 1, 3, 2))
            ltr = jnp.tril(jnp.ones((s, s), dtype=bool))
            log_fg = jnp.where(ltr, fg_mat[:, :, 1:, 1:], -jnp.inf)
            log_D = log_fg + jnp.transpose(ig, (0, 1, 3, 2))
            max_log_D = jnp.max(log_D, axis=-1, keepdims=True)
            D = jnp.exp(log_D - max_log_D)
            qk = jnp.einsum('bhsd,bhtd->bhst', qh, kh) / jnp.sqrt(jnp.asarray(dh, q.dtype))
            C = qk * D
            normalizer = jnp.maximum(jnp.abs(C.sum(-1, keepdims=True)), jnp.exp(-max_log_D))
            Cn = C / (normalizer + EPS)
            h = jnp.einsum('bhst,bhtd->bhsd', Cn, vh)
            mu = h.mean(-1, keepdims=True)
            var = ((h - mu) ** 2).mean(-1, keepdims=True)
            hn = (h - mu) * jax.lax.rsqrt(var + EPS)
            hn = hn * ln_scale.reshape(1, nh, 1, dh)
            return hn.transpose(0, 2, 1, 3).reshape(b, s, e)
        return _mlstm_forward(q, k, v, Wi, bi, Wf, bf, ln_scale)

    def _L1_ffn_ref(hidden_states, wq, bq, wk, bk, wv, bv, wo, bo, ln1_w, ln1_b, ln2_w, ln2_b, w_gate, we1, be1, we2, be2):
        import jax, jax.numpy as jnp
        import numpy as np
        import math
        B, S, D = (2, 256, 256)
        H, HD = (16, 128)
        E, I = (4, 256)
        TOP_K = 2
        ROPE_THETA = 10000.0

        def _layernorm(x, w, b):
            mu = jnp.mean(x, axis=-1, keepdims=True)
            var = jnp.mean(jnp.square(x - mu), axis=-1, keepdims=True)
            return (x - mu) * jax.lax.rsqrt(var + 1e-05) * w + b

        def _rotate_half(x):
            x1, x2 = jnp.split(x, 2, axis=-1)
            return jnp.concatenate((-x2, x1), axis=-1)

        def _attention(h, wq, bq, wk, bk, wv, bv, wo, bo):
            b, s, _ = h.shape
            q = (h @ wq + bq).reshape(b, s, H, HD).transpose(0, 2, 1, 3)
            k = (h @ wk + bk).reshape(b, s, H, HD).transpose(0, 2, 1, 3)
            v = (h @ wv + bv).reshape(b, s, H, HD).transpose(0, 2, 1, 3)
            inv_freq = 1.0 / ROPE_THETA ** (jnp.arange(0, HD, 2, dtype=jnp.float32) / HD)
            freqs = jnp.arange(s, dtype=jnp.float32)[:, None] * inv_freq[None, :]
            emb = jnp.concatenate((freqs, freqs), axis=-1)
            cos = jnp.cos(emb)[None, None]
            sin = jnp.sin(emb)[None, None]
            q = q * cos + _rotate_half(q) * sin
            k = k * cos + _rotate_half(k) * sin
            scores = jnp.einsum('bhqd,bhkd->bhqk', q, k) / math.sqrt(HD)
            causal = jnp.tril(jnp.ones((s, s), bool))
            scores = jnp.where(causal[None, None], scores, jnp.finfo(jnp.float32).min)
            probs = jax.nn.softmax(scores.astype(jnp.float32), axis=-1).astype(q.dtype)
            out = jnp.einsum('bhqk,bhkd->bhqd', probs, v)
            out = out.transpose(0, 2, 1, 3).reshape(b, s, H * HD)
            return out @ wo + bo

        def _moe(h, w_gate, we1, be1, we2, be2):
            b, s, d = h.shape
            x = h.reshape(-1, d)
            t = x.shape[0]
            raw = jax.nn.softmax(x @ w_gate, axis=-1)
            top_vals, top_idx = jax.lax.top_k(raw, TOP_K)
            w = jax.nn.softmax(top_vals, axis=-1)
            comb = jnp.zeros((t, E), x.dtype).at[jnp.arange(t)[:, None], top_idx].add(w)
            hmid = jax.nn.gelu(jnp.einsum('td,edi->tei', x, we1) + be1[None], approximate=False)
            eout = jnp.einsum('tei,eid->ted', hmid, we2) + be2[None]
            out = jnp.einsum('te,ted->td', comb, eout)
            return out.reshape(b, s, d)
        a = _attention(_layernorm(hidden_states, ln1_w, ln1_b), wq, bq, wk, bk, wv, bv, wo, bo)
        h = hidden_states + a
        m = _moe(_layernorm(h, ln2_w, ln2_b), w_gate, we1, be1, we2, be2)
        return h + m
    x = x + jnp.tanh(g_xattn[0]) * _L0_xattn_ref(_layernorm(x, axis=-1), ctx_2048, ctx_2048, L0_xattn_Wq, L0_xattn_bq, L0_xattn_Wk, L0_xattn_bk, L0_xattn_Wv, L0_xattn_bv, L0_xattn_Wo, L0_xattn_bo)
    x = x + jnp.tanh(g_ffn[0]) * _L0_ffn_ref(_layernorm(x, axis=-1), L0_ffn_router_w, L0_ffn_gate_up_proj, L0_ffn_down_proj, L0_ffn_shared_gate_w, L0_ffn_shared_up_w, L0_ffn_shared_down_w, L0_ffn_shared_expert_gate_w)
    x = x + jnp.tanh(g_xattn[1]) * _L1_xattn_ref(_layernorm(x, axis=-1), ctx_2048, ctx_2048, L1_xattn_Wi, L1_xattn_bi, L1_xattn_Wf, L1_xattn_bf, L1_xattn_ln_scale)
    x = x + jnp.tanh(g_ffn[1]) * _L1_ffn_ref(_layernorm(x, axis=-1), L1_ffn_wq, L1_ffn_bq, L1_ffn_wk, L1_ffn_bk, L1_ffn_wv, L1_ffn_bv, L1_ffn_wo, L1_ffn_bo, L1_ffn_ln1_w, L1_ffn_ln1_b, L1_ffn_ln2_w, L1_ffn_ln2_b, L1_ffn_w_gate, L1_ffn_we1, L1_ffn_be1, L1_ffn_we2, L1_ffn_be2)
    return x

_drawn_inputs = setup_inputs


def setup_inputs(seed=0):
    import zlib

    import numpy as np

    out = dict(_drawn_inputs(seed))
    spreads = {'g_ffn': (-1.0, 0.2),
     'L0_xattn_bq': (0.0, 0.284),
     'L0_xattn_bk': (0.0, 2.0),
     'L0_xattn_bv': (0.0, 0.1),
     'L0_xattn_bo': (0.0, 0.1),
     'L1_xattn_ln_scale': (1.0, 0.2),
     'L1_ffn_bq': (0.0, 0.661),
     'L1_ffn_bk': (0.0, 0.8),
     'L1_ffn_bv': (0.0, 0.1),
     'L1_ffn_bo': (0.0, 0.1),
     'L1_ffn_ln1_w': (1.0, 0.2),
     'L1_ffn_ln1_b': (0.0, 0.1),
     'L1_ffn_ln2_w': (1.0, 0.2),
     'L1_ffn_ln2_b': (0.0, 0.1),
     'L1_ffn_be1': (0.0, 0.1),
     'L1_ffn_be2': (0.0, 0.1)}
    factors = {'L0_ffn_router_w': 3.394,
     'L0_ffn_gate_up_proj': 3.338,
     'L0_ffn_down_proj': 3.003,
     'L0_ffn_shared_gate_w': 4.646,
     'L0_ffn_shared_up_w': 4.063,
     'L0_ffn_shared_down_w': 4.422,
     'L0_ffn_shared_expert_gate_w': 8.0,
     'L1_xattn_bi': 64.0}
    for name, (base, spread) in spreads.items():
        noise = np.random.default_rng([zlib.crc32(name.encode()), seed]).standard_normal(out[name].shape)
        drawn = base * np.exp(spread * noise) if base else spread * noise
        out[name] = jnp.asarray(drawn.astype(out[name].dtype))
    for name, factor in factors.items():
        out[name] = (out[name] * factor).astype(out[name].dtype)
    return out
```

```python
from contextlib import ExitStack

import numpy as np

import concourse.bass as bass
from concourse import mybir

F32 = mybir.dt.float32
BF16 = mybir.dt.bfloat16
ALU = mybir.AluOpType
ACT = mybir.ActivationFunctionType
AX = mybir.AxisListType

P = 128
NB, S, D = 16, 128, 256
T = NB * S
DK = D // P
EPS_LN = 1e-5
BANK = 512


class Tally:

    def __init__(self, name, sem):
        self.name, self.sem, self.count = name, sem, 0

    def mark(self, instruction, by=1):
        instruction.then_inc(self.sem, by)
        self.count += by
        return (self, self.count)


class Core:

    def __init__(self, nc, stack):
        self.nc, self.stack = nc, stack
        self.reached = {}
        self.pe, self.act, self.dve, self.pool = (self.tally(n) for n in ("pe_done", "act_done", "dve_done", "pool_done"))
        self.banks = [stack.enter_context(nc.psum_tensor(f"bank{i}", [P, BANK], F32)) for i in range(8)]

    def tally(self, name):
        return Tally(name, self.stack.enter_context(self.nc.semaphore(name)))

    def sbuf(self, stack, name, shape, dtype=F32):
        return stack.enter_context(self.nc.sbuf_tensor(name, shape, dtype))

    def need(self, engine, *marks):
        for mark in marks:
            if mark is None:
                continue
            tally, value = mark
            key = (engine.engine, tally.name)
            if self.reached.get(key, 0) < value:
                engine.wait_ge(tally.sem, value)
                self.reached[key] = value

    def on_pe(self, make, *marks):
        self.need(self.nc.tensor, *marks)
        return self.pe.mark(make(self.nc.tensor))

    def on_act(self, make, *marks):
        self.need(self.nc.scalar, *marks)
        return self.act.mark(make(self.nc.scalar))

    def on_dve(self, make, *marks):
        self.need(self.nc.vector, *marks)
        return self.dve.mark(make(self.nc.vector))

    def on_pool(self, make, *marks):
        self.need(self.nc.gpsimd, (self.pool, self.pool.count), *marks)
        return self.pool.mark(make(self.nc.gpsimd))

    def load(self, dst, src, tally, *marks, queue=None):
        queue = queue or self.nc.sync
        self.need(queue, *marks)
        return tally.mark(queue.dma_start(dst, src), 16)

    def now(self):
        return [(t, t.count) for t in (self.pe, self.act, self.dve, self.pool) if t.count]

    def join(self, *more):
        marks = self.now() + list(more)
        for engine in (self.nc.tensor, self.nc.scalar, self.nc.vector, self.nc.gpsimd, self.nc.sync):
            self.need(engine, *marks)


def row_norm(c, w, tag, src, dst, ready, tiles=NB, eps=EPS_LN):
    stats = c.sbuf(w, f"{tag}_stats", [P, tiles, 6])
    mean_var = c.sbuf(w, f"{tag}_mean_var", [P, tiles, 2])
    rstd = c.sbuf(w, f"{tag}_rstd", [P, tiles])
    last = None
    for b in range(tiles):
        m = c.on_dve(lambda e: e.bn_stats(stats[:, b, :], src[:, b, :]), ready[b])
    for b in range(tiles):
        last = c.on_dve(lambda e: e.bn_aggr(mean_var[:, b, :], stats[:, b, :]), m)
    last = c.on_dve(lambda e: e.tensor_scalar(rstd[:, :], mean_var[:, :, 1], eps, None, ALU.add), last)
    root = c.on_act(lambda e: e.activation(rstd[:, :], rstd[:, :], ACT.Sqrt), last)
    inv = c.on_dve(lambda e: e.reciprocal(rstd[:, :], rstd[:, :]), root)
    return [c.on_dve(lambda e: e.tensor_scalar(dst[:, b, :], src[:, b, :], mean_var[:, b, 0:1], rstd[:, b:b + 1],
                                               ALU.subtract, ALU.mult), inv) for b in range(tiles)]


def to_columns(c, src, dst, ready, scale=None, bias=None, vectors_in=None, banks=(0, 1, 2, 3)):
    out, freed = [], {}
    for b in range(NB):
        bank = c.banks[banks[b % len(banks)]]
        for k in range(DK):
            t = c.on_pe(lambda e: e.transpose(bank[:, k * P:(k + 1) * P], src[:, b, k * P:(k + 1) * P], c.ident[:, :]),
                        ready[b], c.ident_ready, *freed.get(b % len(banks), ()))
        if scale is None:
            copy = lambda e: e.tensor_copy(dst[:, :, b * P:(b + 1) * P], bank[:, 0:DK * P].rearrange("p (k n) -> p k n", k=DK))
            marks = [c.on_dve(copy, t) if b % 2 else
                     c.on_act(lambda e: e.copy(dst[:, :, b * P:(b + 1) * P], bank[:, 0:DK * P].rearrange("p (k n) -> p k n", k=DK)), t)]
        else:
            marks = [c.on_act(lambda e: e.activation(dst[:, 0, b * P:(b + 1) * P], bank[:, 0:P], ACT.Identity,
                                                     bias=bias[:, 0:1], scale=scale[:, 0:1]), t, vectors_in),
                     c.on_act(lambda e: e.activation(dst[:, 1, b * P:(b + 1) * P], bank[:, P:2 * P], ACT.Identity,
                                                     bias=bias[:, 1:2], scale=scale[:, 1:2]), t, vectors_in)]
        freed[b % len(banks)] = marks
        out.append(marks[-1])
    return out


HEADS, HD = 16, 8
POS = D
QPART = (0, 0, 0, 1, 1, 1, 2, 2, 2)
KPART = (0, 1, 2, 0, 1, 2, 0, 1, 2)
TERM_ROWS = len(QPART) * HD
MAX_ROWS = 3
TILES = 4


def split3(c, on, whole, parts, ready):
    m = on(lambda e: e.tensor_tensor(whole, whole, parts[:, 0, :], ALU.subtract), *ready)
    m = on(lambda e: e.tensor_copy(parts[:, 1, :], whole), m)
    return on(lambda e: e.tensor_tensor(parts[:, 2, :], whole, parts[:, 1, :], ALU.subtract), m)


def layer0_attention(c, io):
    nc, resid, ctx = c.nc, c.resid, c.ctx
    with ExitStack() as w:
        sb = lambda name, shape, dtype=F32: c.sbuf(w, name, shape, dtype)
        wqT, wkT, wvT, woT = (sb(f"a_{n}", [P, P]) for n in ("wqT", "wkT", "wvT", "woT"))
        bias = sb("a_bias", [P, 4])
        normed = sb("a_normed", [P, NB, D])
        vaug = sb("a_vaug", [P, NB, 2, HEADS, HD + 1])
        whole = [sb(f"a_whole{i}", [P, 2, BANK]) for i in range(2)]
        parts = [sb(f"a_parts{i}", [P, 2, 3, BANK], BF16) for i in range(2)]
        RING = 4
        rows = TERM_ROWS + MAX_ROWS
        qs = [sb(f"a_qs{i}", [rows, HEADS, POS], BF16) for i in range(RING)]
        ks = [sb(f"a_ks{i}", [96, HEADS, POS], BF16) for i in range(RING)]
        negmax = [sb(f"a_negmax{i}", [P, HEADS, 2]) for i in range(2)]
        mrow = [sb(f"a_mrow{i}", [32, P]) for i in range(2)]
        mparts = [sb(f"a_mparts{i}", [32, 3, P], BF16) for i in range(2)]
        EXPS = 8
        expo = [sb(f"a_exp{i}", [P, 2, POS]) for i in range(EXPS)]
        inv = [sb(f"a_inv{i}", [P, 2, TILES]) for i in range(2)]
        outq = [sb(f"a_outq{i}", [P, 2, HEADS, HD]) for i in range(2)]
        sumT = [sb(f"a_sumT{i}", [P, POS]) for i in range(2)]
        outT = [sb(f"a_outT{i}", [P, POS]) for i in range(2)]
        proj = [sb(f"a_proj{i}", [P, POS]) for i in range(2)]

        weights_in, x_in, ctx_in = c.tally("a_weights_in"), c.x_in, c.ctx_in
        for dst, name in ((wqT, "wqT"), (wkT, "wkT"), (wvT, "wvT"), (woT, "woT")):
            c.load(dst[:, :], io["a_" + name], weights_in)
        weights = c.load(bias[:, :], io["a_bias"], weights_in)

        ones = c.on_dve(lambda e: e.memset(vaug[:, :, :, :, HD], 1.0))
        for r in range(RING):
            ks_ones = c.on_pool(lambda e: e.memset(ks[r][64:96, :, :], 1.0))

        norm = row_norm(c, w, "a", resid, normed, x_in)
        split_out = {n: [c.tally(f"a_{n}_out{i}") for i in range(NB // 2)] for n in "qk"}
        stored = {}
        freed = {}
        for i in range(NB // 2):
            r = i % 2
            cols = slice(i * BANK, (i + 1) * BANK)
            for n, (wT, src, b, on) in enumerate(((wqT, normed, 0, c.on_dve), (wkT, ctx, 1, c.on_pool))):
                bank = c.banks[n + 4 * r]
                pe = c.on_pe(lambda e: e.matmul(bank[:, :], wT[:, :], src[:, 2 * i:2 * i + 2, :].rearrange("p b n -> p (b n)"),
                                                start=True, stop=True),
                             weights, norm[2 * i + 1] if n == 0 else None, *(ctx_in[2 * i:2 * i + 2] if n else ()),
                             freed.get((n, r)))
                c.on_act(lambda e: e.activation(whole[r][:, n, :], bank[:, :], ACT.Identity, bias=bias[:, b:b + 1]),
                         pe, stored.get((n, i - 2)))
                act = c.on_act(lambda e: e.activation(parts[r][:, n, 0, :], bank[:, :], ACT.Identity, bias=bias[:, b:b + 1]))
                freed[n, r] = act
                done = split3(c, on, whole[r][:, n, :], parts[r][:, n, :, :], (act,))
                name = "qk"[n]
                stored[n, i] = c.load(io[f"a_{name}_parts"][:, :, cols].rearrange("t p n -> p t n"), parts[r][:, n, :, :],
                                      split_out[name][i], done)
            bank = c.banks[2 + 4 * r]
            for j in range(4):
                b, kb = 2 * i + j // 2, j % 2
                pe = c.on_pe(lambda e: e.matmul(bank[:, j * P:(j + 1) * P], ctx[:, b, kb * P:(kb + 1) * P], wvT[:, :],
                                                start=True, stop=True), freed.get(("v", r)))
            freed["v", r] = v_ready = c.on_dve(
                lambda e: e.tensor_copy(vaug[:, 2 * i:2 * i + 2, :, :, 0:HD].rearrange("p b k h d -> p (b k) h d"),
                                        bank[:, :].rearrange("p (j h d) -> p j h d", j=4, h=HEADS)), pe, ones)
        bank_free = {n: c.now() for n in range(8)}

        stack_in = [c.tally(f"a_stack_in{i}") for i in range(RING)]
        max_in = [c.tally(f"a_max_in{i}") for i in range(RING)]
        by_head = {n: io[f"a_{n}_parts"].rearrange("t (h d) n -> t d h n", d=HD) for n in "qk"}

        def stack(b, *free):
            r, cols = b % RING, slice(b * POS, (b + 1) * POS)
            for t in range(len(QPART)):
                c.load(qs[r][t * HD:(t + 1) * HD, :, :], by_head["q"][QPART[t], :, :, cols], stack_in[r],
                       stored[0, b // 2], stored[1, b // 2], ks_ones, *free)
                m = c.load(ks[r][t * HD:(t + 1) * HD, :, :], by_head["k"][KPART[t], :, :, cols], stack_in[r])
            return m

        stacked, max_rows, max_done, row_ready, mfree = {}, {}, {}, {}, {}

        def score_max(b, j):
            for qb in range(2):
                for half in range(2):
                    h = 2 * j + half
                    pe = c.on_pe(lambda e: e.matmul(
                        c.banks[half][:, qb * POS:(qb + 1) * POS], qs[b % RING][0:TERM_ROWS, h, qb * P:(qb + 1) * P],
                        ks[b % RING][0:TERM_ROWS, h, :], start=True, stop=True), stacked[b], *bank_free[half])
            for half in range(2):
                m = c.on_dve(lambda e: e.tensor_reduce(negmax[b % 2][:, 2 * j + half, :], c.banks[half][:, :].rearrange("p (q n) -> p q n", q=2),
                                                       AX.X, ALU.max, negate=True), pe, mfree.get(b % 2))
                bank_free[half] = [m]
            max_done[b] = m

        def max_to_rows(b):
            i, bank = b % 2, c.banks[7]
            pe = c.on_pe(lambda e: e.transpose(bank[0:32, 0:P], negmax[i][:, :, :].rearrange("p h q -> p (h q)"), c.ident[:, :]),
                         max_done[b], c.ident_ready, *bank_free[7])
            mfree[i] = pe
            c.on_act(lambda e: e.copy(mrow[i][:, :], bank[0:32, 0:P]), pe, max_rows.get(b - 2))
            a = c.on_act(lambda e: e.copy(mparts[i][:, 0, :], bank[0:32, 0:P]))
            bank_free[7] = [a]
            done = split3(c, c.on_pool, mrow[i][:, :], mparts[i][:, :, :], (a,))
            for part in range(MAX_ROWS):
                row = TERM_ROWS + part
                max_rows[b] = c.load(qs[b % RING][row:row + 1, :, :].rearrange("o h (q n) -> o (h q) n", q=2),
                                     mparts[i][:, part, :], max_in[b % RING], done)

        exp_done, exp_free, added, divided = {}, {}, {}, {}
        GROUPS = HEADS // TILES

        def exponentials(b, j):
            for kb in range(2):
                for half in range(2):
                    h, bank = 2 * j + half, 2 + half
                    pe = c.on_pe(lambda e: e.matmul(
                        c.banks[bank][:, kb * POS:(kb + 1) * POS], ks[b % RING][0:rows, h, kb * P:(kb + 1) * P],
                        qs[b % RING][0:rows, h, :], start=True, stop=True), max_rows[b], *bank_free[bank])
            for half in range(2):
                h, bank = 2 * j + half, 2 + half
                n = (b * HEADS + h) % EXPS
                exp_done[b, h] = c.on_act(lambda e: e.activation(expo[n][:, :, :].rearrange("p k q -> p (k q)"), c.banks[bank][:, :], ACT.Exp,
                                                                 scale=float(1 / np.sqrt(np.float32(P)))), pe, exp_free.get(n))
                bank_free[bank] = [exp_done[b, h]]

        def times_v(b, g):
            bank = 4 + g % 2
            for kb in range(2):
                for tile in range(TILES):
                    h = TILES * g + tile
                    n = (b * HEADS + h) % EXPS
                    pe = c.on_pe(lambda e: e.matmul(
                        c.banks[bank][32 * tile:32 * tile + HD + 1, 0:POS], vaug[:, b, kb, h, :], expo[n][:, kb, :],
                        start=kb == 0, stop=kb == 1), exp_done[b, h], v_ready, *bank_free[bank])
                    if kb == 1:
                        exp_free[n] = pe
            a = c.on_act(lambda e: e.copy(sumT[g % 2][:, :], c.banks[bank][:, 0:POS]), pe, divided.get((b, g - 2), divided.get((b - 1, g + 2))))
            bank_free[bank] = [a]
            return a

        def normalise(b, g, copied):
            i, bank = b % 2, c.banks[6]
            for qb in range(2):
                pe = c.on_pe(lambda e: e.transpose(bank[:, qb * P:(qb + 1) * P], sumT[g % 2][:, qb * P:(qb + 1) * P], c.ident[:, :]),
                             copied, *bank_free[6])
            view = bank[:, 0:2 * P].rearrange("p (q h d) -> p q h d", q=2, h=TILES)
            m = c.on_dve(lambda e: e.reciprocal(inv[g % 2][:, :, :], view[:, :, :, HD]), pe)
            m = c.on_dve(lambda e: e.tensor_tensor(outq[i][:, :, TILES * g:TILES * (g + 1), :], view[:, :, :, 0:HD],
                                                   inv[g % 2][:, :, :].unsqueeze(3).to_broadcast([P, 2, TILES, HD]), ALU.mult), m, added.get(b - 2))
            bank_free[6] = [m]
            divided[b, g] = pe
            return m

        def to_features(b, ready):
            i, bank = b % 2, c.banks[7]
            for qb in range(2):
                pe = c.on_pe(lambda e: e.transpose(bank[:, qb * P:(qb + 1) * P], outq[i][:, qb, :, :].rearrange("p h d -> p (h d)"),
                                                   c.ident[:, :]), ready, *bank_free[7])
            a = c.on_act(lambda e: e.activation(outT[i][:, :], bank[:, 0:POS], ACT.Identity, bias=bias[:, 2:3]), pe)
            bank_free[7] = [a]
            return a

        def residual(b, ready):
            i, bank = b % 2, c.banks[7]
            pe = c.on_pe(lambda e: e.matmul(bank[:, 0:POS], woT[:, :], outT[i][:, :], start=True, stop=True), ready, *bank_free[7])
            a = c.on_act(lambda e: e.activation(proj[i][:, :], bank[:, 0:POS], ACT.Identity, bias=bias[:, 3:4]), pe, added.get(b - 2))
            bank_free[7] = [a]
            added[b] = c.on_dve(lambda e: e.scalar_tensor_tensor(resid[:, b, :], proj[i][:, :], c.gates[:, 0:1], resid[:, b, :],
                                                                 ALU.mult, ALU.add), a, c.gates_ready)

        for bank in (4, 5):
            bank_free[bank] = bank_free[bank] + [c.on_dve(lambda e: e.memset(c.banks[bank][:, :], 0.0), *bank_free[bank])]

        PAIRS = HEADS // 2
        for b in range(min(RING, NB)):
            stacked[b] = stack(b)
        for b in range(2):
            for j in range(PAIRS):
                score_max(b, j)
            max_to_rows(b)
        copied, ended = {}, {}
        for n in range(NB * PAIRS + 6):
            b, j = divmod(n, PAIRS)
            if b + 2 < NB:
                score_max(b + 2, j)
            if b < NB:
                exponentials(b, j)
            if n % 2 == 0 and 2 <= n < NB * PAIRS + 2:
                b, g = divmod((n - 2) // 2, GROUPS)
                copied[b, g] = times_v(b, g)
            if n % 2 == 1 and 3 <= n < NB * PAIRS + 3:
                b, g = divmod((n - 3) // 2, GROUPS)
                ended[b] = normalise(b, g, copied[b, g])
            if n >= 12 and (n - 12) % PAIRS == 0:
                ended[n // PAIRS - 1] = to_features(n // PAIRS - 1, ended[n // PAIRS - 1])
            if n >= 13 and (n - 13) % PAIRS == 0:
                residual(n // PAIRS - 1, ended[n // PAIRS - 1])
            b, j = divmod(n, PAIRS)
            if j == PAIRS - 1 and b + 2 < NB:
                max_to_rows(b + 2)
            if j == PAIRS - 1 and b + RING < NB:
                stacked[b + RING] = stack(b + RING, (c.pe, c.pe.count))
        c.join()


EXPERTS, WIDTH, TOP = 64, 64, 8
PAIRS = EXPERTS // 2


def layer0_experts(c, io):
    nc, resid, xT = c.nc, c.resid, c.columns
    with ExitStack() as w:
        sb = lambda name, shape, dtype=F32: c.sbuf(w, name, shape, dtype)
        RING = 4
        gate_up = [sb(f"e_gate_up{i}", [P, DK, 2, P]) for i in range(RING)]
        down = [sb(f"e_down{i}", [P, D]) for i in range(RING)]
        TOKENS = T // 2
        comb_wide = [sb(f"e_comb_wide{i}", [P, TOKENS]) for i in range(RING)]
        loaded = [c.tally(f"e_loaded{i}") for i in range(RING)]
        comb_loaded = [c.tally(f"e_comb_loaded{i}") for i in range(RING)]
        router = sb("e_router", [P, DK, EXPERTS + 1])
        router_in = c.load(router[:, :, :], io["e_router"], c.tally("e_router_in"))
        comb = sb("e_comb", [P, NB, EXPERTS + 1])
        combT = sb("e_comb_rows", [EXPERTS + 1, T])

        weights_in, slot_free, comb_free = {}, {}, {}
        units = [(half, pair) for half in range(2) for pair in range(PAIRS + 1)]

        def load_weights(u):
            pair, r = units[u][1], u % RING
            if pair < PAIRS:
                c.load(gate_up[r][:, :, :, :], io["e_gate_up"][pair], loaded[r], slot_free.get(r))
                weights_in[u] = c.load(down[r][:, :], io["e_down"][pair], loaded[r])
            else:
                c.load(gate_up[r][:, :, :, 0:WIDTH], io["e_shared_gate_up"], loaded[r], slot_free.get(r))
                weights_in[u] = c.load(down[r][0:WIDTH, :], io["e_shared_down"], loaded[r])

        for u in range(RING - 1):
            load_weights(u)

        with ExitStack() as w2:
            s2 = lambda name, shape, dtype=F32: c.sbuf(w2, name, shape, dtype)
            normed = s2("e_normed", [P, NB, D])
            probs, left = s2("e_probs", [P, NB, EXPERTS]), s2("e_left", [P, NB, EXPERTS])
            logits = s2("e_logits", [P, NB, EXPERTS + 1])
            best = s2("e_best", [P, NB, TOP])
            peak, total, weight = (s2(f"e_{n}", [P, NB]) for n in ("peak", "total", "weight"))
            norm = row_norm(c, w2, "e", resid, normed, c.x_in)
            columns = to_columns(c, normed, xT, norm)
            GROUP = 4
            for g in range(NB // GROUP):
                bank = c.banks[4 + g]
                for i in range(GROUP):
                    b = g * GROUP + i
                    for k in range(DK):
                        pe = c.on_pe(lambda e: e.matmul(bank[:, i * (EXPERTS + 1):(i + 1) * (EXPERTS + 1)], xT[:, k, b * P:(b + 1) * P],
                                                        router[:, k, :], start=k == 0, stop=k == DK - 1), columns[b], router_in)
                a = c.on_act(lambda e: e.copy(logits[:, g * GROUP:(g + 1) * GROUP, :], bank[:, 0:GROUP * (EXPERTS + 1)]
                                              .rearrange("p (b n) -> p b n", b=GROUP)), pe)
            wide = lambda t: t[:, :].unsqueeze(2).to_broadcast([P, NB, EXPERTS])
            routed = logits[:, :, 0:EXPERTS]
            m = c.on_dve(lambda e: e.tensor_reduce(peak[:, :], routed, AX.X, ALU.max), a)
            m = c.on_dve(lambda e: e.tensor_tensor(probs[:, :, :], routed, wide(peak), ALU.subtract), m)
            m = c.on_act(lambda e: e.activation(probs[:, :, :], probs[:, :, :], ACT.Exp), m)
            shared = c.on_act(lambda e: e.activation(comb[:, :, EXPERTS], logits[:, :, EXPERTS], ACT.Exp, scale=-1.0))
            m = c.on_dve(lambda e: e.tensor_reduce(total[:, :], probs[:, :, :], AX.X, ALU.add), m)
            m = c.on_dve(lambda e: e.reciprocal(total[:, :], total[:, :]), m)
            m = c.on_dve(lambda e: e.tensor_tensor(probs[:, :, :], probs[:, :, :], wide(total), ALU.mult), m)
            for b in range(NB):
                m8 = c.on_dve(lambda e: e.max(best[:, b, :], probs[:, b, :]), m)
            for b in range(NB):
                m = c.on_dve(lambda e: e.match_replace(left[:, b, :], best[:, b, :], probs[:, b, :], -1.0), m8)
            m = c.on_dve(lambda e: e.tensor_reduce(weight[:, :], best[:, :, :], AX.X, ALU.add), m)
            m = c.on_dve(lambda e: e.reciprocal(weight[:, :], weight[:, :]), m)
            m = c.on_dve(lambda e: e.scalar_tensor_tensor(left[:, :, :], left[:, :, :], 0.0, probs[:, :, :], ALU.is_lt, ALU.mult), m)
            m = c.on_dve(lambda e: e.tensor_tensor(comb[:, :, 0:EXPERTS], left[:, :, :], wide(weight), ALU.mult), m)
            m = c.on_dve(lambda e: e.tensor_scalar(comb[:, :, EXPERTS], comb[:, :, EXPERTS], 1.0, None, ALU.add), shared)
            comb_ready = c.on_dve(lambda e: e.reciprocal(comb[:, :, EXPERTS], comb[:, :, EXPERTS]), m)
            for g in range(NB // GROUP):
                for i in range(GROUP):
                    pe = c.on_pe(lambda e: e.transpose(c.banks[4 + g][0:EXPERTS + 1, i * P:(i + 1) * P], comb[:, g * GROUP + i, :],
                                                       c.ident[:, :]), comb_ready, a)
                a2 = c.on_act(lambda e: e.copy(combT[:, g * BANK:(g + 1) * BANK], c.banks[4 + g][0:EXPERTS + 1, :]), pe)
            comb_stored = c.load(io["e_combT"], combT[:, :], c.tally("e_comb_stored"), a2)
            free_after_router = c.now()

        def load_comb(u):
            (half, pair), r = units[u], u % RING
            cols = slice(half * TOKENS, (half + 1) * TOKENS)
            for i in range(2 if pair < PAIRS else 1):
                m = c.load(comb_wide[r][i * WIDTH:(i + 1) * WIDTH, :],
                           io["e_combT"][2 * pair + i:2 * pair + i + 1, cols].broadcast_to([WIDTH, TOKENS]),
                           comb_loaded[r], comb_stored, comb_free.get(r))
            comb_in[u] = m

        with ExitStack() as w3:
            s3 = lambda name, shape, dtype=F32: c.sbuf(w3, name, shape, dtype)
            silu = [s3(f"e_silu{i}", [P, BANK]) for i in range(2)]
            gated = [s3(f"e_gated{i}", [P, BANK]) for i in range(2)]
            hidden = [s3(f"e_hidden{i}", [P, BANK]) for i in range(2)]
            comb_in, bank_free = {}, {n: free_after_router for n in range(8)}
            chunks = TOKENS // BANK
            steps = [(u, chunk) for u in range(len(units)) for chunk in range(chunks)]
            down_done, hidden_ready = {}, {}
            gated_used = {}

            def gate_and_up(n):
                u, chunk = steps[n]
                (half, pair), r, i = units[u], u % RING, n % 2
                cols = slice(half * TOKENS + chunk * BANK, half * TOKENS + (chunk + 1) * BANK)
                rows = P if pair < PAIRS else WIDTH
                for which in range(2):
                    bank = c.banks[2 * i + which]
                    for k in range(DK):
                        pe = c.on_pe(lambda e: e.matmul(bank[0:rows, :], gate_up[r][:, k, which, 0:rows], xT[:, k, cols],
                                                        start=k == 0, stop=k == DK - 1), weights_in[u], *bank_free[2 * i + which])
                    if which == 0:
                        a = c.on_act(lambda e: e.activation(silu[i][0:rows, :], c.banks[2 * i][0:rows, :], ACT.Silu), pe, gated_used.get(i))
                        bank_free[2 * i] = [a]
                m = c.on_dve(lambda e: e.tensor_tensor(gated[i][0:rows, :], silu[i][0:rows, :], c.banks[2 * i + 1][0:rows, :], ALU.mult), a, pe,
                             hidden_ready.get(n - 2))
                bank_free[2 * i + 1] = [m]
                gated_used[i] = m
                hidden_ready[n] = c.on_pool(lambda e: e.tensor_tensor(hidden[i][0:rows, :], gated[i][0:rows, :],
                                                                      comb_wide[r][0:rows, chunk * BANK:(chunk + 1) * BANK], ALU.mult),
                                            m, comb_in[u], down_done.get(n - 2))
                comb_free[r] = hidden_ready[n]

            def to_out(n):
                u, chunk = steps[n]
                (half, pair), r, i = units[u], u % RING, n % 2
                rows = P if pair < PAIRS else WIDTH
                for t in range(BANK // P):
                    tile = chunk * (BANK // P) + t
                    bank = 4 + tile // 2
                    pe = c.on_pe(lambda e: e.matmul(c.banks[bank][:, (tile % 2) * D:(tile % 2 + 1) * D], hidden[i][0:rows, t * P:(t + 1) * P],
                                                    down[r][0:rows, :], start=pair == 0 and tile % 2 == 0, stop=pair == PAIRS,
                                                    skip_group_check=True), hidden_ready[n], *bank_free[bank])
                down_done[n] = slot_free[r] = pe
                if pair == PAIRS:
                    for bank in (4 + 2 * chunk, 5 + 2 * chunk):
                        b = half * NB // 2 + 2 * (bank - 4)
                        bank_free[bank] = [c.on_dve(lambda e: e.scalar_tensor_tensor(
                            resid[:, b:b + 2, :], c.banks[bank][:, :].rearrange("p (b n) -> p b n", b=2), c.gates[:, 1:2], resid[:, b:b + 2, :],
                            ALU.mult, ALU.add), pe, c.gates_ready)]

            for u in range(RING - 1):
                load_comb(u)
            for n in range(len(steps)):
                u, chunk = steps[n]
                gate_and_up(n)
                if n > 0:
                    to_out(n - 1)
                if chunk == 0 and u + RING - 1 < len(units):
                    load_weights(u + RING - 1)
                    load_comb(u + RING - 1)
            to_out(len(steps) - 1)
            c.join()


CELLS, CD = 16, 16
CELL_EPS = 1e-6
LOWEST = -3e38
GATE_ROWS = 48


def layer1_mlstm(c, io):
    nc, resid, ctx, xT = c.nc, c.resid, c.ctx, c.columns
    with ExitStack() as w:
        sb = lambda name, shape, dtype=F32: c.sbuf(w, name, shape, dtype)
        ctxT = sb("m_ctxT", [P, DK, T])
        ctxT_in = c.load(ctxT[:, :, :], io["m_ctxT"].rearrange("(k p) t -> p k t", p=P), c.tally("m_ctxT_in"))
        small_in = c.tally("m_small_in")
        gate_w = sb("m_gate_w", [P, 3 * DK, GATE_ROWS])
        gate_bias, head_mask, ln_scale = sb("m_gate_bias", [CELLS, 2]), sb("m_head_mask", [P, CELLS // DK]), sb("m_ln_scale", [P, D])
        for dst, src in ((gate_w[:, :, :], io["m_gate_w"]), (gate_bias[:, :], io["m_gate_bias"]), (head_mask[:, :], io["m_head_mask"])):
            c.load(dst, src, small_in)
        small = c.load(ln_scale[:, :], io["m_ln_scale"].broadcast_to([P, D]), small_in)
        vaug = sb("m_vaug", [P, NB, CELLS, CD + 1])
        decay_rows = sb("m_decay_rows", [GATE_ROWS, T])
        per_token = sb("m_per_token", [P, NB, GATE_ROWS])
        cell = sb("m_cell", [P, NB, D])

        c.on_dve(lambda e: e.memset(vaug[:, :, :, CD], 1.0))
        vaug_ready = c.on_dve(lambda e: e.tensor_copy(vaug[:, :, :, 0:CD], ctx[:, :, :].rearrange("p b (h d) -> p b h d", h=CELLS)), *c.ctx_in)
        rows_clear = c.on_pool(lambda e: e.memset(decay_rows[:, :], 0.0))

        with ExitStack() as w2:
            s2 = lambda name, shape, dtype=F32: c.sbuf(w2, name, shape, dtype)
            with ExitStack() as w3:
                normed = c.sbuf(w3, "m_normed", [P, NB, D])
                norm = row_norm(c, w3, "m", resid, normed, c.x_in)
                columns = to_columns(c, normed, xT, norm)
            ig, fg, scratch, keep, drop, peak = (s2(f"m_{n}", [CELLS, T]) for n in ("ig", "fg", "scratch", "keep", "drop", "peak"))
            first = lambda t: t[:, :].rearrange("p (b t) -> p b t", b=NB)[:, :, 0]
            m0 = c.on_pool(lambda e: e.memset(keep[:, :], 1.0), columns[-1])
            m0 = c.on_pool(lambda e: e.memset(drop[:, :], 0.0))
            m0 = c.on_pool(lambda e: e.memset(first(keep), 0.0))
            resets = c.on_pool(lambda e: e.memset(first(drop), LOWEST))
            bank_used = {}
            for n in range(T // BANK):
                cols, bank = slice(n * BANK, (n + 1) * BANK), 4 + n
                for k in range(3 * DK):
                    src = xT if k < DK else ctxT
                    pe = c.on_pe(lambda e: e.matmul(c.banks[bank][0:GATE_ROWS, :], gate_w[:, k, :], src[:, k % DK, cols],
                                                    start=k == 0, stop=k == 3 * DK - 1), small, ctxT_in, *columns[4 * n:4 * n + 4])
                c.on_act(lambda e: e.activation(ig[:, cols], c.banks[bank][0:CELLS, :], ACT.Identity, bias=gate_bias[:, 0:1]), pe, columns[-1])
                a = c.on_act(lambda e: e.copy(fg[:, cols], c.banks[bank][32:32 + CELLS, :]))
            gates_read = a
            m = c.on_dve(lambda e: e.tensor_scalar(fg[:, :], fg[:, :], gate_bias[:, 1:2], None, ALU.add), a)
            m = c.on_dve(lambda e: e.scalar_tensor_tensor(scratch[:, :], fg[:, :], -1.0, fg[:, :], ALU.mult, ALU.min), m)
            m = c.on_act(lambda e: e.activation(scratch[:, :], scratch[:, :], ACT.Exp), m)
            m = c.on_act(lambda e: e.activation(scratch[:, :], scratch[:, :], ACT.Ln, bias=1.0), m)
            m = c.on_dve(lambda e: e.scalar_tensor_tensor(scratch[:, :], fg[:, :], 0.0, scratch[:, :], ALU.min, ALU.subtract), m)
            m = c.on_dve(lambda e: e.tensor_tensor_scan(fg[:, :], keep[:, :], scratch[:, :], 0.0, ALU.mult, ALU.add), m, resets)
            g = c.on_dve(lambda e: e.tensor_tensor(decay_rows[0:CELLS, :], ig[:, :], fg[:, :], ALU.subtract), m, rows_clear)
            m = c.on_dve(lambda e: e.tensor_tensor_scan(peak[:, :], drop[:, :], decay_rows[0:CELLS, :], 0.0, ALU.add, ALU.max), g)
            mm = c.on_dve(lambda e: e.tensor_tensor(fg[:, :], fg[:, :], peak[:, :], ALU.add), m)
            m = c.on_dve(lambda e: e.tensor_scalar(scratch[:, :], peak[:, :], -1.0, None, ALU.mult), m)
            peak_stored = c.load(io["m_negpeak"], scratch[:, :], c.tally("m_peak_stored"), m)
            rows_ready = c.on_act(lambda e: e.activation(decay_rows[32:32 + CELLS, :], fg[:, :], ACT.Exp, scale=-1.0), mm)
            for b in range(NB):
                pe = c.on_pe(lambda e: e.transpose(c.banks[4 + b % 4][:, 0:GATE_ROWS], decay_rows[:, b * P:(b + 1) * P],
                                                   c.ident[0:GATE_ROWS, 0:GATE_ROWS]), rows_ready, gates_read, bank_used.get(b % 4))
                bank_used[b % 4] = a = c.on_act(lambda e: e.copy(per_token[:, b, :], c.banks[4 + b % 4][:, 0:GATE_ROWS]), pe)
            token_ready = a
            scans_done = c.now() + [peak_stored]

        with ExitStack() as w2:
            s2 = lambda name, shape, dtype=F32: c.sbuf(w2, name, shape, dtype)
            RING = 3
            qblock = [s2(f"m_qblock{i}", [P, DK, CELLS // DK, P]) for i in range(2)]
            decay = [s2(f"m_decay{i}", [P, CELLS, P]) for i in range(RING)]
            product = [s2(f"m_product{i}", [P, CELLS, P]) for i in range(2)]
            sums = [s2(f"m_sums{i}", [P, BANK]) for i in range(2)]
            denom = [s2(f"m_denom{i}", [P, CELLS]) for i in range(2)]
            peak_in = [c.tally(f"m_peak_in{i}") for i in range(RING)]
            bank_free = {n: scans_done for n in range(8)}
            for bank in (4, 5):
                bank_free[bank] = [c.on_dve(lambda e: e.memset(c.banks[bank][:, :], 0.0), *scans_done)]
            decayed, multiplied, sums_free, out = {}, {}, {}, {}
            per_half = CELLS // DK

            def decay_of(b):
                d = decay[b % RING]
                arrived = c.load(d[:, :, :], io["m_negpeak"].rearrange("h (b s) -> b h s", b=NB)[b].unsqueeze(0).broadcast_to([P, CELLS, P]),
                                 peak_in[b % RING], peak_stored, *scans_done, multiplied.get(b - RING))
                gt = per_token[:, b, 0:CELLS].unsqueeze(2).to_broadcast([P, CELLS, P])
                m = c.on_dve(lambda e: e.tensor_tensor(d[:, :, :], d[:, :, :], gt, ALU.add), arrived, token_ready)
                m = c.on_pool(lambda e: e.affine_select(out=d[:, :, :], in_=d[:, :, :], compare_op=ALU.is_ge, fill=LOWEST, base=0,
                                                        pattern=[[0, CELLS], [1, P]], channel_multiplier=-1), m)
                decayed[b] = c.on_act(lambda e: e.activation(d[:, :, :], d[:, :, :], ACT.Exp), m)

            def block_queries(b):
                for k in range(DK):
                    q = xT[:, k, b * P:(b + 1) * P].unsqueeze(1).to_broadcast([P, per_half, P])
                    h = head_mask[:, :].unsqueeze(2).to_broadcast([P, per_half, P])
                    blocked[b] = c.on_pool(lambda e: e.tensor_tensor(qblock[b % 2][:, k, :, :], q, h, ALU.mult), *scans_done, scored.get(b - 2))

            blocked, scored, cells, copied = {}, {}, {}, {}

            def scores(b):
                for i in range(4):
                    k, q4 = divmod(i, 2)
                    pe = c.on_pe(lambda e: e.matmul(c.banks[i][:, :], ctxT[:, k, b * P:(b + 1) * P],
                                                    qblock[b % 2][:, k, 4 * q4:4 * q4 + 4, :].rearrange("p h s -> p (h s)"),
                                                    start=True, stop=True), blocked[b], *bank_free[i])
                    m = c.on_dve(lambda e: e.tensor_tensor(product[b % 2][:, 4 * i:4 * i + 4, :].rearrange("p h s -> p (h s)"), c.banks[i][:, :],
                                                           decay[b % RING][:, 4 * i:4 * i + 4, :].rearrange("p h s -> p (h s)"), ALU.mult),
                                 pe, decayed[b], out.get(b - 2))
                    bank_free[i] = [m]
                scored[b], multiplied[b] = pe, m

            def times_v(b):
                bank = 4 + b % 2
                for i in range(4):
                    for tile in range(4):
                        h = 4 * i + tile
                        pe = c.on_pe(lambda e: e.matmul(c.banks[bank][32 * tile:32 * tile + CD + 1, i * P:(i + 1) * P], vaug[:, b, h, :],
                                                        product[b % 2][:, h, :], start=True, stop=True),
                                     multiplied[b], vaug_ready, *bank_free[bank])
                out[b] = pe
                a = c.on_act(lambda e: e.copy(sums[b % 2][:, :], c.banks[bank][:, :]), pe, sums_free.get(b - 2))
                bank_free[bank] = [a]
                return a

            def divide(b, copied):
                for i in range(4):
                    pe = c.on_pe(lambda e: e.transpose(c.banks[6][:, i * P:(i + 1) * P], sums[b % 2][:, i * P:(i + 1) * P], c.ident[:, :]),
                                 copied, *bank_free[6])
                sums_free[b] = pe
                view, den = c.banks[6][:, :].rearrange("p (h d) -> p h d", h=CELLS), denom[b % 2]
                m = c.on_dve(lambda e: e.scalar_tensor_tensor(den[:, :], view[:, :, CD], -1.0, per_token[:, b, 32:32 + CELLS], ALU.mult, ALU.max), pe)
                m = c.on_dve(lambda e: e.tensor_tensor(den[:, :], view[:, :, CD], den[:, :], ALU.max), m)
                m = c.on_dve(lambda e: e.tensor_scalar(den[:, :], den[:, :], CELL_EPS, None, ALU.add), m)
                m = c.on_dve(lambda e: e.reciprocal(den[:, :], den[:, :]), m)
                m = c.on_dve(lambda e: e.tensor_tensor(cell[:, b, :].rearrange("p (h d) -> p h d", h=CELLS), view[:, :, 0:CD],
                                                       den[:, :].unsqueeze(2).to_broadcast([P, CELLS, CD]), ALU.mult), m)
                bank_free[6] = [m]
                cells[b] = m

            for n in range(NB + 3):
                if n < NB:
                    block_queries(n)
                    decay_of(n)
                if 1 <= n <= NB:
                    scores(n - 1)
                if 2 <= n <= NB + 1:
                    copied[n - 2] = times_v(n - 2)
                if n >= 3:
                    divide(n - 3, copied[n - 3])
            cells_done = c.now()

        with ExitStack() as w2:
            s2 = lambda name, shape, dtype=F32: c.sbuf(w2, name, shape, dtype)
            GROUP = 4
            square = [s2(f"m_square{i}", [P, GROUP, D]) for i in range(2)]
            mean, rstd = s2("m_head_mean", [P, NB * CELLS]), s2("m_head_rstd", [P, NB * CELLS])
            heads = lambda t: t.rearrange("p b (h d) -> p (b h) d", d=CD)
            wide = lambda t, g: t[:, g * GROUP * CELLS:(g + 1) * GROUP * CELLS].unsqueeze(2).to_broadcast([P, GROUP * CELLS, CD])
            part = lambda t, g: t[:, g * GROUP * CELLS:(g + 1) * GROUP * CELLS]
            for g in range(NB // GROUP):
                x = cell[:, g * GROUP:(g + 1) * GROUP, :]
                m = c.on_dve(lambda e: e.tensor_reduce(part(mean, g), heads(x), AX.X, ALU.add), *cells_done)
                m = c.on_dve(lambda e: e.tensor_scalar(part(mean, g), part(mean, g), 1.0 / CD, None, ALU.mult), m)
                m = c.on_dve(lambda e: e.tensor_tensor(heads(x), heads(x), wide(mean, g), ALU.subtract), m)
                a = c.on_act(lambda e: e.activation(square[g % 2][:, :, :], x, ACT.Square), m)
                m = c.on_dve(lambda e: e.tensor_reduce(part(rstd, g), heads(square[g % 2][:, :, :]), AX.X, ALU.add), a)
            m = c.on_dve(lambda e: e.tensor_scalar(rstd[:, :], rstd[:, :], 1.0 / CD, CELL_EPS, ALU.mult, ALU.add), m)
            m = c.on_act(lambda e: e.activation(rstd[:, :], rstd[:, :], ACT.Sqrt), m)
            m = c.on_dve(lambda e: e.reciprocal(rstd[:, :], rstd[:, :]), m)
            for g in range(NB // GROUP):
                x = cell[:, g * GROUP:(g + 1) * GROUP, :]
                m1 = c.on_dve(lambda e: e.tensor_tensor(heads(x), heads(x), wide(rstd, g), ALU.mult), m)
                m1 = c.on_pool(lambda e: e.tensor_tensor(x, x, ln_scale[:, :].unsqueeze(1).to_broadcast([P, GROUP, D]), ALU.mult), m1, small)
                c.on_dve(lambda e: e.scalar_tensor_tensor(resid[:, g * GROUP:(g + 1) * GROUP, :], x, c.gates[:, 2:3],
                                                          resid[:, g * GROUP:(g + 1) * GROUP, :], ALU.mult, ALU.add), m1, c.gates_ready)
            c.join()


RH, RD = 16, 128
MOE, MW = 4, 256
CHUNK = BANK // P
NCHUNK = NB // CHUNK
MASKED = -3e38


def layer1_block(c, io):
    nc, resid, xT = c.nc, c.resid, c.columns
    with ExitStack() as w:
        sb = lambda name, shape, dtype=F32: c.sbuf(w, name, shape, dtype)
        y = sb("b_y", [P, NB, D])
        small_in = c.tally("b_small_in")
        vectors = sb("b_vectors", [P, 8])
        head_bias = sb("b_head_bias", [P, 3, RH])
        swap_bias = sb("b_swap_bias", [P, 2, RH])
        bo = sb("b_bo", [P, D])
        for dst, src in ((vectors[:, :], io["b_vectors"]), (head_bias[:, :, :], io["b_head_bias"]), (swap_bias[:, :, :], io["b_swap_bias"])):
            c.load(dst, src, small_in)
        small = c.load(bo[:, :], io["b_bo"].broadcast_to([P, D]), small_in)
        block_attention(c, io, y, vectors, head_bias, swap_bias, bo, small)
        block_experts(c, io, y, vectors, small)


def block_attention(c, io, y, vectors, head_bias, swap_bias, bo, small):
    nc, resid, xT = c.nc, c.resid, c.columns
    SCALE = 1.0 / float(np.sqrt(RD))
    with ExitStack() as w:
        sb = lambda name, shape, dtype=F32: c.sbuf(w, name, shape, dtype)
        wqk = sb("b_wqk", [P, RH, 2, DK, RD])
        wv = sb("b_wv", [P, DK, RH * RD])
        wo = sb("b_wo", [P, RH, D])
        rope, mask = sb("b_rope", [P, 2, S]), sb("b_mask", [P, S])
        tables_in = c.tally("b_tables_in")
        c.load(rope[:, :, :], io["b_rope"], tables_in)
        tables = c.load(mask[:, :], io["b_mask"], tables_in)
        wv_in = c.load(wv[:, :, :], io["b_wv"], c.tally("b_wv_in"))
        GROUP = 4
        wqk_in = [c.load(wqk[:, g:g + GROUP, :, :, :], io["b_wqk"][:, g:g + GROUP, :, :, :], c.tally(f"b_wqk_in{g}")) for g in range(0, RH, GROUP)]
        wo_in = c.load(wo[:, :, :], io["b_wo"], c.tally("b_wo_in"))

        with ExitStack() as w2:
            z = c.sbuf(w2, "b_z", [P, NB, D])
            first = row_norm(c, w2, "b0", resid, y, c.x_in)
            second = row_norm(c, w2, "b1", y, z, first)
            columns = to_columns(c, z, xT, second, scale=vectors[:, 0:2], bias=vectors[:, 2:4], vectors_in=small)
            with_bo = c.on_pool(lambda e: e.tensor_tensor(y[:, :, :], y[:, :, :], bo[:, :].unsqueeze(1).to_broadcast([P, NB, D]), ALU.add),
                                second[-1], small)
            z_done = c.now()

        with ExitStack() as w2:
            s2 = lambda name, shape, dtype=F32: c.sbuf(w2, name, shape, dtype)
            v = [s2(f"b_v{i}", [P, CHUNK, GROUP * RD]) for i in range(3)]
            turned = [s2(f"b_turned{i}", [P, 2, BANK]) for i in range(2)]
            straight = [s2(f"b_straight{i}", [P, 2, BANK]) for i in range(2)]
            probs = [s2(f"b_probs{i}", [P, CHUNK, S]) for i in range(3)]
            peak, peak_scaled, total, inv = ([s2(f"b_{n}{i}", [P, CHUNK]) for i in range(2)] for n in ("peak", "peak_scaled", "total", "inv"))
            probsT = [s2(f"b_probsT{i}", [P, BANK]) for i in range(2)]
            outT = [s2(f"b_outT{i}", [P, BANK]) for i in range(2)]
            Q, K, V, SC, PT, OT, OUT = 0, 1, 2, 3, 4, 5, 6
            free = {n: z_done for n in range(8)}
            steps = NCHUNK * RH
            v_ready, v_used, rotated, scored, prob_ready, out_ready, done = {}, {}, {}, {}, {}, {}, {}

            def values(n):
                group, tile = divmod(n, CHUNK)
                chunk, g = divmod(group, RH // GROUP)
                b = chunk * CHUNK + tile
                for k in range(DK):
                    pe = c.on_pe(lambda e: e.matmul(c.banks[V][:, :], xT[:, k, b * P:(b + 1) * P], wv[:, k, g * BANK:(g + 1) * BANK],
                                                    start=k == 0, stop=k == DK - 1), columns[b], wv_in, *free[V])
                v_ready[group] = a = c.on_act(lambda e: e.copy(v[group % 3][:, tile, :], c.banks[V][:, :]), pe, *v_used.get(group - 3, z_done))
                free[V] = [a]

            def queries_keys(n):
                chunk, h = divmod(n, RH)
                i = n % 2
                by_batch = lambda t: t.rearrange("p (b s) -> p b s", b=CHUNK)
                wide = lambda which: rope[:, which, :].unsqueeze(1).to_broadcast([P, CHUNK, S])
                for which, bank in ((0, Q), (1, K)):
                    for k in range(DK):
                        pe = c.on_pe(lambda e: e.matmul(c.banks[bank][:, :], wqk[:, h, which, k, :], xT[:, k, chunk * BANK:(chunk + 1) * BANK],
                                                        start=k == 0, stop=k == DK - 1),
                                     *columns[chunk * CHUNK:(chunk + 1) * CHUNK], wqk_in[h // GROUP], *free[bank])
                    half = P // 2
                    for dst, src in ((0, half), (half, 0)):
                        a = c.on_act(lambda e: e.activation(turned[i][dst:dst + half, which, :], c.banks[bank][src:src + half, :], ACT.Identity,
                                                            bias=swap_bias[dst:dst + half, which, h:h + 1]), pe, small, scored.get(n - 2), *z_done)
                    m = c.on_dve(lambda e: e.scalar_tensor_tensor(by_batch(straight[i][:, which, :]), by_batch(c.banks[bank][:, :]),
                                                                  head_bias[:, which, h:h + 1], wide(0), ALU.add, ALU.mult),
                                 pe, a, tables, scored.get(n - 2))
                    free[bank] = [a, m]
                    p = c.on_pool(lambda e: e.tensor_tensor(by_batch(turned[i][:, which, :]), by_batch(turned[i][:, which, :]), wide(1), ALU.mult), a, tables)
                    rotated[n] = c.on_dve(lambda e: e.tensor_tensor(straight[i][:, which, :], straight[i][:, which, :], turned[i][:, which, :], ALU.add), p, m)

            def softmax(n):
                i = n % 2
                for b in range(CHUNK):
                    pe = c.on_pe(lambda e: e.matmul(c.banks[SC][:, b * S:(b + 1) * S], straight[i][:, 0, b * S:(b + 1) * S],
                                                    straight[i][:, 1, b * S:(b + 1) * S], start=True, stop=True), rotated[n], *free[SC])
                scored[n] = pe
                by_batch = c.banks[SC][:, :].rearrange("p (b s) -> p b s", b=CHUNK)
                m = c.on_dve(lambda e: e.tensor_tensor(probs[n % 3][:, :, :], by_batch, mask[:, :].unsqueeze(1).to_broadcast([P, CHUNK, S]), ALU.add),
                             pe, tables, prob_used.get(n - 3))
                free[SC] = [m]
                m = c.on_dve(lambda e: e.tensor_reduce(peak[i][:, :], probs[n % 3][:, :, :], AX.X, ALU.max, negate=True), m)
                m = c.on_dve(lambda e: e.tensor_scalar(peak_scaled[i][:, :], peak[i][:, :], SCALE, None, ALU.mult), m)
                for b in range(CHUNK):
                    a = c.on_act(lambda e: e.activation(probs[n % 3][:, b, :], probs[n % 3][:, b, :], ACT.Exp, scale=SCALE, bias=peak_scaled[i][:, b:b + 1],
                                                        accum_out=total[i][:, b:b + 1]), m)
                m = c.on_dve(lambda e: e.reciprocal(inv[i][:, :], total[i][:, :]), a)
                prob_ready[n] = c.on_pool(lambda e: e.tensor_tensor(probs[n % 3][:, :, :], probs[n % 3][:, :, :],
                                                                    inv[i][:, :].unsqueeze(2).to_broadcast([P, CHUNK, S]), ALU.mult), m)

            prob_used = {}

            def transpose_probs(n):
                i = n % 2
                for b in range(CHUNK):
                    pe = c.on_pe(lambda e: e.transpose(c.banks[PT][:, b * S:(b + 1) * S], probs[n % 3][:, b, :], c.ident[:, :]), prob_ready[n], *free[PT])
                prob_used[n] = pe
                a = c.on_act(lambda e: e.copy(probsT[i][:, :], c.banks[PT][:, :]), pe, out_ready.get(n - 2))
                free[PT] = [a]
                transposed[n] = a

            transposed = {}

            def weigh_values(n):
                chunk, h = divmod(n, RH)
                group, i = n // GROUP, n % 2
                for b in range(CHUNK):
                    pe = c.on_pe(lambda e: e.matmul(c.banks[OT][:, b * S:(b + 1) * S], v[group % 3][:, b, (h % GROUP) * RD:(h % GROUP + 1) * RD],
                                                    probsT[i][:, b * S:(b + 1) * S], start=True, stop=True), transposed[n], v_ready[group], *free[OT])
                v_used[group] = [pe]
                a = c.on_act(lambda e: e.activation(outT[i][:, :], c.banks[OT][:, :], ACT.Identity, bias=head_bias[:, 2, h:h + 1]), pe, done.get(n - 2))
                free[OT], out_ready[n] = [a], a

            def project(n):
                chunk, h = divmod(n, RH)
                i = n % 2
                for b in range(CHUNK):
                    bank = OUT + b // 2
                    pe = c.on_pe(lambda e: e.matmul(c.banks[bank][:, (b % 2) * D:(b % 2 + 1) * D], outT[i][:, b * S:(b + 1) * S], wo[:, h, :],
                                                    start=h == 0 and b % 2 == 0, stop=h == RH - 1, skip_group_check=True),
                                 out_ready[n], wo_in, *free[bank])
                done[n] = pe
                if h == RH - 1:
                    for bank in (OUT, OUT + 1):
                        rows = y[:, chunk * CHUNK + 2 * (bank - OUT):chunk * CHUNK + 2 * (bank - OUT) + 2, :]
                        free[bank] = [c.on_dve(lambda e: e.tensor_tensor(rows, rows, c.banks[bank][:, :].rearrange("p (b n) -> p b n", b=2), ALU.add),
                                               pe, with_bo)]

            for n in range(CHUNK):
                values(n)
            for n in range(steps + 5):
                if n < steps:
                    queries_keys(n)
                if 1 <= n <= steps:
                    softmax(n - 1)
                if CHUNK <= n + CHUNK < steps:
                    values(n + CHUNK)
                if 3 <= n < steps + 3:
                    transpose_probs(n - 3)
                if 4 <= n < steps + 4:
                    weigh_values(n - 4)
                if 5 <= n:
                    project(n - 5)
            c.join()


def block_experts(c, io, y, vectors, small):
    nc, resid, xT = c.nc, c.resid, c.columns
    with ExitStack() as w:
        sb = lambda name, shape, dtype=F32: c.sbuf(w, name, shape, dtype)
        PAD = 12
        w1, w2 = sb("b_w1", [P, MOE, DK, MW]), sb("b_w2", [P, MOE, MW // P, D])
        b1, b2 = sb("b_b1", [P, MOE, MW // P]), sb("b_b2", [MOE, D])
        gate = sb("b_gate", [P, DK, MOE])
        weights_in = c.tally("b_weights_in")
        for dst, name in ((gate[:, :, :], "b_gate"), (w1[:, :, :, :], "b_w1"), (b1[:, :, :], "b_b1"), (w2[:, :, :, :], "b_w2")):
            c.load(dst, io[name], weights_in)
        weights = c.load(b2[:, :], io["b_b2"], weights_in)
        comb = sb("b_comb", [P, NB, MOE])
        combT = sb("b_combT", [MOE, T])
        comb_wide = sb("b_comb_wide", [P, MOE, T])
        with ExitStack() as w3:
            s3 = lambda name, shape, dtype=F32: c.sbuf(w3, name, shape, dtype)
            z = s3("b_z2", [P, NB, D])
            probs, left, lead = s3("b_padded", [P, NB, PAD]), s3("b_left", [P, NB, PAD]), s3("b_lead", [P, NB, 8])
            best = s3("b_best", [P, NB, 8])
            peak, total = s3("b_gate_peak", [P, NB]), s3("b_gate_total", [P, NB])
            pad = c.on_pool(lambda e: e.memset(probs[:, :, :], -1.0))
            pad = c.on_pool(lambda e: e.memset(lead[:, :, :], -1.0))
            norm = row_norm(c, w3, "b2", y, z, [None] * NB)
            columns = to_columns(c, z, xT, norm, scale=vectors[:, 4:6], bias=vectors[:, 6:8], vectors_in=small)
            for b in range(NB):
                for k in range(DK):
                    pe = c.on_pe(lambda e: e.matmul(c.banks[4][:, b * MOE:(b + 1) * MOE], xT[:, k, b * P:(b + 1) * P], gate[:, k, :],
                                                    start=k == 0, stop=k == DK - 1), columns[b], weights)
            wide = lambda t: t.unsqueeze(2).to_broadcast([P, NB, MOE])
            real = probs[:, :, 0:MOE]
            logits = c.banks[4][:, 0:NB * MOE].rearrange("p (b n) -> p b n", b=NB)
            m = c.on_dve(lambda e: e.tensor_reduce(peak[:, :], logits, AX.X, ALU.max), pe, pad)
            m = c.on_dve(lambda e: e.tensor_tensor(real, logits, wide(peak[:, :]), ALU.subtract), m)
            m = c.on_act(lambda e: e.activation(real, real, ACT.Exp), m)
            m = c.on_dve(lambda e: e.tensor_reduce(total[:, :], real, AX.X, ALU.add), m)
            m = c.on_dve(lambda e: e.reciprocal(total[:, :], total[:, :]), m)
            m = c.on_dve(lambda e: e.tensor_tensor(real, real, wide(total[:, :]), ALU.mult), m)
            for b in range(NB):
                m8 = c.on_dve(lambda e: e.max(best[:, b, :], probs[:, b, :]), m)
            m = c.on_dve(lambda e: e.tensor_copy(lead[:, :, 0:2], best[:, :, 0:2]), m8)
            for b in range(NB):
                m8 = c.on_dve(lambda e: e.match_replace(left[:, b, :], lead[:, b, :], probs[:, b, :], -2.0), m)
            m = c.on_dve(lambda e: e.tensor_tensor(comb[:, :, :], real, wide(best[:, :, 0]), ALU.subtract), m8)
            m = c.on_act(lambda e: e.activation(comb[:, :, :], comb[:, :, :], ACT.Exp), m)
            m = c.on_dve(lambda e: e.scalar_tensor_tensor(comb[:, :, :], left[:, :, 0:MOE], -1.5, comb[:, :, :], ALU.is_lt, ALU.mult), m)
            m = c.on_dve(lambda e: e.tensor_reduce(total[:, :], comb[:, :, :], AX.X, ALU.add), m)
            m = c.on_dve(lambda e: e.reciprocal(total[:, :], total[:, :]), m)
            m = c.on_dve(lambda e: e.tensor_tensor(comb[:, :, :], comb[:, :, :], wide(total[:, :]), ALU.mult), m)
            for g in range(NCHUNK):
                for i in range(CHUNK):
                    pe = c.on_pe(lambda e: e.transpose(c.banks[5][0:MOE, i * P:(i + 1) * P], comb[:, g * CHUNK + i, :], c.ident[:, :]),
                                 m, (c.act, c.act.count))
                a = c.on_act(lambda e: e.copy(combT[:, g * BANK:(g + 1) * BANK], c.banks[5][0:MOE, :]), pe)
            stored = c.load(io["b_comb_rows"], combT[:, :], c.tally("b_comb_stored"), a)
            comb_in = [c.load(comb_wide[:, e_, :], io["b_comb_rows"][e_:e_ + 1, :].broadcast_to([P, T]), c.tally(f"b_comb_in{e_}"), stored)
                       for e_ in range(MOE)]
            routed = c.now()

        with ExitStack() as w3:
            s3 = lambda name, shape, dtype=F32: c.sbuf(w3, name, shape, dtype)
            act = [s3(f"b_act{i}", [P, BANK]) for i in range(2)]
            hidden = [s3(f"b_hidden{i}", [P, BANK]) for i in range(2)]
            MB = MW // P
            steps = [(chunk, e_, mb) for chunk in range(NCHUNK) for e_ in range(MOE) for mb in range(MB)]
            free = {n: routed for n in range(8)}
            ready, used, stores = {}, {}, []
            out_stored = c.tally("out_stored")

            def up(n):
                chunk, e_, mb = steps[n]
                i, cols = n % 2, slice(chunk * BANK, (chunk + 1) * BANK)
                for k in range(DK):
                    pe = c.on_pe(lambda e: e.matmul(c.banks[i][:, :], w1[:, e_, k, mb * P:(mb + 1) * P], xT[:, k, cols], start=k == 0, stop=k == DK - 1),
                                 *free[i])
                a = c.on_act(lambda e: e.activation(act[i][:, :], c.banks[i][:, :], ACT.Gelu, bias=b1[:, e_, mb:mb + 1]), pe, ready.get(n - 2))
                free[i] = [a]
                ready[n] = c.on_dve(lambda e: e.tensor_tensor(hidden[i][:, :], act[i][:, :], comb_wide[:, e_, cols], ALU.mult), a, comb_in[e_], used.get(n - 2))

            def down(n):
                chunk, e_, mb = steps[n]
                i, base = n % 2, 4 + 2 * (chunk % 2)
                for t in range(CHUNK):
                    bank = base + t // 2
                    out = c.banks[bank][:, (t % 2) * D:(t % 2 + 1) * D]
                    tok = slice((chunk * CHUNK + t) * P, (chunk * CHUNK + t + 1) * P)
                    if e_ == 0 and mb == 0:
                        c.on_pe(lambda e: e.matmul(out, combT[:, tok], b2[:, :], start=t % 2 == 0, stop=False, skip_group_check=True), *free[bank])
                    pe = c.on_pe(lambda e: e.matmul(out, hidden[i][:, t * P:(t + 1) * P], w2[:, e_, mb, :], start=False,
                                                    stop=n % (MOE * MB) == MOE * MB - 1, skip_group_check=True), ready[n])
                used[n] = pe
                if n % (MOE * MB) == MOE * MB - 1:
                    for bank in (base, base + 1):
                        b = chunk * CHUNK + 2 * (bank - base)
                        rows, x = y[:, b:b + 2, :], resid[:, b:b + 2, :]
                        m = c.on_dve(lambda e: e.tensor_tensor(rows, rows, c.banks[bank][:, :].rearrange("p (b n) -> p b n", b=2), ALU.add), pe)
                        free[bank] = [m]
                        m = c.on_dve(lambda e: e.scalar_tensor_tensor(x, rows, c.gates[:, 3:4], x, ALU.mult, ALU.add), m, c.gates_ready)
                        c.out_mark = c.load(io["out"][b:b + 2, :, :].rearrange("b p n -> p b n"), x, out_stored, m)

            for n in range(len(steps) + 1):
                if n < len(steps):
                    up(n)
                if n > 0:
                    down(n - 1)


def program(nc, io):
    with ExitStack() as stack:
        c = Core(nc, stack)
        sb = lambda name, shape, dtype=F32: c.sbuf(stack, name, shape, dtype)
        c.resid, c.ctx = sb("resid", [P, NB, D]), sb("ctx", [P, NB, D])
        c.columns = sb("columns", [P, DK, T])
        c.ident, c.gates = sb("ident", [P, P]), sb("gates", [P, 4])
        GROUP = 4
        c.x_in, c.ctx_in = [], []
        for g in range(NB // GROUP):
            for name, dst, marks in (("x", c.resid, c.x_in), ("ctx", c.ctx, c.ctx_in)):
                b = slice(g * GROUP, (g + 1) * GROUP)
                marks += [c.load(dst[:, b, :], io[name][b, :, :].rearrange("b p n -> p b n"), c.tally(f"{name}_in{g}"))] * GROUP
        gates_in = c.load(c.gates[:, :], io["gates"], c.tally("gates_in"))
        c.gates_ready = c.on_act(lambda e: e.activation(c.gates[:, :], c.gates[:, :], ACT.Tanh), gates_in)
        zero = c.on_pool(lambda e: e.memset(c.ident[:, :], 0.0))
        c.ident_ready = c.on_pool(lambda e: e.affine_select(out=c.ident[:, :], in_=c.ident[:, :], compare_op=ALU.not_equal, fill=1.0,
                                                            base=0, pattern=[[-1, P]], channel_multiplier=1), zero)
        for stage in (layer0_attention, layer0_experts, layer1_mlstm, layer1_block):
            stage(c, io)
        c.need(nc.sync, c.out_mark)


def layouts(a):
    from_name = lambda n: np.asarray(a[n])
    out = {"x": from_name("x"), "ctx": from_name("ctx_2048")}
    gates = np.concatenate([from_name("g_xattn")[:, None], from_name("g_ffn")[:, None]], 1).reshape(4)
    out["gates"] = np.broadcast_to(gates, (P, 4))
    for n in "qkvo":
        out[f"a_w{n}T"] = from_name(f"L0_xattn_W{n}").T
    out["a_bias"] = np.stack([from_name(f"L0_xattn_b{n}") for n in "qkvo"], 1)
    gu = from_name("L0_ffn_gate_up_proj").reshape(PAIRS, 2, 2, WIDTH, DK, P)
    out["e_gate_up"] = gu.transpose(0, 5, 4, 2, 1, 3).reshape(PAIRS, P, DK, 2, P)
    out["e_down"] = from_name("L0_ffn_down_proj").reshape(PAIRS, 2, D, WIDTH).transpose(0, 1, 3, 2).reshape(PAIRS, P, D)
    shared = np.stack([from_name("L0_ffn_shared_gate_w"), from_name("L0_ffn_shared_up_w")]).reshape(2, WIDTH, DK, P)
    out["e_shared_gate_up"] = shared.transpose(3, 2, 0, 1)
    out["e_shared_down"] = from_name("L0_ffn_shared_down_w").T
    router = np.concatenate([from_name("L0_ffn_router_w"), from_name("L0_ffn_shared_expert_gate_w")])
    out["e_router"] = router.reshape(EXPERTS + 1, DK, P).transpose(2, 1, 0)
    out["m_ctxT"] = out["ctx"].transpose(2, 0, 1).reshape(D, T)
    gate_w = np.zeros((3 * D, GATE_ROWS), np.float32)
    gate_w[:, 0:CELLS], gate_w[:, 32:32 + CELLS] = from_name("L1_xattn_Wi"), from_name("L1_xattn_Wf")
    out["m_gate_w"] = gate_w.reshape(3 * DK, P, GATE_ROWS).transpose(1, 0, 2)
    out["m_gate_bias"] = np.stack([from_name("L1_xattn_bi"), from_name("L1_xattn_bf")], 1)
    head_of = np.arange(P)[:, None] // CD == np.arange(CELLS // DK)[None, :]
    out["m_head_mask"] = head_of.astype(np.float32) / 4
    out["m_ln_scale"] = from_name("L1_xattn_ln_scale").reshape(1, D)
    by_block = lambda v: v.reshape(DK, P).T
    out["b_vectors"] = np.concatenate([by_block(from_name(f"L1_ffn_{n}")) for n in ("ln1_w", "ln1_b", "ln2_w", "ln2_b")], 1)
    biases = np.stack([from_name(f"L1_ffn_b{n}").reshape(RH, RD) for n in "qkv"])
    out["b_head_bias"] = biases.transpose(2, 0, 1)
    swapped = np.concatenate([biases[:2, :, RD // 2:], biases[:2, :, :RD // 2]], 2)
    out["b_swap_bias"] = swapped.transpose(2, 0, 1)
    out["b_bo"] = from_name("L1_ffn_bo").reshape(1, D)
    qk = np.stack([from_name("L1_ffn_wq"), from_name("L1_ffn_wk")]).reshape(2, DK, P, RH, RD)
    out["b_wqk"] = qk.transpose(2, 3, 0, 1, 4)
    out["b_wv"] = from_name("L1_ffn_wv").reshape(DK, P, RH * RD).transpose(1, 0, 2)
    out["b_wo"] = from_name("L1_ffn_wo").reshape(RH, RD, D).transpose(1, 0, 2)
    f32 = np.float32
    inv_freq = (f32(1.0) / f32(10000.0) ** (np.arange(0, RD, 2, dtype=f32) / f32(RD))).astype(f32)
    angle = np.arange(S, dtype=f32)[None, :] * np.concatenate([inv_freq, inv_freq])[:, None]
    sign = np.where(np.arange(RD) < RD // 2, f32(-1), f32(1))[:, None]
    out["b_rope"] = np.stack([np.cos(angle), np.sin(angle) * sign], 1).astype(f32)
    out["b_mask"] = np.where(np.arange(S)[None, :] > np.arange(S)[:, None], f32(MASKED), f32(0))
    out["b_gate"] = from_name("L1_ffn_w_gate").reshape(DK, P, MOE).transpose(1, 0, 2)
    out["b_w1"] = from_name("L1_ffn_we1").reshape(MOE, DK, P, MW).transpose(2, 0, 1, 3)
    out["b_w2"] = from_name("L1_ffn_we2").reshape(MOE, MW // P, P, D).transpose(2, 0, 1, 3)
    out["b_b1"] = from_name("L1_ffn_be1").reshape(MOE, MW // P, P).transpose(2, 0, 1)
    out["b_b2"] = from_name("L1_ffn_be2")
    return {n: np.ascontiguousarray(v) for n, v in out.items()}


SCRATCH = {
    "b_comb_rows": ((MOE, T), F32),
    "m_negpeak": ((CELLS, T), F32),
    "e_combT": ((EXPERTS + 1, T), F32),
    "a_q_parts": ((3, P, T * D // P), BF16),
    "a_k_parts": ((3, P, T * D // P), BF16),
}


def kernel(**inputs):
    import concourse.bacc as _bacc
    from concourse.bass_utils import run_bass_kernel_spmd as _run

    nc = _bacc.Bacc("TRN2", target_bir_lowering=False, num_devices=1)
    arrays, io = layouts(inputs), {}
    for n, v in arrays.items():
        io[n] = nc.dram_tensor("in_" + n, v.shape, mybir.dt.from_np(v.dtype), kind="ExternalInput").ap()
    io["out"] = nc.dram_tensor("out", (NB, S, D), F32, kind="ExternalOutput").ap()
    for n, (shape, dtype) in SCRATCH.items():
        io[n] = nc.dram_tensor(n, shape, dtype).ap()
    program(nc, io)
    return _run(nc, [{"in_" + n: v for n, v in arrays.items()}], core_ids=[0]).results[0]["out"]
```

```python
from contextlib import ExitStack

import numpy as np

import concourse.bass as bass
from concourse import mybir

F32 = mybir.dt.float32
BF16 = mybir.dt.bfloat16
F32R = mybir.dt.float32r
ALU = mybir.AluOpType
ACT = mybir.ActivationFunctionType
AX = mybir.AxisListType

P = 128
NB, S, D = 16, 128, 256
T = NB * S
DK = D // P
EPS_LN = 1e-5
BANK = 512


class Tally:

    def __init__(self, name, sem):
        self.name, self.sem, self.count = name, sem, 0

    def mark(self, instruction, by=1):
        instruction.then_inc(self.sem, by)
        self.count += by
        return (self, self.count)


class Core:

    def __init__(self, nc, stack):
        self.nc, self.stack = nc, stack
        self.reached = {}
        self.pe, self.act, self.dve, self.pool = (self.tally(n) for n in ("pe_done", "act_done", "dve_done", "pool_done"))
        self.banks = [stack.enter_context(nc.psum_tensor(f"bank{i}", [P, BANK], F32)) for i in range(8)]

    def tally(self, name):
        return Tally(name, self.stack.enter_context(self.nc.semaphore(name)))

    def sbuf(self, stack, name, shape, dtype=F32):
        return stack.enter_context(self.nc.sbuf_tensor(name, shape, dtype))

    def need(self, engine, *marks):
        for mark in marks:
            if mark is None:
                continue
            tally, value = mark
            key = (engine.engine, tally.name)
            if self.reached.get(key, 0) < value:
                engine.wait_ge(tally.sem, value)
                self.reached[key] = value

    def on_pe(self, make, *marks):
        self.need(self.nc.tensor, *marks)
        return self.pe.mark(make(self.nc.tensor))

    def on_act(self, make, *marks):
        self.need(self.nc.scalar, *marks)
        return self.act.mark(make(self.nc.scalar))

    def on_dve(self, make, *marks):
        self.need(self.nc.vector, *marks)
        return self.dve.mark(make(self.nc.vector))

    def on_pool(self, make, *marks):
        self.need(self.nc.gpsimd, (self.pool, self.pool.count), *marks)
        return self.pool.mark(make(self.nc.gpsimd))

    def load(self, dst, src, tally, *marks, queue=None):
        queue = queue or self.nc.sync
        self.need(queue, *marks)
        return tally.mark(queue.dma_start(dst, src), 16)

    def now(self):
        return [(t, t.count) for t in (self.pe, self.act, self.dve, self.pool) if t.count]

    def join(self, *more):
        marks = self.now() + list(more)
        for engine in (self.nc.tensor, self.nc.scalar, self.nc.vector, self.nc.gpsimd, self.nc.sync):
            self.need(engine, *marks)


def row_norm(c, w, tag, src, dst, ready, tiles=NB, eps=EPS_LN):
    stats = c.sbuf(w, f"{tag}_stats", [P, tiles, 6])
    mean_var = c.sbuf(w, f"{tag}_mean_var", [P, tiles, 2])
    rstd = c.sbuf(w, f"{tag}_rstd", [P, tiles])
    last = None
    for b in range(tiles):
        m = c.on_dve(lambda e: e.bn_stats(stats[:, b, :], src[:, b, :]), ready[b])
    for b in range(tiles):
        last = c.on_dve(lambda e: e.bn_aggr(mean_var[:, b, :], stats[:, b, :]), m)
    last = c.on_dve(lambda e: e.tensor_scalar(rstd[:, :], mean_var[:, :, 1], eps, None, ALU.add), last)
    root = c.on_act(lambda e: e.activation(rstd[:, :], rstd[:, :], ACT.Sqrt), last)
    inv = c.on_dve(lambda e: e.reciprocal(rstd[:, :], rstd[:, :]), root)
    return [c.on_dve(lambda e: e.tensor_scalar(dst[:, b, :], src[:, b, :], mean_var[:, b, 0:1], rstd[:, b:b + 1],
                                               ALU.subtract, ALU.mult), inv) for b in range(tiles)]


def to_columns(c, src, dst, ready, scale=None, bias=None, vectors_in=None, banks=(0, 1, 2, 3)):
    out, freed = [], {}
    for b in range(NB):
        bank = c.banks[banks[b % len(banks)]]
        for k in range(DK):
            t = c.on_pe(lambda e: e.transpose(bank[:, k * P:(k + 1) * P], src[:, b, k * P:(k + 1) * P], c.ident[:, :]),
                        ready[b], c.ident_ready, *freed.get(b % len(banks), ()))
        if scale is None:
            copy = lambda e: e.tensor_copy(dst[:, :, b * P:(b + 1) * P], bank[:, 0:DK * P].rearrange("p (k n) -> p k n", k=DK))
            marks = [c.on_dve(copy, t) if b % 2 else
                     c.on_act(lambda e: e.copy(dst[:, :, b * P:(b + 1) * P], bank[:, 0:DK * P].rearrange("p (k n) -> p k n", k=DK)), t)]
        else:
            marks = [c.on_act(lambda e: e.activation(dst[:, 0, b * P:(b + 1) * P], bank[:, 0:P], ACT.Identity,
                                                     bias=bias[:, 0:1], scale=scale[:, 0:1]), t, vectors_in),
                     c.on_act(lambda e: e.activation(dst[:, 1, b * P:(b + 1) * P], bank[:, P:2 * P], ACT.Identity,
                                                     bias=bias[:, 1:2], scale=scale[:, 1:2]), t, vectors_in)]
        freed[b % len(banks)] = marks
        out.append(marks[-1])
    return out


def split2(c, on_hi, src, hi, lo, *marks, lo_marks=()):
    copy = (lambda e: e.copy(hi, src)) if on_hi == c.on_act else (lambda e: e.tensor_copy(hi, src))
    m = on_hi(copy, *marks)
    return c.on_dve(lambda e: e.tensor_tensor(lo, src, hi.bitcast(F32), ALU.subtract), m, *lo_marks)


def product(c, out, weights, moving, start, stop, *marks):
    (w_hi, w_lo), (x_hi, x_lo) = weights, moving
    c.on_pe(lambda e: e.matmul(out, w_hi, x_hi, start=start, stop=False, skip_group_check=True), *marks)
    c.on_pe(lambda e: e.matmul(out, w_hi, x_lo, start=False, stop=False, skip_group_check=True))
    return c.on_pe(lambda e: e.matmul(out, w_lo, x_hi, start=False, stop=stop, skip_group_check=True))


HEADS, HD = 16, 8
POS = D
QPART = (0, 0, 0, 1, 1, 1, 2, 2, 2)
KPART = (0, 1, 2, 0, 1, 2, 0, 1, 2)
TERM_ROWS = len(QPART) * HD
MAX_ROWS = 3
TILES = 4


def layer0_attention(c, io):
    nc, resid, ctx = c.nc, c.resid, c.ctx
    with ExitStack() as w:
        sb = lambda name, shape, dtype=F32: c.sbuf(w, name, shape, dtype)
        wqT, wkT, wvT, woT = (sb(f"a_{n}", [P, P]) for n in ("wqT", "wkT", "wvT", "woT"))
        bias = sb("a_bias", [P, 4])
        normed = sb("a_normed", [P, NB, D])
        vaug = sb("a_vaug", [P, NB, 2, HEADS, HD + 1])
        SLOTS = 3
        whole = [sb(f"a_whole{i}", [P, 2, BANK]) for i in range(SLOTS)]
        parts = [sb(f"a_parts{i}", [P, 2, 3, BANK], BF16) for i in range(SLOTS)]
        RING = 4
        rows = TERM_ROWS + MAX_ROWS
        qs = [sb(f"a_qs{i}", [rows, HEADS, POS], BF16) for i in range(RING)]
        ks = [sb(f"a_ks{i}", [96, HEADS, POS], BF16) for i in range(RING)]
        negmax = [sb(f"a_negmax{i}", [P, HEADS, 2]) for i in range(2)]
        mrow = [sb(f"a_mrow{i}", [32, P]) for i in range(2)]
        mparts = [sb(f"a_mparts{i}", [32, 3, P], BF16) for i in range(2)]
        EXPS = 8
        expo = [sb(f"a_exp{i}", [P, 2, POS]) for i in range(EXPS)]
        inv = [sb(f"a_inv{i}", [P, 2, TILES]) for i in range(2)]
        outq = [sb(f"a_outq{i}", [P, 2, HEADS, HD]) for i in range(2)]
        sumT = [sb(f"a_sumT{i}", [P, POS]) for i in range(2)]
        outT = [sb(f"a_outT{i}", [P, POS]) for i in range(2)]
        proj = [sb(f"a_proj{i}", [P, POS]) for i in range(2)]

        weights_in, x_in, ctx_in = c.tally("a_weights_in"), c.x_in, c.ctx_in
        for dst, name in ((wqT, "wqT"), (wkT, "wkT"), (wvT, "wvT"), (woT, "woT")):
            c.load(dst[:, :], io["a_" + name], weights_in)
        weights = c.load(bias[:, :], io["a_bias"], weights_in)

        ones = c.on_dve(lambda e: e.memset(vaug[:, :, :, :, HD], 1.0))
        ks_ones = [c.on_pool(lambda e: e.memset(ks[r][64:96, :, :], 1.0)) for r in range(RING)]

        stacked, stored = {}, {}
        stack_in = [c.tally(f"a_stack_in{i}") for i in range(RING)]
        max_in = [c.tally(f"a_max_in{i}") for i in range(RING)]

        def stack(b, *free):
            r, parts_of = b % RING, lambda n: io[f"a_{n}_parts"][b].rearrange("t (d h) n -> t d (h n)", d=HD)
            flat = lambda t, first, count: t[first * HD:(first + count) * HD, :, :].rearrange("p h n -> p (h n)")
            for t in range(3):
                c.load(flat(qs[r], 3 * t, 3), parts_of("q")[t].unsqueeze(0).broadcast_to([3, HD, HEADS * POS]), stack_in[r],
                       stored[0, b // 2], stored[1, b // 2], ks_ones[r], *free)
                m = c.load(flat(ks[r], 3 * t, 3), parts_of("k"), stack_in[r])
            return m

        norm = row_norm(c, w, "a", resid, normed, x_in)
        split_out = {n: [c.tally(f"a_{n}_out{i}") for i in range(NB // 2)] for n in "qk"}
        freed, rounded = {}, {}

        def project(i):
            r = i % SLOTS
            for n, (wT, src, b) in enumerate(((wqT, normed, 0), (wkT, ctx, 1))):
                bank = c.banks[n + 4 * (i % 2)]
                pe = c.on_pe(lambda e: e.matmul(bank[:, :], wT[:, :], src[:, 2 * i:2 * i + 2, :].rearrange("p b n -> p (b n)"),
                                                start=True, stop=True),
                             weights, norm[2 * i + 1] if n == 0 else None, *(ctx_in[2 * i:2 * i + 2] if n else ()),
                             freed.get((n, i % 2)))
                c.on_act(lambda e: e.activation(whole[r][:, n, :], bank[:, :], ACT.Identity, bias=bias[:, b:b + 1]),
                         pe, stored.get((n, i - SLOTS)))
                rounded[n, i] = freed[n, i % 2] = c.on_act(
                    lambda e: e.activation(parts[r][:, n, 0, :], bank[:, :], ACT.Identity, bias=bias[:, b:b + 1]))
            bank = c.banks[2 + 4 * (i % 2)]
            for j in range(4):
                b, kb = 2 * i + j // 2, j % 2
                pe = c.on_pe(lambda e: e.matmul(bank[:, j * P:(j + 1) * P], ctx[:, b, kb * P:(kb + 1) * P], wvT[:, :],
                                                start=True, stop=True), freed.get(("v", i % 2)))
            freed["v", i % 2] = v_ready = c.on_dve(
                lambda e: e.tensor_copy(vaug[:, 2 * i:2 * i + 2, :, :, 0:HD].rearrange("p b k h d -> p (b k) h d"),
                                        bank[:, :].rearrange("p (j h d) -> p j h d", j=4, h=HEADS)), pe, ones)
            return v_ready

        def split(i):
            r = i % SLOTS
            for n, on in enumerate((c.on_dve, c.on_pool)):
                x, part = whole[r][:, n, :], parts[r][:, n, :, :]
                m = on(lambda e: e.tensor_tensor(x, x, part[:, 0, :], ALU.subtract), rounded[n, i])
                m = c.on_act(lambda e: e.copy(part[:, 1, :], x), m)
                done = on(lambda e: e.tensor_tensor(part[:, 2, :], x, part[:, 1, :], ALU.subtract), m)
                for j in range(2):
                    stored[n, i] = c.load(io[f"a_{'qk'[n]}_parts"][2 * i + j].rearrange("t p n -> p t n"),
                                          part[:, :, j * POS:(j + 1) * POS], split_out["qk"[n]][i], done)

        for i in range(NB // 2 + 1):
            if i < NB // 2:
                v_ready = project(i)
            if i >= 1:
                split(i - 1)
            if i == 4:
                stacked[0] = stack(0)
        bank_free = {n: [(c.pe, c.pe.count), (c.act, c.act.count), freed["v", 0], freed["v", 1]] for n in range(8)}
        for b in range(1, RING):
            stacked[b] = stack(b)

        max_rows, max_done, mfree = {}, {}, {}

        def score_max(b, h):
            bank = h % 2
            for qb in range(2):
                pe = c.on_pe(lambda e: e.matmul(c.banks[bank][:, qb * POS:(qb + 1) * POS], qs[b % RING][0:TERM_ROWS, h, qb * P:(qb + 1) * P],
                                                ks[b % RING][0:TERM_ROWS, h, :], start=True, stop=True), stacked[b], *bank_free[bank])
            m = c.on_dve(lambda e: e.tensor_reduce(negmax[b % 2][:, h, :], c.banks[bank][:, :].rearrange("p (q n) -> p q n", q=2),
                                                   AX.X, ALU.max, negate=True), pe, mfree.get(b % 2))
            bank_free[bank] = [m]
            max_done[b] = m

        def max_to_rows(b):
            i, bank = b % 2, c.banks[7]
            pe = c.on_pe(lambda e: e.transpose(bank[0:32, 0:P], negmax[i][:, :, :].rearrange("p h q -> p (h q)"), c.ident[:, :]),
                         max_done[b], c.ident_ready, *bank_free[7])
            mfree[i] = pe
            c.on_act(lambda e: e.copy(mrow[i][:, :], bank[0:32, 0:P]), pe, max_rows.get(b - 2))
            a = c.on_act(lambda e: e.copy(mparts[i][:, 0, :], bank[0:32, 0:P]))
            bank_free[7] = [a]
            m = c.on_pool(lambda e: e.tensor_tensor(mrow[i][:, :], mrow[i][:, :], mparts[i][:, 0, :], ALU.subtract), a)
            m = c.on_pool(lambda e: e.tensor_copy(mparts[i][:, 1, :], mrow[i][:, :]), m)
            done = c.on_pool(lambda e: e.tensor_tensor(mparts[i][:, 2, :], mrow[i][:, :], mparts[i][:, 1, :], ALU.subtract), m)
            for part in range(MAX_ROWS):
                row = TERM_ROWS + part
                max_rows[b] = c.load(qs[b % RING][row:row + 1, :, :].rearrange("o h (q n) -> o (h q) n", q=2),
                                     mparts[i][:, part, :], max_in[b % RING], done)

        exp_done, exp_free, added, divided = {}, {}, {}, {}
        GROUPS = HEADS // TILES

        def exponentials(b, h):
            bank, n = 2 + h % 2, (b * HEADS + h) % EXPS
            for kb in range(2):
                pe = c.on_pe(lambda e: e.matmul(c.banks[bank][:, kb * POS:(kb + 1) * POS], ks[b % RING][0:rows, h, kb * P:(kb + 1) * P],
                                                qs[b % RING][0:rows, h, :], start=True, stop=True), max_rows[b], *bank_free[bank])
            exp_done[b, h] = c.on_act(lambda e: e.activation(expo[n][:, :, :].rearrange("p k q -> p (k q)"), c.banks[bank][:, :], ACT.Exp,
                                                             scale=float(1 / np.sqrt(np.float32(P)))), pe, exp_free.get(n))
            bank_free[bank] = [exp_done[b, h]]

        def times_v(b, g):
            bank = 4 + g % 2
            for kb in range(2):
                for tile in range(TILES):
                    h = TILES * g + tile
                    n = (b * HEADS + h) % EXPS
                    pe = c.on_pe(lambda e: e.matmul(
                        c.banks[bank][32 * tile:32 * tile + HD + 1, 0:POS], vaug[:, b, kb, h, :], expo[n][:, kb, :],
                        start=kb == 0, stop=kb == 1), exp_done[b, h], v_ready, *bank_free[bank])
                    if kb == 1:
                        exp_free[n] = pe
            a = c.on_act(lambda e: e.copy(sumT[g % 2][:, :], c.banks[bank][:, 0:POS]), pe, divided.get((b, g - 2), divided.get((b - 1, g + 2))))
            bank_free[bank] = [a]
            return a

        def normalise(b, g, copied):
            i, bank = b % 2, c.banks[6]
            for qb in range(2):
                pe = c.on_pe(lambda e: e.transpose(bank[:, qb * P:(qb + 1) * P], sumT[g % 2][:, qb * P:(qb + 1) * P], c.ident[:, :]),
                             copied, *bank_free[6])
            view = bank[:, 0:2 * P].rearrange("p (q h d) -> p q h d", q=2, h=TILES)
            m = c.on_dve(lambda e: e.reciprocal(inv[g % 2][:, :, :], view[:, :, :, HD]), pe)
            m = c.on_dve(lambda e: e.tensor_tensor(outq[i][:, :, TILES * g:TILES * (g + 1), :], view[:, :, :, 0:HD],
                                                   inv[g % 2][:, :, :].unsqueeze(3).to_broadcast([P, 2, TILES, HD]), ALU.mult), m, added.get(b - 2))
            bank_free[6] = [m]
            divided[b, g] = pe
            return m

        def to_features(b, ready):
            i, bank = b % 2, c.banks[7]
            for qb in range(2):
                pe = c.on_pe(lambda e: e.transpose(bank[:, qb * P:(qb + 1) * P], outq[i][:, qb, :, :].rearrange("p h d -> p (h d)"),
                                                   c.ident[:, :]), ready, *bank_free[7])
            a = c.on_act(lambda e: e.activation(outT[i][:, :], bank[:, 0:POS], ACT.Identity, bias=bias[:, 2:3]), pe)
            bank_free[7] = [a]
            return a

        def residual(b, ready):
            i, bank = b % 2, c.banks[7]
            pe = c.on_pe(lambda e: e.matmul(bank[:, 0:POS], woT[:, :], outT[i][:, :], start=True, stop=True), ready, *bank_free[7])
            a = c.on_act(lambda e: e.activation(proj[i][:, :], bank[:, 0:POS], ACT.Identity, bias=bias[:, 3:4]), pe, added.get(b - 2))
            bank_free[7] = [a]
            added[b] = c.on_dve(lambda e: e.scalar_tensor_tensor(resid[:, b, :], proj[i][:, :], c.gates[:, 0:1], resid[:, b, :],
                                                                 ALU.mult, ALU.add), a, c.gates_ready)

        for bank in (4, 5):
            bank_free[bank] = bank_free[bank] + [c.on_dve(lambda e: e.memset(c.banks[bank][:, :], 0.0), *bank_free[bank])]

        PAIRS = HEADS // 2
        AHEAD = HEADS + 3 * HEADS // 4

        def maxima(i):
            if i < NB * HEADS:
                score_max(*divmod(i, HEADS))
            b, h = divmod(i - 2, HEADS)
            if h == HEADS - 1 and 0 <= b < NB:
                max_to_rows(b)

        for i in range(AHEAD):
            maxima(i)
        copied, ended = {}, {}
        for n in range(NB * PAIRS + 6):
            b, j = divmod(n, PAIRS)
            for h in (2 * j, 2 * j + 1):
                maxima(b * HEADS + h + AHEAD)
                if b < NB:
                    exponentials(b, h)
            if n % 2 == 0 and 2 <= n < NB * PAIRS + 2:
                b, g = divmod((n - 2) // 2, GROUPS)
                copied[b, g] = times_v(b, g)
            if n % 2 == 1 and 3 <= n < NB * PAIRS + 3:
                b, g = divmod((n - 3) // 2, GROUPS)
                ended[b] = normalise(b, g, copied[b, g])
            if n >= 12 and (n - 12) % PAIRS == 0:
                ended[n // PAIRS - 1] = to_features(n // PAIRS - 1, ended[n // PAIRS - 1])
            if n >= 13 and (n - 13) % PAIRS == 0:
                residual(n // PAIRS - 1, ended[n // PAIRS - 1])
            b, j = divmod(n, PAIRS)
            if j == PAIRS - 1 and b + RING < NB:
                stacked[b + RING] = stack(b + RING, (c.pe, c.pe.count))
        c.join()


EXPERTS, WIDTH, TOP = 64, 64, 8
PAIRS = EXPERTS // 2


def layer0_experts(c, io):
    nc, resid, xT = c.nc, c.resid, c.columns
    with ExitStack() as w:
        sb = lambda name, shape, dtype=F32: c.sbuf(w, name, shape, dtype)
        RING, SPLITS = 4, 3
        GU = DK * 2 * P
        raw = [sb(f"e_raw{i}", [P, GU + D]) for i in range(RING)]
        split = [[sb(f"e_weights_{n}{i}", [P, GU + D], F32R) for n in ("hi", "lo")] for i in range(SPLITS)]
        x_split = [sb(f"e_x_{n}", [P, DK, T], F32R) for n in ("hi", "lo")]
        TOKENS = T // 2
        comb_wide = [sb(f"e_comb_wide{i}", [P, TOKENS]) for i in range(RING)]
        loaded = [c.tally(f"e_loaded{i}") for i in range(RING)]
        comb_loaded = [c.tally(f"e_comb_loaded{i}") for i in range(RING)]
        router = sb("e_router", [P, DK, EXPERTS + 1])
        router_in = c.load(router[:, :, :], io["e_router"], c.tally("e_router_in"))
        comb = sb("e_comb", [P, NB, EXPERTS + 1])
        combT = sb("e_comb_rows", [EXPERTS + 1, T])

        weights_in, raw_free, split_free, split_done, comb_free = {}, {}, {}, {}, {}
        units = [(half, pair) for half in range(2) for pair in range(PAIRS + 1)]

        def load_weights(u):
            pair, r = units[u][1], u % RING
            if pair < PAIRS:
                weights_in[u] = c.load(raw[r][:, :], io["e_weights"][pair], loaded[r], raw_free.get(r))
            else:
                c.load(raw[r][:, 0:GU // 2], io["e_shared_gate_up"], loaded[r], raw_free.get(r))
                weights_in[u] = c.load(raw[r][0:WIDTH, GU:], io["e_shared_down"], loaded[r])

        def split_weights(u):
            r, i = u % RING, u % SPLITS
            spans = [(P, slice(0, GU + D))] if units[u][1] < PAIRS else [(P, slice(0, GU // 2)), (WIDTH, slice(GU, GU + D))]
            for rows, cols in spans:
                src, (hi, lo) = raw[r][0:rows, cols], (t[0:rows, cols] for t in split[i])
                split_done[u] = raw_free[r] = split2(c, c.on_act, src, hi, lo, weights_in[u], split_free.get(i))

        for u in range(RING - 1):
            load_weights(u)

        with ExitStack() as w2:
            s2 = lambda name, shape, dtype=F32: c.sbuf(w2, name, shape, dtype)
            normed = s2("e_normed", [P, NB, D])
            probs, left = s2("e_probs", [P, NB, EXPERTS]), s2("e_left", [P, NB, EXPERTS])
            logits = s2("e_logits", [P, NB, EXPERTS + 1])
            best = s2("e_best", [P, NB, TOP])
            peak, total, weight = (s2(f"e_{n}", [P, NB]) for n in ("peak", "total", "weight"))
            norm = row_norm(c, w2, "e", resid, normed, c.x_in)
            columns = to_columns(c, normed, xT, norm)
            GROUP = 4
            for g in range(NB // GROUP):
                cols = slice(g * BANK, (g + 1) * BANK)
                x_ready = split2(c, c.on_pool, xT[:, :, cols], *(t[:, :, cols] for t in x_split), *columns[4 * g:4 * g + 4])
            for g in range(NB // GROUP):
                bank = c.banks[4 + g]
                for i in range(GROUP):
                    b = g * GROUP + i
                    for k in range(DK):
                        pe = c.on_pe(lambda e: e.matmul(bank[:, i * (EXPERTS + 1):(i + 1) * (EXPERTS + 1)], xT[:, k, b * P:(b + 1) * P],
                                                        router[:, k, :], start=k == 0, stop=k == DK - 1), columns[b], router_in)
                a = c.on_act(lambda e: e.copy(logits[:, g * GROUP:(g + 1) * GROUP, :], bank[:, 0:GROUP * (EXPERTS + 1)]
                                              .rearrange("p (b n) -> p b n", b=GROUP)), pe)
            wide = lambda t: t[:, :].unsqueeze(2).to_broadcast([P, NB, EXPERTS])
            routed = logits[:, :, 0:EXPERTS]
            m = c.on_dve(lambda e: e.tensor_reduce(peak[:, :], routed, AX.X, ALU.max), a)
            m = c.on_dve(lambda e: e.tensor_tensor(probs[:, :, :], routed, wide(peak), ALU.subtract), m)
            m = c.on_act(lambda e: e.activation(probs[:, :, :], probs[:, :, :], ACT.Exp), m)
            shared = c.on_act(lambda e: e.activation(comb[:, :, EXPERTS], logits[:, :, EXPERTS], ACT.Exp, scale=-1.0))
            m = c.on_dve(lambda e: e.tensor_reduce(total[:, :], probs[:, :, :], AX.X, ALU.add), m)
            m = c.on_dve(lambda e: e.reciprocal(total[:, :], total[:, :]), m)
            m = c.on_dve(lambda e: e.tensor_tensor(probs[:, :, :], probs[:, :, :], wide(total), ALU.mult), m)
            for b in range(NB):
                m8 = c.on_dve(lambda e: e.max(best[:, b, :], probs[:, b, :]), m)
            for b in range(NB):
                m = c.on_dve(lambda e: e.match_replace(left[:, b, :], best[:, b, :], probs[:, b, :], -1.0), m8)
            m = c.on_dve(lambda e: e.tensor_reduce(weight[:, :], best[:, :, :], AX.X, ALU.add), m)
            m = c.on_dve(lambda e: e.reciprocal(weight[:, :], weight[:, :]), m)
            m = c.on_dve(lambda e: e.scalar_tensor_tensor(left[:, :, :], left[:, :, :], 0.0, probs[:, :, :], ALU.is_lt, ALU.mult), m)
            m = c.on_dve(lambda e: e.tensor_tensor(comb[:, :, 0:EXPERTS], left[:, :, :], wide(weight), ALU.mult), m)
            m = c.on_dve(lambda e: e.tensor_scalar(comb[:, :, EXPERTS], comb[:, :, EXPERTS], 1.0, None, ALU.add), shared)
            comb_ready = c.on_dve(lambda e: e.reciprocal(comb[:, :, EXPERTS], comb[:, :, EXPERTS]), m)
            for g in range(NB // GROUP):
                for i in range(GROUP):
                    pe = c.on_pe(lambda e: e.transpose(c.banks[4 + g][0:EXPERTS + 1, i * P:(i + 1) * P], comb[:, g * GROUP + i, :],
                                                       c.ident[:, :]), comb_ready, a)
                a2 = c.on_act(lambda e: e.copy(combT[:, g * BANK:(g + 1) * BANK], c.banks[4 + g][0:EXPERTS + 1, :]), pe)
            comb_stored = c.load(io["e_combT"], combT[:, :], c.tally("e_comb_stored"), a2)
            split_weights(0)
            free_after_router = c.now()

        def load_comb(u):
            (half, pair), r = units[u], u % RING
            cols = slice(half * TOKENS, (half + 1) * TOKENS)
            for i in range(2 if pair < PAIRS else 1):
                m = c.load(comb_wide[r][i * WIDTH:(i + 1) * WIDTH, :],
                           io["e_combT"][2 * pair + i:2 * pair + i + 1, cols].broadcast_to([WIDTH, TOKENS]),
                           comb_loaded[r], comb_stored, comb_free.get(r))
            comb_in[u] = m

        with ExitStack() as w3:
            s3 = lambda name, shape, dtype=F32: c.sbuf(w3, name, shape, dtype)
            HR = 3
            silu = [s3(f"e_silu{i}", [P, BANK]) for i in range(2)]
            gated = [s3(f"e_gated{i}", [P, BANK]) for i in range(2)]
            hidden = [s3(f"e_hidden{i}", [P, BANK]) for i in range(2)]
            hidden_split = [[s3(f"e_hidden_{n}{i}", [P, BANK], F32R) for n in ("hi", "lo")] for i in range(HR)]
            comb_in, bank_free = {}, {n: free_after_router for n in range(8)}
            chunks = TOKENS // BANK
            steps = [(u, chunk) for u in range(len(units)) for chunk in range(chunks)]
            rows_of = lambda n: P if units[steps[n][0]][1] < PAIRS else WIDTH
            down_done, weighed, ready, gated_free, silu_free = {}, {}, {}, {}, {}

            def gate_and_up(n):
                u, chunk = steps[n]
                (half, pair), r, i, rows = units[u], u % RING, n % 2, rows_of(n)
                cols = slice(half * TOKENS + chunk * BANK, half * TOKENS + (chunk + 1) * BANK)
                for which in range(2):
                    bank = 2 * i + which
                    for k in range(DK):
                        at = (2 * k + which) * rows
                        pe = product(c, c.banks[bank][0:rows, :], [t[:, at:at + rows] for t in split[u % SPLITS]],
                                     [t[:, k, cols] for t in x_split], k == 0, k == DK - 1, split_done[u], x_ready, *bank_free[bank])
                    if which == 0:
                        a = c.on_act(lambda e: e.activation(silu[i][0:rows, :], c.banks[bank][0:rows, :], ACT.Silu), pe, silu_free.get(n - 2))
                        bank_free[bank] = [a]
                m = c.on_dve(lambda e: e.tensor_tensor(gated[i][0:rows, :], silu[i][0:rows, :], c.banks[bank][0:rows, :], ALU.mult), a, pe,
                             gated_free.get(n - 2))
                bank_free[bank], silu_free[n] = [m], m
                gated_free[n] = weighed[n] = comb_free[r] = c.on_pool(
                    lambda e: e.tensor_tensor(hidden[i][0:rows, :], gated[i][0:rows, :], comb_wide[r][0:rows, chunk * BANK:(chunk + 1) * BANK],
                                              ALU.mult), m, comb_in[u], ready.get(n - 2))

            def split_hidden(n):
                rows = rows_of(n)
                ready[n] = split2(c, c.on_act, hidden[n % 2][0:rows, :], *(t[0:rows, :] for t in hidden_split[n % HR]),
                                  weighed[n], down_done.get(n - HR))

            def to_out(n):
                u, chunk = steps[n]
                (half, pair), rows = units[u], rows_of(n)
                for t in range(BANK // P):
                    tile = chunk * (BANK // P) + t
                    bank = 4 + tile // 2
                    pe = product(c, c.banks[bank][:, (tile % 2) * D:(tile % 2 + 1) * D], [h[0:rows, t * P:(t + 1) * P] for h in hidden_split[n % HR]],
                                 [v[0:rows, GU:] for v in split[u % SPLITS]], pair == 0 and tile % 2 == 0, pair == PAIRS, ready[n], *bank_free[bank])
                down_done[n] = split_free[u % SPLITS] = pe
                if pair == PAIRS:
                    for bank in (4 + 2 * chunk, 5 + 2 * chunk):
                        b = half * NB // 2 + 2 * (bank - 4)
                        bank_free[bank] = [c.on_dve(lambda e: e.scalar_tensor_tensor(
                            resid[:, b:b + 2, :], c.banks[bank][:, :].rearrange("p (b n) -> p b n", b=2), c.gates[:, 1:2], resid[:, b:b + 2, :],
                            ALU.mult, ALU.add), pe, c.gates_ready)]

            for u in range(RING - 1):
                load_comb(u)
            LAG = 2
            head_mean = s3("e_head_mean", [P, NB, CELLS])
            for n in range(len(steps) + LAG):
                if n < NB:
                    c.ctx_centred = centre_context(c, head_mean, n, *free_after_router)
                if 1 <= n <= len(steps):
                    split_hidden(n - 1)
                if n < len(steps):
                    gate_and_up(n)
                    u, chunk = steps[n]
                    if chunk == chunks - 1 and u + RING - 1 < len(units):
                        load_weights(u + RING - 1)
                        load_comb(u + RING - 1)
                if n >= LAG:
                    to_out(n - LAG)
                if n < len(steps) and steps[n][1] == 0 and steps[n][0] + 1 < len(units):
                    split_weights(steps[n][0] + 1)
            c.join()


CELLS, CD = 16, 16
CELL_EPS = 1e-6
LOWEST = -3e38
SPAN = 32


def centre_context(c, mean, b, *ready):
    heads = c.ctx[:, b, :].rearrange("p (h d) -> p h d", h=CELLS)
    m = c.on_dve(lambda e: e.tensor_reduce(mean[:, b, :], heads, AX.X, ALU.add), *ready)
    m = c.on_dve(lambda e: e.tensor_scalar(mean[:, b, :], mean[:, b, :], 1.0 / CD, None, ALU.mult), m)
    return c.on_dve(lambda e: e.tensor_tensor(heads, heads, mean[:, b, :].unsqueeze(2).to_broadcast([P, CELLS, CD]), ALU.subtract), m)


def layer1_mlstm(c, io):
    nc, resid, ctx, xT = c.nc, c.resid, c.ctx, c.columns
    with ExitStack() as w:
        sb = lambda name, shape, dtype=F32: c.sbuf(w, name, shape, dtype)
        ctxT = sb("m_ctxT", [P, DK, T])
        ctxT_in = c.load(ctxT[:, :, :], io["m_ctxT"].rearrange("(k p) t -> p k t", p=P), c.tally("m_ctxT_in"))
        small_in = c.tally("m_small_in")
        gate_w = sb("m_gate_w", [P, 3 * DK, 2 * SPAN])
        gate_bias, head_mask, ln_scale = sb("m_gate_bias", [P, 2]), sb("m_head_mask", [P, CELLS // DK]), sb("m_ln_scale", [P, D])
        for dst, src in ((gate_w[:, :, :], io["m_gate_w"]), (gate_bias[:, :], io["m_gate_bias"]), (head_mask[:, :], io["m_head_mask"])):
            c.load(dst, src, small_in)
        small = c.load(ln_scale[:, :], io["m_ln_scale"].broadcast_to([P, D]), small_in)
        vaug = sb("m_vaug", [P, NB, CELLS, CD + 1])
        g_token, e_token = sb("m_g_token", [P, NB, CELLS]), sb("m_e_token", [P, NB, CELLS])
        square_sum, inv_norm = sb("m_square_sum", [P, NB * CELLS]), sb("m_inv_norm", [P, NB * CELLS])
        cell = sb("m_cell", [P, NB, D])

        c.on_dve(lambda e: e.memset(vaug[:, :, :, CD], 1.0))
        vaug_ready = c.on_dve(lambda e: e.tensor_copy(vaug[:, :, :, 0:CD], ctx[:, :, :].rearrange("p b (h d) -> p b h d", h=CELLS)), c.ctx_centred)

        with ExitStack() as w2:
            s2 = lambda name, shape, dtype=F32: c.sbuf(w2, name, shape, dtype)
            for which, bank in ((0, 5), (1, 4)):
                for n in range(T // BANK):
                    rows = slice(n * SPAN, (n + 1) * SPAN)
                    for k in range(DK, 3 * DK):
                        c.on_pe(lambda e: e.matmul(c.banks[bank][rows, :], gate_w[:, k, which * SPAN:(which + 1) * SPAN],
                                                   ctxT[:, k % DK, n * BANK:(n + 1) * BANK], start=k == DK, stop=False, skip_group_check=True),
                                small, ctxT_in)
            with ExitStack() as w3:
                normed = c.sbuf(w3, "m_normed", [P, NB, D])
                norm = row_norm(c, w3, "m", resid, normed, c.x_in)
                columns = to_columns(c, normed, xT, norm)
            ig, fg, scratch, keep, drop, peak = (s2(f"m_{n}", [P, BANK]) for n in ("ig", "fg", "scratch", "keep", "drop", "peak"))
            first = lambda t: t[:, :].rearrange("p (b t) -> p b t", t=P)[:, :, 0]
            m0 = c.on_pool(lambda e: e.memset(keep[:, :], 1.0), columns[-1])
            m0 = c.on_pool(lambda e: e.memset(drop[:, :], 0.0))
            m0 = c.on_pool(lambda e: e.memset(first(keep), 0.0))
            resets = c.on_pool(lambda e: e.memset(first(drop), LOWEST))
            for which, bank in ((0, 5), (1, 4)):
                for n in range(T // BANK):
                    cols, rows = slice(n * BANK, (n + 1) * BANK), slice(n * SPAN, (n + 1) * SPAN)
                    for k in range(DK):
                        pe = c.on_pe(lambda e: e.matmul(c.banks[bank][rows, :], gate_w[:, k, which * SPAN:(which + 1) * SPAN], xT[:, k, cols],
                                                        start=False, stop=k == DK - 1, skip_group_check=True), *columns[4 * n:4 * n + 4])
                if which == 0:
                    i_done = pe
            a = c.on_act(lambda e: e.activation(fg[:, :], c.banks[4][:, :], ACT.Identity, bias=gate_bias[:, 1:2]), pe, columns[-1])
            i_ready = gates_read = c.on_act(lambda e: e.activation(ig[:, :], c.banks[5][:, :], ACT.Identity, bias=gate_bias[:, 0:1]), i_done)
            m = c.on_dve(lambda e: e.scalar_tensor_tensor(scratch[:, :], fg[:, :], -1.0, fg[:, :], ALU.mult, ALU.min), a)
            m = c.on_act(lambda e: e.activation(scratch[:, :], scratch[:, :], ACT.Exp), m)
            m = c.on_act(lambda e: e.activation(scratch[:, :], scratch[:, :], ACT.Ln, bias=1.0), m)
            m = c.on_dve(lambda e: e.scalar_tensor_tensor(scratch[:, :], fg[:, :], 0.0, scratch[:, :], ALU.min, ALU.subtract), m)
            m = c.on_dve(lambda e: e.tensor_tensor_scan(fg[:, :], keep[:, :], scratch[:, :], 0.0, ALU.mult, ALU.add), m, resets)
            g = c.on_dve(lambda e: e.tensor_tensor(ig[:, :], ig[:, :], fg[:, :], ALU.subtract), m, i_ready)
            m = c.on_dve(lambda e: e.tensor_tensor_scan(peak[:, :], drop[:, :], ig[:, :], 0.0, ALU.add, ALU.max), g)
            neg = c.on_dve(lambda e: e.tensor_scalar(scratch[:, :], peak[:, :], -1.0, None, ALU.mult), m)
            peak_stored = c.tally("m_peak_stored")
            for n in range(T // BANK):
                negpeak_in = c.load(io["m_negpeak"][:, n * BANK:(n + 1) * BANK], scratch[n * SPAN:n * SPAN + CELLS, :], peak_stored, neg)
            peak_stored = negpeak_in
            m = c.on_dve(lambda e: e.tensor_tensor(fg[:, :], fg[:, :], peak[:, :], ALU.add), m)
            a = c.on_act(lambda e: e.activation(fg[:, :], fg[:, :], ACT.Exp, scale=-1.0), m)
            for rows, bank, dst, ready in ((ig, 6, g_token, g), (fg, 7, e_token, a)):
                for j in range(BANK // P):
                    pe = c.on_pe(lambda e: e.transpose(c.banks[bank][:, j * P:(j + 1) * P], rows[:, j * P:(j + 1) * P], c.ident[:, :]), ready)
                by_token = c.banks[bank][:, :].rearrange("p (j n h) -> p n j h", j=BANK // P, n=T // BANK)[:, :, :, 0:CELLS]
                a = c.on_act(lambda e: e.copy(dst[:, :, :].rearrange("p (n j) h -> p n j h", n=T // BANK), by_token), pe)
            token_ready = a
            scans_done = c.now() + [peak_stored]

        with ExitStack() as w2:
            s2 = lambda name, shape, dtype=F32: c.sbuf(w2, name, shape, dtype)
            RING = 3
            qblock = [s2(f"m_qblock{i}", [P, DK, CELLS // DK, P]) for i in range(2)]
            decay = [s2(f"m_decay{i}", [P, CELLS, P]) for i in range(RING)]
            product = [s2(f"m_product{i}", [P, CELLS, P]) for i in range(2)]
            sums = [s2(f"m_sums{i}", [P, BANK]) for i in range(2)]
            row_sums = [s2(f"m_row_sums{i}", [P, CELLS]) for i in range(2)]
            square = [s2(f"m_square{i}", [P, D]) for i in range(2)]
            denom = [s2(f"m_denom{i}", [P, CELLS]) for i in range(2)]
            peak_in = [c.tally(f"m_peak_in{i}") for i in range(RING)]
            bank_free = {n: scans_done for n in range(8)}
            for bank in (4, 5):
                bank_free[bank] = [c.on_dve(lambda e: e.memset(c.banks[bank][:, :], 0.0), *scans_done)]
            masked, decayed, multiplied, sums_free, out = {}, {}, {}, {}, {}
            per_half = CELLS // DK

            def decay_of(b):
                d = decay[b % RING]
                arrived = c.load(d[:, :, :], io["m_negpeak"].rearrange("h (b s) -> b h s", b=NB)[b].unsqueeze(0).broadcast_to([P, CELLS, P]),
                                 peak_in[b % RING], peak_stored, *scans_done, multiplied.get(b - RING))
                gt = g_token[:, b, :].unsqueeze(2).to_broadcast([P, CELLS, P])
                m = c.on_dve(lambda e: e.tensor_tensor(d[:, :, :], d[:, :, :], gt, ALU.add), arrived, token_ready)
                m = c.on_pool(lambda e: e.affine_select(out=d[:, :, :], in_=d[:, :, :], compare_op=ALU.is_ge, fill=LOWEST, base=0,
                                                        pattern=[[0, CELLS], [1, P]], channel_multiplier=-1), m)
                masked[b] = m

            def exponential(b):
                d = decay[b % RING]
                decayed[b] = c.on_act(lambda e: e.activation(d[:, :, :], d[:, :, :], ACT.Exp), masked[b])

            def block_queries(b):
                q = xT[:, 0, b * P:(b + 1) * P].unsqueeze(1).to_broadcast([P, per_half, P])
                h = head_mask[:, :].unsqueeze(2).to_broadcast([P, per_half, P])
                m = c.on_pool(lambda e: e.tensor_tensor(qblock[b % 2][:, 0, :, :], q, h, ALU.mult), *scans_done, scored.get(b - 2))
                for h in range(per_half):
                    a = c.on_act(lambda e: e.activation(qblock[b % 2][:, 1, h, :], xT[:, 1, b * P:(b + 1) * P], ACT.Identity,
                                                        scale=head_mask[:, h:h + 1]), *scans_done, scored.get(b - 2))
                blocked[b] = [m, a]

            blocked, scored, copied = {}, {}, {}

            def scores(b):
                for i in range(4):
                    k, q4 = divmod(i, 2)
                    pe = c.on_pe(lambda e: e.matmul(c.banks[i][:, :], ctxT[:, k, b * P:(b + 1) * P],
                                                    qblock[b % 2][:, k, 4 * q4:4 * q4 + 4, :].rearrange("p h s -> p (h s)"),
                                                    start=True, stop=True), *blocked[b], *bank_free[i])
                    m = c.on_dve(lambda e: e.tensor_tensor(product[b % 2][:, 4 * i:4 * i + 4, :].rearrange("p h s -> p (h s)"), c.banks[i][:, :],
                                                           decay[b % RING][:, 4 * i:4 * i + 4, :].rearrange("p h s -> p (h s)"), ALU.mult),
                                 pe, decayed[b], out.get(b - 2))
                    bank_free[i] = [m]
                scored[b], multiplied[b] = pe, m

            def times_v(b):
                bank = 4 + b % 2
                for i in range(4):
                    for tile in range(4):
                        h = 4 * i + tile
                        pe = c.on_pe(lambda e: e.matmul(c.banks[bank][32 * tile:32 * tile + CD + 1, i * P:(i + 1) * P], vaug[:, b, h, :],
                                                        product[b % 2][:, h, :], start=True, stop=True),
                                     multiplied[b], vaug_ready, *bank_free[bank])
                out[b] = pe
                a = c.on_act(lambda e: e.copy(sums[b % 2][:, :], c.banks[bank][:, :]), pe, sums_free.get(b - 2))
                bank_free[bank] = [a]
                return a

            def by_token(b, copied):
                for i in range(4):
                    pe = c.on_pe(lambda e: e.transpose(c.banks[6][:, i * P:(i + 1) * P], sums[b % 2][:, i * P:(i + 1) * P], c.ident[:, :]),
                                 copied, *bank_free[6])
                sums_free[b] = pe
                view, den = c.banks[6][:, :].rearrange("p (h d) -> p h d", h=CELLS), denom[b % 2]
                as_heads = lambda t: t.rearrange("p (h d) -> p h d", h=CELLS)
                row_sum, features = row_sums[b % 2], cell[:, b, :]
                copied = c.on_act(lambda e: e.copy(as_heads(features), view[:, :, 0:CD]), pe)
                m = c.on_act(lambda e: e.copy(row_sum[:, :], view[:, :, CD]), normed_by.get(b - 2))
                bank_free[6] = [m]
                squared[b] = c.on_act(lambda e: e.activation(square[b % 2][:, :], features, ACT.Square), copied, summed.get(b - 2))
                m = c.on_dve(lambda e: e.scalar_tensor_tensor(den[:, :], row_sum[:, :], -1.0, e_token[:, b, :], ALU.mult, ALU.max), m)
                normed_by[b] = m = c.on_dve(lambda e: e.tensor_tensor(den[:, :], row_sum[:, :], den[:, :], ALU.max), m)
                m = c.on_dve(lambda e: e.tensor_scalar(den[:, :], den[:, :], CELL_EPS, None, ALU.add), m)
                c.on_dve(lambda e: e.reciprocal(inv_norm[:, b * CELLS:(b + 1) * CELLS], den[:, :]), m)

            def sum_squares(b):
                summed[b] = c.on_dve(lambda e: e.tensor_reduce(square_sum[:, b * CELLS:(b + 1) * CELLS],
                                                               square[b % 2][:, :].rearrange("p (h d) -> p h d", h=CELLS), AX.X, ALU.add), squared[b])

            squared, summed, normed_by = {}, {}, {}
            for n in range(NB + 4):
                if n < NB:
                    block_queries(n)
                    decay_of(n)
                if 1 <= n <= NB:
                    exponential(n - 1)
                    scores(n - 1)
                if 2 <= n <= NB + 1:
                    copied[n - 2] = times_v(n - 2)
                if 3 <= n < NB + 3:
                    by_token(n - 3, copied[n - 3])
                if n >= 4:
                    sum_squares(n - 4)
            cells_done = c.now()

        with ExitStack() as w2:
            factor, root = c.sbuf(w2, "m_factor", [P, NB * CELLS]), c.sbuf(w2, "m_root", [P, NB * CELLS])
            m = c.on_dve(lambda e: e.tensor_tensor(root[:, :], inv_norm[:, :], inv_norm[:, :], ALU.mult), *cells_done)
            m = c.on_dve(lambda e: e.tensor_tensor(root[:, :], root[:, :], square_sum[:, :], ALU.mult), m)
            m = c.on_dve(lambda e: e.tensor_scalar(root[:, :], root[:, :], 1.0 / CD, CELL_EPS, ALU.mult, ALU.add), m)
            m = c.on_act(lambda e: e.activation(root[:, :], root[:, :], ACT.Sqrt), m)
            m = c.on_dve(lambda e: e.reciprocal(root[:, :], root[:, :]), m)
            m = c.on_dve(lambda e: e.tensor_tensor(factor[:, :], root[:, :], inv_norm[:, :], ALU.mult), m)
            GROUP = 4
            groups = [slice(g * GROUP, (g + 1) * GROUP) for g in range(NB // GROUP)]
            scaled = [c.on_dve(lambda e: e.tensor_tensor(
                cell[:, g, :].rearrange("p b (h d) -> p (b h) d", d=CD), cell[:, g, :].rearrange("p b (h d) -> p (b h) d", d=CD),
                factor[:, g.start * CELLS:g.stop * CELLS].unsqueeze(2).to_broadcast([P, GROUP * CELLS, CD]), ALU.mult), m) for g in groups]
            for g, ready in zip(groups, scaled):
                m = c.on_pool(lambda e: e.tensor_tensor(cell[:, g, :], cell[:, g, :], ln_scale[:, :].unsqueeze(1).to_broadcast([P, GROUP, D]), ALU.mult),
                              ready, small)
                c.on_dve(lambda e: e.scalar_tensor_tensor(resid[:, g, :], cell[:, g, :], c.gates[:, 2:3], resid[:, g, :], ALU.mult, ALU.add),
                         m, c.gates_ready)
            c.join()


RH, RD = 16, 128
MOE, MW = 4, 256
CHUNK = BANK // P
NCHUNK = NB // CHUNK
MASKED = -3e38


def layer1_block(c, io):
    nc, resid, xT = c.nc, c.resid, c.columns
    with ExitStack() as w:
        sb = lambda name, shape, dtype=F32: c.sbuf(w, name, shape, dtype)
        y = sb("b_y", [P, NB, D])
        small_in = c.tally("b_small_in")
        vectors = sb("b_vectors", [P, 8])
        head_bias = sb("b_head_bias", [P, 3, RH])
        swap_bias = sb("b_swap_bias", [P, 2, RH])
        bo = sb("b_bo", [P, D])
        for dst, src in ((vectors[:, :], io["b_vectors"]), (head_bias[:, :, :], io["b_head_bias"]), (swap_bias[:, :, :], io["b_swap_bias"])):
            c.load(dst, src, small_in)
        small = c.load(bo[:, :], io["b_bo"].broadcast_to([P, D]), small_in)
        x_split = [sb(f"b_x_{n}", [P, DK, T], F32R) for n in ("hi", "lo")]
        experts = ExpertsInput(c, io, w, y, x_split, vectors, small)
        block_attention(c, io, y, x_split, experts, vectors, head_bias, swap_bias, bo, small)
        block_experts(c, io, y, x_split, experts)



def norm_pieces(c, work, src, dst, *ready):
    stats, mean_var, rstd = work
    for b in range(CHUNK):
        m = c.on_dve(lambda e: e.bn_stats(stats[:, b, :], src[:, b, :]), *ready)
    for b in range(CHUNK):
        last = c.on_dve(lambda e: e.bn_aggr(mean_var[:, b, :], stats[:, b, :]), m)
    last = c.on_dve(lambda e: e.tensor_scalar(rstd[:, :], mean_var[:, :, 1], EPS_LN, None, ALU.add), last)
    yield
    root = c.on_act(lambda e: e.activation(rstd[:, :], rstd[:, :], ACT.Sqrt), last)
    yield
    inv = c.on_dve(lambda e: e.reciprocal(rstd[:, :], rstd[:, :]), root)
    for b in range(CHUNK):
        m = c.on_dve(lambda e: e.tensor_scalar(dst[:, b, :], src[:, b, :], mean_var[:, b, 0:1], rstd[:, b:b + 1], ALU.subtract, ALU.mult), inv)
    return m


def column_pieces(c, src, dst, place, scale, bias, *ready):
    for half in range(2):
        bank, free = c.banks[place[0]], place[1][place[0]]
        for b in range(2):
            for k in range(DK):
                pe = c.on_pe(lambda e: e.transpose(bank[:, (2 * k + b) * P:(2 * k + b + 1) * P], src[:, 2 * half + b, k * P:(k + 1) * P], c.ident[:, :]),
                             c.ident_ready, *ready, *free)
        for k in range(DK):
            a = c.on_act(lambda e: e.activation(dst[:, k, half * 2 * P:(half + 1) * 2 * P], bank[:, 2 * k * P:2 * (k + 1) * P], ACT.Identity,
                                                bias=bias[:, k:k + 1], scale=scale[:, k:k + 1]), pe)
        place[1][place[0]] = [a]
        yield
    return pe, a


class NormWork:

    def __init__(self, c, w, tag):
        sb = lambda name, shape: c.sbuf(w, f"{tag}_{name}", shape)
        self.work = sb("stats", [P, CHUNK, 6]), sb("mean_var", [P, CHUNK, 2]), sb("rstd", [P, CHUNK])
        self.rows, self.columns = sb("rows", [P, CHUNK, D]), sb("columns", [P, DK, BANK])
        self.read = []


class ExpertsInput:

    def __init__(self, c, io, w, y, x_split, vectors, small):
        self.c, self.io, self.y, self.x_split, self.vectors, self.small = c, io, y, x_split, vectors, small
        sb = lambda name, shape: c.sbuf(w, f"b_{name}", shape)
        PAD = 12
        self.norm = NormWork(c, w, "b_second")
        self.gate = sb("gate", [P, DK, MOE])
        self.b1, self.b2 = sb("b1", [P, MOE, MW // P]), sb("b2", [MOE, D])
        self.w1, self.w2 = (c.columns[:, i, :] for i in range(2))
        self.probs, self.left, self.lead, self.best = (sb(n, [P, CHUNK, s]) for n, s in (("padded", PAD), ("left", PAD), ("lead", 8), ("best", 8)))
        self.peak, self.total = sb("gate_peak", [P, CHUNK]), sb("gate_total", [P, CHUNK])
        self.comb, self.combT = sb("comb", [P, CHUNK, MOE]), sb("combT", [MOE, T])
        c.on_pool(lambda e: e.memset(self.probs[:, :, :], -1.0))
        self.pad = c.on_pool(lambda e: e.memset(self.lead[:, :, :], -1.0))
        self.x_ready, self.comb_stored, self.comb_used = {}, {}, None

    def load_weights(self):
        c, io, small_in, raw_in = self.c, self.io, self.c.tally("b_gate_in"), self.c.tally("b_experts_in")
        c.load(self.gate[:, :, :], io["b_gate"], small_in)
        c.load(self.b1[:, :, :], io["b_b1"], small_in)
        self.gate_in = c.load(self.b2[:, :], io["b_b2"], small_in)
        c.load(self.w1, io["b_w1"], raw_in)
        self.raw_in = c.load(self.w2, io["b_w2"], raw_in)

    def pieces(self, chunk, place, *ready):
        c, probs, left, lead, best, peak, total, comb, norm = (self.c, self.probs, self.left, self.lead, self.best, self.peak, self.total,
                                                              self.comb, self.norm)
        rows, cols = self.y[:, chunk * CHUNK:(chunk + 1) * CHUNK, :], slice(chunk * BANK, (chunk + 1) * BANK)
        m = yield from norm_pieces(c, norm.work, rows, norm.rows, *ready, *norm.read)
        yield
        pe, a = yield from column_pieces(c, norm.rows, norm.columns, place, self.vectors[:, 4:6], self.vectors[:, 6:8], m, self.small)
        bank, free = c.banks[place[0]], place[1][place[0]]
        for b in range(CHUNK):
            for k in range(DK):
                pe = c.on_pe(lambda e: e.matmul(bank[:, b * MOE:(b + 1) * MOE], norm.columns[:, k, b * P:(b + 1) * P], self.gate[:, k, :],
                                                start=k == 0, stop=k == DK - 1), a, self.gate_in, *free)
        real = probs[:, :, 0:MOE]
        wide = lambda t: t.unsqueeze(2).to_broadcast([P, CHUNK, MOE])
        m = c.on_dve(lambda e: e.tensor_copy(real, bank[:, 0:CHUNK * MOE].rearrange("p (b n) -> p b n", b=CHUNK)), pe, self.pad)
        place[1][place[0]] = [m]
        yield
        hi, lo = (t[:, :, cols] for t in self.x_split)
        a = c.on_act(lambda e: e.copy(hi, norm.columns[:, :, :]))
        self.x_ready[chunk] = c.on_pool(lambda e: e.tensor_tensor(lo, norm.columns[:, :, :], hi.bitcast(F32), ALU.subtract), a)
        norm.read = [pe, self.x_ready[chunk]]
        m = c.on_dve(lambda e: e.tensor_reduce(peak[:, :], real, AX.X, ALU.max), m)
        m = c.on_dve(lambda e: e.tensor_tensor(real, real, wide(peak[:, :]), ALU.subtract), m)
        yield
        a = c.on_act(lambda e: e.activation(real, real, ACT.Exp), m)
        yield
        m = c.on_dve(lambda e: e.tensor_reduce(total[:, :], real, AX.X, ALU.add), a)
        m = c.on_dve(lambda e: e.reciprocal(total[:, :], total[:, :]), m)
        m = c.on_dve(lambda e: e.tensor_tensor(real, real, wide(total[:, :]), ALU.mult), m)
        for b in range(CHUNK):
            m8 = c.on_dve(lambda e: e.max(best[:, b, :], probs[:, b, :]), m)
        m = c.on_dve(lambda e: e.tensor_copy(lead[:, :, 0:2], best[:, :, 0:2]), m8)
        for b in range(CHUNK):
            m8 = c.on_dve(lambda e: e.match_replace(left[:, b, :], lead[:, b, :], probs[:, b, :], -2.0), m)
        m = c.on_dve(lambda e: e.tensor_tensor(comb[:, :, :], real, wide(best[:, :, 0]), ALU.subtract), m8, self.comb_used)
        yield
        a = c.on_act(lambda e: e.activation(comb[:, :, :], comb[:, :, :], ACT.Exp), m)
        yield
        m = c.on_dve(lambda e: e.scalar_tensor_tensor(comb[:, :, :], left[:, :, 0:MOE], -1.5, comb[:, :, :], ALU.is_lt, ALU.mult), a)
        m = c.on_dve(lambda e: e.tensor_reduce(total[:, :], comb[:, :, :], AX.X, ALU.add), m)
        m = c.on_dve(lambda e: e.reciprocal(total[:, :], total[:, :]), m)
        m = c.on_dve(lambda e: e.tensor_tensor(comb[:, :, :], comb[:, :, :], wide(total[:, :]), ALU.mult), m)
        yield
        bank, free = c.banks[place[0]], place[1][place[0]]
        for b in range(CHUNK):
            pe = c.on_pe(lambda e: e.transpose(bank[0:MOE, b * P:(b + 1) * P], comb[:, b, :], c.ident[:, :]), m, *free)
        self.comb_used = pe
        a = c.on_act(lambda e: e.copy(self.combT[:, cols], bank[0:MOE, :]), pe)
        place[1][place[0]] = [a]
        self.comb_stored[chunk] = c.load(self.io["b_comb_rows"][:, cols], self.combT[:, cols], c.tally(f"b_comb_stored{chunk}"), a)


def block_attention(c, io, y, x_split, experts, vectors, head_bias, swap_bias, bo, small):
    resid = c.resid
    SCALE = 1.0 / float(np.sqrt(RD))
    with ExitStack() as w:
        sb = lambda name, shape, dtype=F32: c.sbuf(w, name, shape, dtype)
        GROUP = 4
        NQK, NV = 2 * DK * RD, DK * GROUP * RD
        raw_qk, raw_o = [sb(f"b_raw_qk{i}", [P, NQK]) for i in range(3)], [sb(f"b_raw_o{i}", [P, D]) for i in range(3)]
        raw_v = [sb(f"b_raw_v{i}", [P, NV]) for i in range(2)]
        pair = lambda name, n: [sb(f"b_{name}_{half}", [P, n], F32R) for half in ("hi", "lo")]
        split_qk, split_o, split_v = ([pair(f"{name}{i}", n) for i in range(2)] for name, n in (("qk", NQK), ("o", D), ("vw", NV)))
        rope, mask = sb("b_rope", [P, 2, S]), sb("b_mask", [P, S])
        qk_in, o_in, v_in = ([c.tally(f"b_{n}_in{i}") for i in range(count)] for n, count in (("qk", 3), ("o", 3), ("v", 2)))
        steps = NCHUNK * RH
        loaded, raw_free, split_done, split_free = {}, {}, {}, {}
        kinds = {"qk": (raw_qk, split_qk, qk_in, io["b_wqk"], RH), "o": (raw_o, split_o, o_in, io["b_wo"], RH),
                 "v": (raw_v, split_v, v_in, io["b_wv"], RH // GROUP)}

        def load_weights(kind, n):
            raw, _, tallies, src, period = kinds[kind]
            r = n % len(raw)
            loaded[kind, n] = c.load(raw[r][:, :], src[n % period], tallies[r], raw_free.get((kind, r)))

        def split_weights(kind, n):
            raw, split = kinds[kind][:2]
            r, i = n % len(raw), n % 2
            hi, lo = (t[:, :] for t in split[i])
            m = c.on_dve(lambda e: e.tensor_copy(hi, raw[r][:, :]), loaded[kind, n], split_free.get((kind, i)))
            rest_to_split.append((kind, n, r, hi, lo, m))

        def split_rest():
            for kind, n, r, hi, lo, m in rest_to_split:
                split_done[kind, n] = raw_free[kind, r] = c.on_pool(
                    lambda e: e.tensor_tensor(lo, kinds[kind][0][r][:, :], hi.bitcast(F32), ALU.subtract), m)
            rest_to_split.clear()

        rest_to_split = []

        load_weights("qk", 0)
        load_weights("v", 0)
        tables_in = c.tally("b_tables_in")
        c.load(rope[:, :, :], io["b_rope"], tables_in)
        tables = c.load(mask[:, :], io["b_mask"], tables_in)
        for n in range(3):
            if n >= 1:
                load_weights("qk", n)
            load_weights("o", n)
        load_weights("v", 1)

        first = NormWork(c, w, "b_first")
        x_ready, with_bo = {}, {}

        def input_pieces(chunk, place):
            rows, cols = slice(chunk * CHUNK, (chunk + 1) * CHUNK), slice(chunk * BANK, (chunk + 1) * BANK)
            m = yield from norm_pieces(c, first.work, resid[:, rows, :], y[:, rows, :], c.x_in[chunk * CHUNK])
            yield
            m = yield from norm_pieces(c, first.work, y[:, rows, :], first.rows, m, *first.read)
            with_bo[chunk] = c.on_pool(lambda e: e.tensor_tensor(y[:, rows, :], y[:, rows, :], bo[:, :].unsqueeze(1).to_broadcast([P, CHUNK, D]),
                                                                 ALU.add), m, small)
            yield
            pe, a = yield from column_pieces(c, first.rows, first.columns, place, vectors[:, 0:2], vectors[:, 2:4], m, small)
            hi, lo = (t[:, :, cols] for t in x_split)
            a = c.on_act(lambda e: e.copy(hi, first.columns[:, :, :]), a)
            x_ready[chunk] = c.on_pool(lambda e: e.tensor_tensor(lo, first.columns[:, :, :], hi.bitcast(F32), ALU.subtract), a)
            first.read = [pe, x_ready[chunk]]

        with ExitStack() as w2:
            s2 = lambda name, shape, dtype=F32: c.sbuf(w2, name, shape, dtype)
            v = [s2(f"b_v{i}", [P, CHUNK, GROUP * RD]) for i in range(2)]
            turned = [s2(f"b_turned{i}", [P, 2, BANK]) for i in range(2)]
            straight = [s2(f"b_straight{i}", [P, 2, BANK]) for i in range(2)]
            probs = [s2(f"b_probs{i}", [P, CHUNK, S]) for i in range(3)]
            peak, peak_scaled, total, inv = ([s2(f"b_{n}{i}", [P, CHUNK]) for i in range(2)] for n in ("peak", "peak_scaled", "total", "inv"))
            probsT = [s2(f"b_probsT{i}", [P, BANK]) for i in range(2)]
            outT = [[s2(f"b_outT_{n}{i}", [P, BANK], F32R) for n in ("hi", "lo")] for i in range(2)]
            Q, K, V, SC, PT, OT, OUT = 0, 1, 2, 3, 4, 5, 6
            free = {n: [] for n in range(8)}
            v_ready, v_used, rotated, scored, prob_ready, out_ready, done = {}, {}, {}, {}, {}, {}, {}

            def values(n):
                group, tile = divmod(n, CHUNK)
                chunk, g = divmod(group, RH // GROUP)
                b = chunk * CHUNK + tile
                for k in range(DK):
                    pe = product(c, c.banks[V][:, :], [t[:, k, b * P:(b + 1) * P] for t in x_split],
                                 [t[:, k * BANK:(k + 1) * BANK] for t in split_v[group % 2]], k == 0, k == DK - 1,
                                 x_ready[chunk], split_done["v", group], *free[V])
                split_free["v", group % 2] = pe
                v_ready[group] = a = c.on_act(lambda e: e.copy(v[group % 2][:, tile, :], c.banks[V][:, :]), pe, *v_used.get(group - 2, ()))
                free[V] = [a]

            def queries_keys(n):
                chunk, h = divmod(n, RH)
                i = n % 2
                by_batch = lambda t: t.rearrange("p (b s) -> p b s", b=CHUNK)
                wide = lambda which: rope[:, which, :].unsqueeze(1).to_broadcast([P, CHUNK, S])
                both[n] = []
                for which, bank in ((0, Q), (1, K)):
                    for k in range(DK):
                        at = (which * DK + k) * RD
                        pe = product(c, c.banks[bank][:, :], [t[:, at:at + RD] for t in split_qk[i]],
                                     [t[:, k, chunk * BANK:(chunk + 1) * BANK] for t in x_split], k == 0, k == DK - 1,
                                     x_ready[chunk], split_done["qk", n], *free[bank])
                        split_free["qk", i] = pe
                    half = P // 2
                    for dst, src in ((0, half), (half, 0)):
                        a = c.on_act(lambda e: e.activation(turned[i][dst:dst + half, which, :], c.banks[bank][src:src + half, :], ACT.Identity,
                                                            bias=swap_bias[dst:dst + half, which, h:h + 1]), pe, small, scored.get(n - 2))
                    m = c.on_dve(lambda e: e.scalar_tensor_tensor(by_batch(straight[i][:, which, :]), by_batch(c.banks[bank][:, :]),
                                                                  head_bias[:, which, h:h + 1], wide(0), ALU.add, ALU.mult),
                                 pe, a, tables, scored.get(n - 2))
                    free[bank] = [a, m]
                    turned_ready = m, c.on_pool(lambda e: e.tensor_tensor(by_batch(turned[i][:, which, :]), by_batch(turned[i][:, which, :]), wide(1), ALU.mult), a, tables)
                    both[n].append(turned_ready)

            def rotate(n):
                i = n % 2
                for which in range(2):
                    rotated[n] = c.on_dve(lambda e: e.tensor_tensor(straight[i][:, which, :], straight[i][:, which, :], turned[i][:, which, :], ALU.add),
                                          *both[n][which])

            def softmax(n):
                i = n % 2
                for b in range(CHUNK):
                    pe = c.on_pe(lambda e: e.matmul(c.banks[SC][:, b * S:(b + 1) * S], straight[i][:, 0, b * S:(b + 1) * S],
                                                    straight[i][:, 1, b * S:(b + 1) * S], start=True, stop=True), rotated[n], *free[SC])
                scored[n] = pe
                by_batch = c.banks[SC][:, :].rearrange("p (b s) -> p b s", b=CHUNK)
                m = c.on_dve(lambda e: e.tensor_tensor(probs[n % 3][:, :, :], by_batch, mask[:, :].unsqueeze(1).to_broadcast([P, CHUNK, S]), ALU.add),
                             pe, tables, prob_used.get(n - 3))
                free[SC] = [m]
                m = c.on_dve(lambda e: e.tensor_reduce(peak[i][:, :], probs[n % 3][:, :, :], AX.X, ALU.max, negate=True), m)
                peak_ready[n] = c.on_dve(lambda e: e.tensor_scalar(peak_scaled[i][:, :], peak[i][:, :], SCALE, None, ALU.mult), m)

            def exponentials(n):
                i = n % 2
                for b in range(CHUNK):
                    a = c.on_act(lambda e: e.activation(probs[n % 3][:, b, :], probs[n % 3][:, b, :], ACT.Exp, scale=SCALE, bias=peak_scaled[i][:, b:b + 1],
                                                        accum_out=total[i][:, b:b + 1]), peak_ready[n])
                exp_ready[n] = a

            def normalise(n):
                i = n % 2
                m = c.on_dve(lambda e: e.reciprocal(inv[i][:, :], total[i][:, :]), exp_ready[n])
                prob_ready[n] = c.on_pool(lambda e: e.tensor_tensor(probs[n % 3][:, :, :], probs[n % 3][:, :, :],
                                                                    inv[i][:, :].unsqueeze(2).to_broadcast([P, CHUNK, S]), ALU.mult), m)

            y_ready, both = {}, {}
            prob_used, peak_ready, exp_ready = {}, {}, {}

            def transpose_probs(n):
                i = n % 2
                for b in range(CHUNK):
                    pe = c.on_pe(lambda e: e.transpose(c.banks[PT][:, b * S:(b + 1) * S], probs[n % 3][:, b, :], c.ident[:, :]), prob_ready[n], *free[PT])
                prob_used[n] = pe
                if n % 2:
                    a = c.on_act(lambda e: e.copy(probsT[i][:, :], c.banks[PT][:, :]), pe, weighed.get(n - 2))
                else:
                    a = c.on_dve(lambda e: e.tensor_copy(probsT[i][:, :], c.banks[PT][:, :]), pe, weighed.get(n - 2))
                free[PT] = [a]
                transposed[n] = a

            transposed, weighed = {}, {}

            def weigh_values(n):
                chunk, h = divmod(n, RH)
                group, i = n // GROUP, n % 2
                for b in range(CHUNK):
                    pe = c.on_pe(lambda e: e.matmul(c.banks[OT][:, b * S:(b + 1) * S], v[group % 2][:, b, (h % GROUP) * RD:(h % GROUP + 1) * RD],
                                                    probsT[i][:, b * S:(b + 1) * S], start=True, stop=True), transposed[n], v_ready[group], *free[OT])
                v_used[group], weighed[n] = [pe], pe
                hi, lo = outT[i]
                a = c.on_act(lambda e: e.activation(hi[:, :], c.banks[OT][:, :], ACT.Identity, bias=head_bias[:, 2, h:h + 1]), pe, done.get(n - 2))
                m = c.on_dve(lambda e: e.scalar_tensor_tensor(lo[:, :], c.banks[OT][:, :], head_bias[:, 2, h:h + 1], hi[:, :].bitcast(F32),
                                                              ALU.add, ALU.subtract), a)
                free[OT], out_ready[n] = [m], m

            def project(n):
                chunk, h = divmod(n, RH)
                i = n % 2
                for b in range(CHUNK):
                    bank = OUT + b // 2
                    pe = product(c, c.banks[bank][:, (b % 2) * D:(b % 2 + 1) * D], [t[:, b * S:(b + 1) * S] for t in outT[i]],
                                 [t[:, :] for t in split_o[i]], h == 0 and b % 2 == 0, h == RH - 1, out_ready[n], split_done["o", n], *free[bank])
                done[n] = split_free["o", i] = pe
                if h == RH - 1:
                    for bank in (OUT, OUT + 1):
                        rows = y[:, chunk * CHUNK + 2 * (bank - OUT):chunk * CHUNK + 2 * (bank - OUT) + 2, :]
                        free[bank] = [c.on_dve(lambda e: e.tensor_tensor(rows, rows, c.banks[bank][:, :].rearrange("p (b n) -> p b n", b=2), ALU.add),
                                               pe, with_bo[chunk])]
                    y_ready[chunk] = free[OUT] + free[OUT + 1]

            groups = steps // GROUP
            place = (V, free)
            first_input = input_pieces(0, place)
            for _ in range(6):
                next(first_input)
            for kind in ("qk", "v"):
                split_weights(kind, 0)
            split_rest()
            for _ in first_input:
                pass
            behind = []
            for n in range(steps + 5):
                chunk, h = divmod(n, RH)
                if n == RH:
                    experts.load_weights()
                if h == 0 and chunk + 1 < NCHUNK:
                    behind.append(input_pieces(chunk + 1, place))
                if h == 5 and chunk >= 1:
                    behind.append(experts.pieces(chunk - 1, place, *y_ready[chunk - 1], (c.pe, c.pe.count)))
                if n + 1 < steps:
                    split_weights("qk", n + 1)
                split_rest()
                if 4 <= n < steps + 4:
                    split_weights("o", n - 4)
                if n % GROUP == 0 and n // GROUP + 1 < groups:
                    split_weights("v", n // GROUP + 1)
                if 2 <= n <= steps + 1:
                    exponentials(n - 2)
                if n < steps:
                    queries_keys(n)
                if 2 <= n <= steps + 1:
                    normalise(n - 2)
                split_rest()
                if n + 3 < steps:
                    load_weights("qk", n + 3)
                if 4 <= n <= steps:
                    load_weights("o", n - 1)
                if n % GROUP == 0 and n // GROUP + 2 < groups:
                    load_weights("v", n // GROUP + 2)
                if 1 <= n <= steps:
                    softmax(n - 1)
                if n < steps:
                    rotate(n)
                    values(n)
                if 3 <= n < steps + 3:
                    transpose_probs(n - 3)
                if 4 <= n < steps + 4:
                    weigh_values(n - 4)
                behind = [pieces for pieces in behind if next(pieces, "ended") != "ended"]
                if 5 <= n:
                    project(n - 5)
            for pieces in behind:
                for _ in pieces:
                    pass
            experts.y_ready = y_ready[NCHUNK - 1]
            c.join()


def block_experts(c, io, y, x_split, experts):
    resid, b1, b2, combT = c.resid, experts.b1, experts.b2, experts.combT
    with ExitStack() as w:
        sb = lambda name, shape, dtype=F32: c.sbuf(w, name, shape, dtype)
        comb_wide = sb("b_comb_wide", [P, MOE, T])
        w1_split = [sb(f"b_w1_{n}", [P, MOE, DK, MW], F32R) for n in ("hi", "lo")]
        w2_split = [sb(f"b_w2_{n}", [P, MOE, MW // P, D], F32R) for n in ("hi", "lo")]
        w1_ready, w2_ready = {}, {}
        for e_ in range(MOE):
            for raw, dst, marks in ((experts.w1, w1_split, w1_ready), (experts.w2, w2_split, w2_ready)):
                whole = raw.rearrange("p (e k n) -> p e k n", e=MOE, k=DK)[:, e_]
                marks[e_] = split2(c, c.on_act, whole, *(t[:, e_, :, :] for t in dst), experts.raw_in)
        comb_in = {}

        def load_comb(chunk):
            cols, tally = slice(chunk * BANK, (chunk + 1) * BANK), c.tally(f"b_comb_in{chunk}")
            for e_ in range(MOE):
                comb_in[chunk] = c.load(comb_wide[:, e_, cols], io["b_comb_rows"][e_:e_ + 1, cols].broadcast_to([P, BANK]), tally,
                                        experts.comb_stored[chunk])

        for chunk in range(NCHUNK - 1):
            load_comb(chunk)

        with ExitStack() as w3:
            s3 = lambda name, shape, dtype=F32: c.sbuf(w3, name, shape, dtype)
            act = [s3(f"b_act{i}", [P, BANK]) for i in range(2)]
            hidden = [s3(f"b_hidden{i}", [P, BANK]) for i in range(2)]
            hidden_split = [[s3(f"b_hidden_{n}{i}", [P, BANK], F32R) for n in ("hi", "lo")] for i in range(3)]
            MB = MW // P
            steps = [(chunk, e_, mb) for chunk in range(NCHUNK) for e_ in range(MOE) for mb in range(MB)]
            free = {n: [] for n in range(8)}
            ready, used, weighed = {}, {}, {}
            out_stored = c.tally("out_stored")

            def up(n):
                chunk, e_, mb = steps[n]
                i, cols = n % 2, slice(chunk * BANK, (chunk + 1) * BANK)
                for k in range(DK):
                    pe = product(c, c.banks[i][:, :], [t[:, e_, k, mb * P:(mb + 1) * P] for t in w1_split], [t[:, k, cols] for t in x_split],
                                 k == 0, k == DK - 1, experts.x_ready[chunk], w1_ready[e_], *free[i])
                a = c.on_act(lambda e: e.activation(act[i][:, :], c.banks[i][:, :], ACT.Gelu, bias=b1[:, e_, mb:mb + 1]), pe, weighed.get(n - 2))
                free[i] = [a]
                weighed[n] = c.on_dve(lambda e: e.tensor_tensor(hidden[i][:, :], act[i][:, :], comb_wide[:, e_, cols], ALU.mult), a, comb_in[chunk],
                                      ready.get(n - 2))

            def split_hidden(n):
                ready[n] = split2(c, c.on_act, hidden[n % 2][:, :], *(t[:, :] for t in hidden_split[n % 3]), weighed[n], used.get(n - 3))

            def down(n):
                chunk, e_, mb = steps[n]
                i, base = n % 2, 4 + 2 * (chunk % 2)
                for t in range(CHUNK):
                    bank = base + t // 2
                    out = c.banks[bank][:, (t % 2) * D:(t % 2 + 1) * D]
                    tok = slice((chunk * CHUNK + t) * P, (chunk * CHUNK + t + 1) * P)
                    if e_ == 0 and mb == 0:
                        c.on_pe(lambda e: e.matmul(out, combT[:, tok], b2[:, :], start=t % 2 == 0, stop=False, skip_group_check=True), *free[bank])
                    pe = product(c, out, [v[:, t * P:(t + 1) * P] for v in hidden_split[n % 3]], [v[:, e_, mb, :] for v in w2_split],
                                 False, n % (MOE * MB) == MOE * MB - 1, ready[n], w2_ready[e_])
                used[n] = pe
                if n % (MOE * MB) == MOE * MB - 1:
                    for bank in (base, base + 1):
                        b = chunk * CHUNK + 2 * (bank - base)
                        rows, x = y[:, b:b + 2, :], resid[:, b:b + 2, :]
                        m = c.on_dve(lambda e: e.tensor_tensor(rows, rows, c.banks[bank][:, :].rearrange("p (b n) -> p b n", b=2), ALU.add), pe)
                        free[bank] = [m]
                        m = c.on_dve(lambda e: e.scalar_tensor_tensor(x, rows, c.gates[:, 3:4], x, ALU.mult, ALU.add), m, c.gates_ready)
                        c.out_mark = c.load(io["out"][b:b + 2, :, :].rearrange("b p n -> p b n"), x, out_stored, m)

            LAG = 2
            behind = [experts.pieces(NCHUNK - 1, (2, free), *experts.y_ready)]
            for n in range(len(steps) + LAG):
                if n >= 1 and behind and next(behind[0], "ended") == "ended":
                    behind = []
                    load_comb(NCHUNK - 1)
                if 1 <= n <= len(steps):
                    split_hidden(n - 1)
                if n < len(steps):
                    up(n)
                if n >= LAG:
                    down(n - LAG)


def program(nc, io):
    with ExitStack() as stack:
        c = Core(nc, stack)
        sb = lambda name, shape, dtype=F32: c.sbuf(stack, name, shape, dtype)
        c.resid = sb("resid", [P, NB, D])
        c.columns = sb("columns", [P, DK, T])
        c.ident, c.gates = sb("ident", [P, P]), sb("gates", [P, 4])
        GROUP = 4
        context = ExitStack()
        c.ctx = c.sbuf(context, "ctx", [P, NB, D])
        c.x_in, c.ctx_in = [], []
        for g in range(NB // GROUP):
            for name, dst, marks in (("x", c.resid, c.x_in), ("ctx", c.ctx, c.ctx_in)):
                b = slice(g * GROUP, (g + 1) * GROUP)
                marks += [c.load(dst[:, b, :], io[name][b, :, :].rearrange("b p n -> p b n"), c.tally(f"{name}_in{g}"))] * GROUP
        gates_in = c.load(c.gates[:, :], io["gates"], c.tally("gates_in"))
        c.gates_ready = c.on_act(lambda e: e.activation(c.gates[:, :], c.gates[:, :], ACT.Tanh), gates_in)
        zero = c.on_pool(lambda e: e.memset(c.ident[:, :], 0.0))
        c.ident_ready = c.on_pool(lambda e: e.affine_select(out=c.ident[:, :], in_=c.ident[:, :], compare_op=ALU.not_equal, fill=1.0,
                                                            base=0, pattern=[[-1, P]], channel_multiplier=1), zero)
        for stage in (layer0_attention, layer0_experts, layer1_mlstm):
            stage(c, io)
        context.close()
        layer1_block(c, io)
        c.need(nc.sync, c.out_mark)


def layouts(a):
    from_name = lambda n: np.asarray(a[n])
    out = {"x": from_name("x"), "ctx": from_name("ctx_2048")}
    gates = np.concatenate([from_name("g_xattn")[:, None], from_name("g_ffn")[:, None]], 1).reshape(4)
    out["gates"] = np.broadcast_to(gates, (P, 4))
    turned = lambda t: t.reshape((HEADS, HD) + t.shape[1:]).swapaxes(0, 1).reshape(t.shape)
    for n in "qkvo":
        wT = from_name(f"L0_xattn_W{n}")
        out[f"a_w{n}T"] = (turned(wT) if n in "qk" else wT).T
    out["a_bias"] = np.stack([turned(from_name(f"L0_xattn_b{n}")) if n in "qk" else from_name(f"L0_xattn_b{n}") for n in "qkvo"], 1)
    gu = from_name("L0_ffn_gate_up_proj").reshape(PAIRS, 2, 2, WIDTH, DK, P)
    gu = gu.transpose(0, 5, 4, 2, 1, 3).reshape(PAIRS, P, DK * 2 * P)
    down = from_name("L0_ffn_down_proj").reshape(PAIRS, 2, D, WIDTH).transpose(0, 1, 3, 2).reshape(PAIRS, P, D)
    out["e_weights"] = np.concatenate([gu, down], 2)
    shared = np.stack([from_name("L0_ffn_shared_gate_w"), from_name("L0_ffn_shared_up_w")]).reshape(2, WIDTH, DK, P)
    out["e_shared_gate_up"] = shared.transpose(3, 2, 0, 1).reshape(P, DK * 2 * WIDTH)
    out["e_shared_down"] = from_name("L0_ffn_shared_down_w").T
    router = np.concatenate([from_name("L0_ffn_router_w"), from_name("L0_ffn_shared_expert_gate_w")])
    out["e_router"] = router.reshape(EXPERTS + 1, DK, P).transpose(2, 1, 0)
    out["m_ctxT"] = out["ctx"].transpose(2, 0, 1).reshape(D, T)
    gate_w, gate_bias = np.zeros((3 * D, 2, SPAN), np.float32), np.zeros((P // SPAN, SPAN, 2), np.float32)
    for i, n in enumerate("if"):
        gate_w[:, i, 0:CELLS], gate_bias[:, 0:CELLS, i] = from_name(f"L1_xattn_W{n}"), from_name(f"L1_xattn_b{n}")
    out["m_gate_w"] = gate_w.reshape(3 * DK, P, 2 * SPAN).transpose(1, 0, 2)
    out["m_gate_bias"] = gate_bias.reshape(P, 2)
    head_of = np.arange(P)[:, None] // CD == np.arange(CELLS // DK)[None, :]
    out["m_head_mask"] = head_of.astype(np.float32) / 4
    out["m_ln_scale"] = from_name("L1_xattn_ln_scale").reshape(1, D)
    by_block = lambda v: v.reshape(DK, P).T
    out["b_vectors"] = np.concatenate([by_block(from_name(f"L1_ffn_{n}")) for n in ("ln1_w", "ln1_b", "ln2_w", "ln2_b")], 1)
    biases = np.stack([from_name(f"L1_ffn_b{n}").reshape(RH, RD) for n in "qkv"])
    out["b_head_bias"] = biases.transpose(2, 0, 1)
    swapped = np.concatenate([biases[:2, :, RD // 2:], biases[:2, :, :RD // 2]], 2)
    out["b_swap_bias"] = swapped.transpose(2, 0, 1)
    out["b_bo"] = from_name("L1_ffn_bo").reshape(1, D)
    qk = np.stack([from_name("L1_ffn_wq"), from_name("L1_ffn_wk")]).reshape(2, DK, P, RH, RD)
    out["b_wqk"] = qk.transpose(3, 2, 0, 1, 4).reshape(RH, P, 2 * DK * RD)
    out["b_wv"] = from_name("L1_ffn_wv").reshape(DK, P, RH // 4, 4 * RD).transpose(2, 1, 0, 3).reshape(RH // 4, P, DK * 4 * RD)
    out["b_wo"] = from_name("L1_ffn_wo").reshape(RH, RD, D)
    f32 = np.float32
    inv_freq = (f32(1.0) / f32(10000.0) ** (np.arange(0, RD, 2, dtype=f32) / f32(RD))).astype(f32)
    angle = np.arange(S, dtype=f32)[None, :] * np.concatenate([inv_freq, inv_freq])[:, None]
    sign = np.where(np.arange(RD) < RD // 2, f32(-1), f32(1))[:, None]
    out["b_rope"] = np.stack([np.cos(angle), np.sin(angle) * sign], 1).astype(f32)
    out["b_mask"] = np.where(np.arange(S)[None, :] > np.arange(S)[:, None], f32(MASKED), f32(0))
    out["b_gate"] = from_name("L1_ffn_w_gate").reshape(DK, P, MOE).transpose(1, 0, 2)
    out["b_w1"] = from_name("L1_ffn_we1").reshape(MOE, DK, P, MW).transpose(2, 0, 1, 3).reshape(P, MOE * DK * MW)
    out["b_w2"] = from_name("L1_ffn_we2").reshape(MOE, MW // P, P, D).transpose(2, 0, 1, 3).reshape(P, MOE * MW // P * D)
    out["b_b1"] = from_name("L1_ffn_be1").reshape(MOE, MW // P, P).transpose(2, 0, 1)
    out["b_b2"] = from_name("L1_ffn_be2")
    return {n: np.ascontiguousarray(v) for n, v in out.items()}


SCRATCH = {
    "b_comb_rows": ((MOE, T), F32),
    "m_negpeak": ((CELLS, T), F32),
    "e_combT": ((EXPERTS + 1, T), F32),
    "a_q_parts": ((NB, 3, P, D), BF16),
    "a_k_parts": ((NB, 3, P, D), BF16),
}


def kernel(**inputs):
    import concourse.bacc as _bacc
    from concourse.bass_utils import run_bass_kernel_spmd as _run

    nc = _bacc.Bacc("TRN2", target_bir_lowering=False, num_devices=1)
    arrays, io = layouts(inputs), {}
    for n, v in arrays.items():
        io[n] = nc.dram_tensor("in_" + n, v.shape, mybir.dt.from_np(v.dtype), kind="ExternalInput").ap()
    io["out"] = nc.dram_tensor("out", (NB, S, D), F32, kind="ExternalOutput").ap()
    for n, (shape, dtype) in SCRATCH.items():
        io[n] = nc.dram_tensor(n, shape, dtype).ap()
    program(nc, io)
    return _run(nc, [{"in_" + n: v for n, v in arrays.items()}], core_ids=[0]).results[0]["out"]
```

```python
from contextlib import ExitStack

import numpy as np

import concourse.bass as bass
from concourse import mybir

F32 = mybir.dt.float32
BF16 = mybir.dt.bfloat16
F32R = mybir.dt.float32r
ALU = mybir.AluOpType
ACT = mybir.ActivationFunctionType
AX = mybir.AxisListType

P = 128
NB, S, D = 16, 128, 256
T = NB * S
DK = D // P
EPS_LN = 1e-5
BANK = 512
CHUNK = BANK // P
NCHUNK = NB // CHUNK


class Tally:

    def __init__(self, name, sem):
        self.name, self.sem, self.count = name, sem, 0

    def mark(self, instruction, by=1):
        instruction.then_inc(self.sem, by)
        self.count += by
        return (self, self.count)


class Core:

    def __init__(self, nc, stack):
        self.nc, self.stack = nc, stack
        self.reached = {}
        self.pe, self.act, self.dve, self.pool = (self.tally(n) for n in ("pe_done", "act_done", "dve_done", "pool_done"))
        self.banks = [stack.enter_context(nc.psum_tensor(f"bank{i}", [P, BANK], F32)) for i in range(8)]

    def tally(self, name):
        return Tally(name, self.stack.enter_context(self.nc.semaphore(name)))

    def sbuf(self, stack, name, shape, dtype=F32):
        return stack.enter_context(self.nc.sbuf_tensor(name, shape, dtype))

    def need(self, engine, *marks):
        for mark in marks:
            if mark is None:
                continue
            tally, value = mark
            key = (engine.engine, tally.name)
            if self.reached.get(key, 0) < value:
                engine.wait_ge(tally.sem, value)
                self.reached[key] = value

    def on_pe(self, make, *marks):
        self.need(self.nc.tensor, *marks)
        return self.pe.mark(make(self.nc.tensor))

    def on_act(self, make, *marks):
        self.need(self.nc.scalar, *marks)
        return self.act.mark(make(self.nc.scalar))

    def on_dve(self, make, *marks):
        self.need(self.nc.vector, *marks)
        return self.dve.mark(make(self.nc.vector))

    def on_pool(self, make, *marks):
        self.need(self.nc.gpsimd, (self.pool, self.pool.count), *marks)
        return self.pool.mark(make(self.nc.gpsimd))

    def load(self, dst, src, tally, *marks, queue=None):
        queue = queue or self.nc.sync
        self.need(queue, *marks)
        return tally.mark(queue.dma_start(dst, src), 16)

    def now(self):
        return [(t, t.count) for t in (self.pe, self.act, self.dve, self.pool) if t.count]

    def join(self, *more):
        marks = self.now() + list(more)
        for engine in (self.nc.tensor, self.nc.scalar, self.nc.vector, self.nc.gpsimd, self.nc.sync):
            self.need(engine, *marks)


def split2(c, on_hi, src, hi, lo, *marks, lo_marks=()):
    copy = (lambda e: e.copy(hi, src)) if on_hi == c.on_act else (lambda e: e.tensor_copy(hi, src))
    m = on_hi(copy, *marks)
    return c.on_dve(lambda e: e.tensor_tensor(lo, src, hi.bitcast(F32), ALU.subtract), m, *lo_marks)


def product(c, out, weights, moving, start, stop, *marks):
    (w_hi, w_lo), (x_hi, x_lo) = weights, moving
    c.on_pe(lambda e: e.matmul(out, w_hi, x_hi, start=start, stop=False, skip_group_check=True), *marks)
    c.on_pe(lambda e: e.matmul(out, w_hi, x_lo, start=False, stop=False, skip_group_check=True))
    return c.on_pe(lambda e: e.matmul(out, w_lo, x_hi, start=False, stop=stop, skip_group_check=True))



def norm_pieces(c, work, src, dst, *ready):
    stats, mean_var, rstd = work
    for b in range(CHUNK):
        m = c.on_dve(lambda e: e.bn_stats(stats[:, b, :], src[:, b, :]), *ready)
    for b in range(CHUNK):
        last = c.on_dve(lambda e: e.bn_aggr(mean_var[:, b, :], stats[:, b, :]), m)
    last = c.on_dve(lambda e: e.tensor_scalar(rstd[:, :], mean_var[:, :, 1], EPS_LN, None, ALU.add), last)
    yield
    root = c.on_act(lambda e: e.activation(rstd[:, :], rstd[:, :], ACT.Sqrt), last)
    yield
    inv = c.on_dve(lambda e: e.reciprocal(rstd[:, :], rstd[:, :]), root)
    for b in range(CHUNK):
        m = c.on_dve(lambda e: e.tensor_scalar(dst[:, b, :], src[:, b, :], mean_var[:, b, 0:1], rstd[:, b:b + 1], ALU.subtract, ALU.mult), inv)
    return m


def column_pieces(c, src, dst, place, *ready, scale=None, bias=None):
    for half in range(2):
        bank, free = c.banks[place[0]], place[1][place[0]]
        for b in range(2):
            for k in range(DK):
                pe = c.on_pe(lambda e: e.transpose(bank[:, (2 * k + b) * P:(2 * k + b + 1) * P], src[:, 2 * half + b, k * P:(k + 1) * P], c.ident[:, :]),
                             c.ident_ready, *ready, *free)
        if scale is None:
            a = c.on_act(lambda e: e.copy(dst[:, :, half * 2 * P:(half + 1) * 2 * P], bank[:, :].rearrange("p (k n) -> p k n", k=DK)), pe)
        for k in range(DK if scale is not None else 0):
            a = c.on_act(lambda e: e.activation(dst[:, k, half * 2 * P:(half + 1) * 2 * P], bank[:, 2 * k * P:2 * (k + 1) * P], ACT.Identity,
                                                bias=bias[:, k:k + 1], scale=scale[:, k:k + 1]), pe)
        place[1][place[0]] = [a]
        yield
    return pe, a


def run(pieces):
    while True:
        try:
            next(pieces)
        except StopIteration as end:
            return end.value


def norm_work(c, w, tag):
    return tuple(c.sbuf(w, f"{tag}_{name}", shape) for name, shape in (("stats", [P, CHUNK, 6]), ("mean_var", [P, CHUNK, 2]), ("rstd", [P, CHUNK])))


class NormWork:

    def __init__(self, c, w, tag, columns=False):
        sb = lambda name, shape: c.sbuf(w, f"{tag}_{name}", shape)
        self.work = norm_work(c, w, tag)
        self.rows = sb("rows", [P, CHUNK, D])
        self.columns = sb("columns", [P, DK, BANK]) if columns else None
        self.read = []


HEADS, HD = 16, 8
POS = D
QPART = (0, 0, 0, 1, 1, 1, 2, 2, 2)
KPART = (0, 1, 2, 0, 1, 2, 0, 1, 2)
TERM_ROWS = len(QPART) * HD
MAX_ROWS = 3
TILES = 4


def layer0_attention(c, io):
    resid, ctx = c.resid, c.ctx
    with ExitStack() as w:
        sb = lambda name, shape, dtype=F32: c.sbuf(w, name, shape, dtype)
        wqT, wkT, wvT, woT = (sb(f"a_{n}", [P, P]) for n in ("wqT", "wkT", "wvT", "woT"))
        bias = sb("a_bias", [P, 4])
        normed = sb("a_normed", [P, NB, D])
        vaug = sb("a_vaug", [P, NB, 2, HEADS, HD + 1])
        SLOTS = 3
        whole = [sb(f"a_whole{i}", [P, 2, BANK]) for i in range(SLOTS)]
        parts = [sb(f"a_parts{i}", [P, 2, 3, BANK], BF16) for i in range(SLOTS)]
        RING = 4
        rows = TERM_ROWS + MAX_ROWS
        qs = [sb(f"a_qs{i}", [rows, HEADS, POS], BF16) for i in range(RING)]
        ks = [sb(f"a_ks{i}", [96, HEADS, POS], BF16) for i in range(RING)]
        negmax = [sb(f"a_negmax{i}", [P, HEADS, 2]) for i in range(2)]
        mrow = [sb(f"a_mrow{i}", [32, P]) for i in range(2)]
        mparts = [sb(f"a_mparts{i}", [32, 3, P], BF16) for i in range(2)]
        EXPS = 8
        expo = [sb(f"a_exp{i}", [P, 2, POS]) for i in range(EXPS)]
        inv = [sb(f"a_inv{i}", [P, 2, TILES]) for i in range(2)]
        outq = [sb(f"a_outq{i}", [P, 2, HEADS, HD]) for i in range(2)]
        sumT = [sb(f"a_sumT{i}", [P, POS]) for i in range(2)]
        outT = [sb(f"a_outT{i}", [P, POS]) for i in range(2)]
        proj = [sb(f"a_proj{i}", [P, POS]) for i in range(2)]

        weights_in, x_in, ctx_in = c.tally("a_weights_in"), c.x_in, c.ctx_in
        for dst, name in ((wqT, "wqT"), (wkT, "wkT"), (wvT, "wvT"), (woT, "woT")):
            c.load(dst[:, :], io["a_" + name], weights_in)
        weights = c.load(bias[:, :], io["a_bias"], weights_in)

        for chunk in range(1, NCHUNK):
            c.load_inputs(chunk)

        ones = c.on_dve(lambda e: e.memset(vaug[:, :, :, :, HD], 1.0))
        ks_ones = [c.on_pool(lambda e: e.memset(ks[r][64:96, :, :], 1.0)) for r in range(RING)]

        stacked, stored = {}, {}
        stack_in = [c.tally(f"a_stack_in{i}") for i in range(RING)]
        max_in = [c.tally(f"a_max_in{i}") for i in range(RING)]

        def stack(b, *free):
            r, parts_of = b % RING, lambda n: io[f"a_{n}_parts"][b].rearrange("t (d h) n -> t d (h n)", d=HD)
            flat = lambda t, first, count: t[first * HD:(first + count) * HD, :, :].rearrange("p h n -> p (h n)")
            for t in range(3):
                c.load(flat(qs[r], 3 * t, 3), parts_of("q")[t].unsqueeze(0).broadcast_to([3, HD, HEADS * POS]), stack_in[r],
                       stored[0, b // 2], stored[1, b // 2], ks_ones[r], *free)
                m = c.load(flat(ks[r], 3 * t, 3), parts_of("k"), stack_in[r])
            return m

        normed_by = [norm_pieces(c, norm_work(c, w, f"a_norm{chunk}"), resid[:, chunk * CHUNK:(chunk + 1) * CHUNK, :],
                                 normed[:, chunk * CHUNK:(chunk + 1) * CHUNK, :], x_in[chunk * CHUNK]) for chunk in range(NCHUNK)]
        norm = [run(normed_by[0])] * CHUNK
        split_out = {n: [c.tally(f"a_{n}_out{i}") for i in range(NB // 2)] for n in "qk"}
        freed, rounded = {}, {}

        def project(i):
            r = i % SLOTS
            for n, (wT, src, b) in enumerate(((wqT, normed, 0), (wkT, ctx, 1))):
                bank = c.banks[n + 4 * (i % 2)]
                pe = c.on_pe(lambda e: e.matmul(bank[:, :], wT[:, :], src[:, 2 * i:2 * i + 2, :].rearrange("p b n -> p (b n)"),
                                                start=True, stop=True),
                             weights, norm[2 * i + 1] if n == 0 else None, *(ctx_in[2 * i:2 * i + 2] if n else ()),
                             freed.get((n, i % 2)))
                c.on_act(lambda e: e.activation(whole[r][:, n, :], bank[:, :], ACT.Identity, bias=bias[:, b:b + 1]),
                         pe, stored.get((n, i - SLOTS)))
                rounded[n, i] = freed[n, i % 2] = c.on_act(
                    lambda e: e.activation(parts[r][:, n, 0, :], bank[:, :], ACT.Identity, bias=bias[:, b:b + 1]))
            bank = c.banks[2 + 4 * (i % 2)]
            for j in range(4):
                b, kb = 2 * i + j // 2, j % 2
                pe = c.on_pe(lambda e: e.matmul(bank[:, j * P:(j + 1) * P], ctx[:, b, kb * P:(kb + 1) * P], wvT[:, :],
                                                start=True, stop=True), freed.get(("v", i % 2)))
            freed["v", i % 2] = v_ready = c.on_dve(
                lambda e: e.tensor_copy(vaug[:, 2 * i:2 * i + 2, :, :, 0:HD].rearrange("p b k h d -> p (b k) h d"),
                                        bank[:, :].rearrange("p (j h d) -> p j h d", j=4, h=HEADS)), pe, ones)
            return v_ready

        def split(i):
            r = i % SLOTS
            for n, on in enumerate((c.on_dve, c.on_pool)):
                x, part = whole[r][:, n, :], parts[r][:, n, :, :]
                m = on(lambda e: e.tensor_tensor(x, x, part[:, 0, :], ALU.subtract), rounded[n, i])
                m = c.on_act(lambda e: e.copy(part[:, 1, :], x), m)
                done = on(lambda e: e.tensor_tensor(part[:, 2, :], x, part[:, 1, :], ALU.subtract), m)
                for j in range(2):
                    stored[n, i] = c.load(io[f"a_{'qk'[n]}_parts"][2 * i + j].rearrange("t p n -> p t n"),
                                          part[:, :, j * POS:(j + 1) * POS], split_out["qk"[n]][i], done)

        for i in range(NB // 2 + 1):
            if i < NB // 2:
                v_ready = project(i)
            if i % 2 == 0 and i // 2 + 1 < NCHUNK:
                norm += [run(normed_by[i // 2 + 1])] * CHUNK
            if i >= 1:
                split(i - 1)
            if i == 3:
                stacked[0] = stack(0)
        bank_free = {n: [(c.pe, c.pe.count), (c.act, c.act.count), freed["v", 0], freed["v", 1]] for n in range(8)}
        for b in range(1, RING):
            stacked[b] = stack(b)

        max_rows, max_done, mfree = {}, {}, {}

        def score_max(b, h):
            bank = h % 2
            for qb in range(2):
                pe = c.on_pe(lambda e: e.matmul(c.banks[bank][:, qb * POS:(qb + 1) * POS], qs[b % RING][0:TERM_ROWS, h, qb * P:(qb + 1) * P],
                                                ks[b % RING][0:TERM_ROWS, h, :], start=True, stop=True), stacked[b], *bank_free[bank])
            m = c.on_dve(lambda e: e.tensor_reduce(negmax[b % 2][:, h, :], c.banks[bank][:, :].rearrange("p (q n) -> p q n", q=2),
                                                   AX.X, ALU.max, negate=True), pe, mfree.get(b % 2))
            bank_free[bank] = [m]
            max_done[b] = m

        def max_to_rows(b):
            i, bank = b % 2, c.banks[7]
            pe = c.on_pe(lambda e: e.transpose(bank[0:32, 0:P], negmax[i][:, :, :].rearrange("p h q -> p (h q)"), c.ident[:, :]),
                         max_done[b], c.ident_ready, *bank_free[7])
            mfree[i] = pe
            c.on_act(lambda e: e.copy(mrow[i][:, :], bank[0:32, 0:P]), pe, max_rows.get(b - 2))
            a = c.on_act(lambda e: e.copy(mparts[i][:, 0, :], bank[0:32, 0:P]))
            bank_free[7] = [a]
            m = c.on_pool(lambda e: e.tensor_tensor(mrow[i][:, :], mrow[i][:, :], mparts[i][:, 0, :], ALU.subtract), a)
            m = c.on_pool(lambda e: e.tensor_copy(mparts[i][:, 1, :], mrow[i][:, :]), m)
            done = c.on_pool(lambda e: e.tensor_tensor(mparts[i][:, 2, :], mrow[i][:, :], mparts[i][:, 1, :], ALU.subtract), m)
            for part in range(MAX_ROWS):
                row = TERM_ROWS + part
                max_rows[b] = c.load(qs[b % RING][row:row + 1, :, :].rearrange("o h (q n) -> o (h q) n", q=2),
                                     mparts[i][:, part, :], max_in[b % RING], done)

        exp_done, exp_free, added, divided = {}, {}, {}, {}
        GROUPS = HEADS // TILES

        def exponentials(b, h):
            bank, n = 2 + h % 2, (b * HEADS + h) % EXPS
            for kb in range(2):
                pe = c.on_pe(lambda e: e.matmul(c.banks[bank][:, kb * POS:(kb + 1) * POS], ks[b % RING][0:rows, h, kb * P:(kb + 1) * P],
                                                qs[b % RING][0:rows, h, :], start=True, stop=True), max_rows[b], *bank_free[bank])
            exp_done[b, h] = c.on_act(lambda e: e.activation(expo[n][:, :, :].rearrange("p k q -> p (k q)"), c.banks[bank][:, :], ACT.Exp,
                                                             scale=float(1 / np.sqrt(np.float32(P)))), pe, exp_free.get(n))
            bank_free[bank] = [exp_done[b, h]]

        def times_v(b, g):
            bank = 4 + g % 2
            for kb in range(2):
                for tile in range(TILES):
                    h = TILES * g + tile
                    n = (b * HEADS + h) % EXPS
                    pe = c.on_pe(lambda e: e.matmul(
                        c.banks[bank][32 * tile:32 * tile + HD + 1, 0:POS], vaug[:, b, kb, h, :], expo[n][:, kb, :],
                        start=kb == 0, stop=kb == 1), exp_done[b, h], v_ready, *bank_free[bank])
                    if kb == 1:
                        exp_free[n] = pe
            a = c.on_act(lambda e: e.copy(sumT[g % 2][:, :], c.banks[bank][:, 0:POS]), pe, divided.get((b, g - 2), divided.get((b - 1, g + 2))))
            bank_free[bank] = [a]
            return a

        def normalise(b, g, copied):
            i, bank = b % 2, c.banks[6]
            for qb in range(2):
                pe = c.on_pe(lambda e: e.transpose(bank[:, qb * P:(qb + 1) * P], sumT[g % 2][:, qb * P:(qb + 1) * P], c.ident[:, :]),
                             copied, *bank_free[6])
            view = bank[:, 0:2 * P].rearrange("p (q h d) -> p q h d", q=2, h=TILES)
            m = c.on_dve(lambda e: e.reciprocal(inv[g % 2][:, :, :], view[:, :, :, HD]), pe)
            m = c.on_dve(lambda e: e.tensor_tensor(outq[i][:, :, TILES * g:TILES * (g + 1), :], view[:, :, :, 0:HD],
                                                   inv[g % 2][:, :, :].unsqueeze(3).to_broadcast([P, 2, TILES, HD]), ALU.mult), m, added.get(b - 2))
            bank_free[6] = [m]
            divided[b, g] = pe
            return m

        def to_features(b, ready):
            i, bank = b % 2, c.banks[7]
            for qb in range(2):
                pe = c.on_pe(lambda e: e.transpose(bank[:, qb * P:(qb + 1) * P], outq[i][:, qb, :, :].rearrange("p h d -> p (h d)"),
                                                   c.ident[:, :]), ready, *bank_free[7])
            a = c.on_act(lambda e: e.activation(outT[i][:, :], bank[:, 0:POS], ACT.Identity, bias=bias[:, 2:3]), pe)
            bank_free[7] = [a]
            return a

        def residual(b, ready):
            i, bank = b % 2, c.banks[7]
            pe = c.on_pe(lambda e: e.matmul(bank[:, 0:POS], woT[:, :], outT[i][:, :], start=True, stop=True), ready, *bank_free[7])
            a = c.on_act(lambda e: e.activation(proj[i][:, :], bank[:, 0:POS], ACT.Identity, bias=bias[:, 3:4]), pe, added.get(b - 2))
            bank_free[7] = [a]
            added[b] = c.on_dve(lambda e: e.scalar_tensor_tensor(resid[:, b, :], proj[i][:, :], c.gates[:, 0:1], resid[:, b, :],
                                                                 ALU.mult, ALU.add), a, c.gates_ready)

        for bank in (4, 5):
            bank_free[bank] = bank_free[bank] + [c.on_dve(lambda e: e.memset(c.banks[bank][:, :], 0.0), *bank_free[bank])]

        PAIRS = HEADS // 2
        AHEAD = HEADS + 3 * HEADS // 4

        def maxima(i):
            if i < NB * HEADS:
                score_max(*divmod(i, HEADS))
            b, h = divmod(i - 2, HEADS)
            if h == HEADS - 1 and 0 <= b < NB:
                max_to_rows(b)

        for i in range(AHEAD):
            maxima(i)
        copied, ended = {}, {}
        for n in range(NB * PAIRS + 6):
            b, j = divmod(n, PAIRS)
            for h in (2 * j, 2 * j + 1):
                maxima(b * HEADS + h + AHEAD)
                if b < NB:
                    exponentials(b, h)
            if n % 2 == 0 and 2 <= n < NB * PAIRS + 2:
                b, g = divmod((n - 2) // 2, GROUPS)
                copied[b, g] = times_v(b, g)
            if n % 2 == 1 and 3 <= n < NB * PAIRS + 3:
                b, g = divmod((n - 3) // 2, GROUPS)
                ended[b] = normalise(b, g, copied[b, g])
            if n >= 12 and (n - 12) % PAIRS == 0:
                ended[n // PAIRS - 1] = to_features(n // PAIRS - 1, ended[n // PAIRS - 1])
            if n >= 13 and (n - 13) % PAIRS == 0:
                residual(n // PAIRS - 1, ended[n // PAIRS - 1])
            b, j = divmod(n, PAIRS)
            if j == PAIRS - 1 and b + RING < NB:
                stacked[b + RING] = stack(b + RING, (c.pe, c.pe.count))
        c.join()


EXPERTS, WIDTH, TOP = 64, 64, 8
PAIRS = EXPERTS // 2


def layer0_experts(c, io):
    resid, xT = c.resid, c.columns
    with ExitStack() as w:
        sb = lambda name, shape, dtype=F32: c.sbuf(w, name, shape, dtype)
        RING, SPLITS = 4, 3
        GU = DK * 2 * P
        raw = [sb(f"e_raw{i}", [P, GU + D]) for i in range(RING)]
        split = [[sb(f"e_weights_{n}{i}", [P, GU + D], F32R) for n in ("hi", "lo")] for i in range(SPLITS)]
        x_split = [sb(f"e_x_{n}", [P, DK, T], F32R) for n in ("hi", "lo")]
        TOKENS = T // 2
        comb_wide = [sb(f"e_comb_wide{i}", [P, TOKENS]) for i in range(RING)]
        loaded = [c.tally(f"e_loaded{i}") for i in range(RING)]
        comb_loaded = [c.tally(f"e_comb_loaded{i}") for i in range(RING)]
        router = sb("e_router", [P, DK, EXPERTS + 1])
        router_in = c.load(router[:, :, :], io["e_router"], c.tally("e_router_in"))
        combT = sb("e_comb_rows", [EXPERTS + 1, T])

        weights_in, raw_free, split_free, split_done, comb_free = {}, {}, {}, {}, {}
        units = [(half, pair) for half in range(2) for pair in range(PAIRS + 1)]

        def load_weights(u):
            pair, r = units[u][1], u % RING
            if pair < PAIRS:
                weights_in[u] = c.load(raw[r][:, :], io["e_weights"][pair], loaded[r], raw_free.get(r))
            else:
                c.load(raw[r][:, 0:GU // 2], io["e_shared_gate_up"], loaded[r], raw_free.get(r))
                weights_in[u] = c.load(raw[r][0:WIDTH, GU:], io["e_shared_down"], loaded[r])

        def split_weights(u):
            r, i = u % RING, u % SPLITS
            spans = [(P, slice(0, GU + D))] if units[u][1] < PAIRS else [(P, slice(0, GU // 2)), (WIDTH, slice(GU, GU + D))]
            for rows, cols in spans:
                src, (hi, lo) = raw[r][0:rows, cols], (t[0:rows, cols] for t in split[i])
                split_done[u] = raw_free[r] = split2(c, c.on_act, src, hi, lo, weights_in[u], split_free.get(i))

        for u in range(RING - 1):
            load_weights(u)

        class Router:

            def __init__(self, tag):
                s2 = lambda name, shape: sb(f"e_{name}_{tag}", shape)
                self.norm = NormWork(c, w, f"e_{tag}")
                self.probs, self.left = s2("probs", [P, CHUNK, EXPERTS]), s2("left", [P, CHUNK, EXPERTS])
                self.logits, self.comb = s2("logits", [P, CHUNK, EXPERTS + 1]), s2("comb", [P, CHUNK, EXPERTS + 1])
                self.best = s2("best", [P, CHUNK, TOP])
                self.peak, self.total, self.weight = (s2(n, [P, CHUNK]) for n in ("peak", "total", "weight"))
                self.done = []

        x_ready, comb_stored = {}, {}

        def route(router_of, chunk, place):
            t, norm = router_of, router_of.norm
            rows, cols = slice(chunk * CHUNK, (chunk + 1) * CHUNK), slice(chunk * BANK, (chunk + 1) * BANK)
            m = yield from norm_pieces(c, norm.work, resid[:, rows, :], norm.rows, c.x_in[chunk * CHUNK], *t.done)
            yield
            pe, a = yield from column_pieces(c, norm.rows, xT[:, :, cols], place, m)
            bank, free = c.banks[place[0]], place[1][place[0]]
            for i in range(CHUNK):
                b = chunk * CHUNK + i
                for k in range(DK):
                    pe = c.on_pe(lambda e: e.matmul(bank[:, i * (EXPERTS + 1):(i + 1) * (EXPERTS + 1)], xT[:, k, b * P:(b + 1) * P],
                                                    router[:, k, :], start=k == 0, stop=k == DK - 1), a, router_in, *free)
            m = c.on_act(lambda e: e.copy(t.logits[:, :, :], bank[:, 0:CHUNK * (EXPERTS + 1)].rearrange("p (b n) -> p b n", b=CHUNK)), pe)
            place[1][place[0]] = [m]
            hi, lo = (part[:, :, cols] for part in x_split)
            a = c.on_act(lambda e: e.copy(hi, xT[:, :, cols]))
            x_ready[chunk] = c.on_pool(lambda e: e.tensor_tensor(lo, xT[:, :, cols], hi.bitcast(F32), ALU.subtract), a)
            yield
            wide = lambda v: v[:, :].unsqueeze(2).to_broadcast([P, CHUNK, EXPERTS])
            routed, probs, left, best, comb = t.logits[:, :, 0:EXPERTS], t.probs, t.left, t.best, t.comb
            m = c.on_dve(lambda e: e.tensor_reduce(t.peak[:, :], routed, AX.X, ALU.max), m)
            m = c.on_dve(lambda e: e.tensor_tensor(probs[:, :, :], routed, wide(t.peak), ALU.subtract), m)
            yield
            m = c.on_act(lambda e: e.activation(probs[:, :, :], probs[:, :, :], ACT.Exp), m)
            shared = c.on_act(lambda e: e.activation(comb[:, :, EXPERTS], t.logits[:, :, EXPERTS], ACT.Exp, scale=-1.0))
            yield
            m = c.on_dve(lambda e: e.tensor_reduce(t.total[:, :], probs[:, :, :], AX.X, ALU.add), m)
            m = c.on_dve(lambda e: e.reciprocal(t.total[:, :], t.total[:, :]), m)
            m = c.on_dve(lambda e: e.tensor_tensor(probs[:, :, :], probs[:, :, :], wide(t.total), ALU.mult), m)
            yield
            for b in range(CHUNK):
                m8 = c.on_dve(lambda e: e.max(best[:, b, :], probs[:, b, :]), m)
            for b in range(CHUNK):
                m = c.on_dve(lambda e: e.match_replace(left[:, b, :], best[:, b, :], probs[:, b, :], -1.0), m8)
            yield
            m = c.on_dve(lambda e: e.tensor_reduce(t.weight[:, :], best[:, :, :], AX.X, ALU.add), m)
            m = c.on_dve(lambda e: e.reciprocal(t.weight[:, :], t.weight[:, :]), m)
            m = c.on_dve(lambda e: e.scalar_tensor_tensor(left[:, :, :], left[:, :, :], 0.0, probs[:, :, :], ALU.is_lt, ALU.mult), m)
            m = c.on_dve(lambda e: e.tensor_tensor(comb[:, :, 0:EXPERTS], left[:, :, :], wide(t.weight), ALU.mult), m)
            m = c.on_dve(lambda e: e.tensor_scalar(comb[:, :, EXPERTS], comb[:, :, EXPERTS], 1.0, None, ALU.add), shared)
            m = c.on_dve(lambda e: e.reciprocal(comb[:, :, EXPERTS], comb[:, :, EXPERTS]), m)
            yield
            bank, free = c.banks[place[0]], place[1][place[0]]
            for i in range(CHUNK):
                pe = c.on_pe(lambda e: e.transpose(bank[0:EXPERTS + 1, i * P:(i + 1) * P], comb[:, i, :], c.ident[:, :]), m, *free)
            a = c.on_act(lambda e: e.copy(combT[:, cols], bank[0:EXPERTS + 1, :]), pe)
            place[1][place[0]] = [a]
            comb_stored[chunk] = c.load(io["e_combT"][:, cols], combT[:, cols], c.tally(f"e_comb_stored{chunk}"), a)
            t.done = [m, pe, a, x_ready[chunk]]

        bank_free = {n: [] for n in range(8)}
        routers = [Router(i) for i in range(2)]
        HALF = NCHUNK // 2
        first = [route(routers[i], i, [i, bank_free]) for i in range(HALF)]
        while first:
            first = [pieces for pieces in first if next(pieces, "ended") != "ended"]
            if 0 not in split_done:
                split_weights(0)

        def load_comb(u):
            (half, pair), r = units[u], u % RING
            cols = slice(half * TOKENS, (half + 1) * TOKENS)
            for i in range(2 if pair < PAIRS else 1):
                m = c.load(comb_wide[r][i * WIDTH:(i + 1) * WIDTH, :],
                           io["e_combT"][2 * pair + i:2 * pair + i + 1, cols].broadcast_to([WIDTH, TOKENS]),
                           comb_loaded[r], *(comb_stored[half * HALF + k] for k in range(HALF)), comb_free.get(r))
            comb_in[u] = m

        with ExitStack() as w3:
            s3 = lambda name, shape, dtype=F32: c.sbuf(w3, name, shape, dtype)
            HR = 3
            silu = [s3(f"e_silu{i}", [P, BANK]) for i in range(2)]
            gated = [s3(f"e_gated{i}", [P, BANK]) for i in range(2)]
            hidden = [s3(f"e_hidden{i}", [P, BANK]) for i in range(2)]
            hidden_split = [[s3(f"e_hidden_{n}{i}", [P, BANK], F32R) for n in ("hi", "lo")] for i in range(HR)]
            comb_in, resid_ready = {}, {}
            chunks = TOKENS // BANK
            steps = [(u, chunk) for u in range(len(units)) for chunk in range(chunks)]
            rows_of = lambda n: P if units[steps[n][0]][1] < PAIRS else WIDTH
            down_done, weighed, ready, gated_free, silu_free = {}, {}, {}, {}, {}

            def gate_and_up(n):
                u, chunk = steps[n]
                (half, pair), r, i, rows = units[u], u % RING, n % 2, rows_of(n)
                cols = slice(half * TOKENS + chunk * BANK, half * TOKENS + (chunk + 1) * BANK)
                for which in range(2):
                    bank = 2 * i + which
                    for k in range(DK):
                        at = (2 * k + which) * rows
                        pe = product(c, c.banks[bank][0:rows, :], [t[:, at:at + rows] for t in split[u % SPLITS]],
                                     [t[:, k, cols] for t in x_split], k == 0, k == DK - 1, split_done[u], x_ready[half * HALF + chunk], *bank_free[bank])
                    if which == 0:
                        a = c.on_act(lambda e: e.activation(silu[i][0:rows, :], c.banks[bank][0:rows, :], ACT.Silu), pe, silu_free.get(n - 2))
                        bank_free[bank] = [a]
                m = c.on_dve(lambda e: e.tensor_tensor(gated[i][0:rows, :], silu[i][0:rows, :], c.banks[bank][0:rows, :], ALU.mult), a, pe,
                             gated_free.get(n - 2))
                bank_free[bank], silu_free[n] = [m], m
                gated_free[n] = weighed[n] = comb_free[r] = c.on_pool(
                    lambda e: e.tensor_tensor(hidden[i][0:rows, :], gated[i][0:rows, :], comb_wide[r][0:rows, chunk * BANK:(chunk + 1) * BANK],
                                              ALU.mult), m, comb_in[u], ready.get(n - 2))

            def split_hidden(n):
                rows = rows_of(n)
                ready[n] = split2(c, c.on_act, hidden[n % 2][0:rows, :], *(t[0:rows, :] for t in hidden_split[n % HR]),
                                  weighed[n], down_done.get(n - HR))

            def to_out(n):
                u, chunk = steps[n]
                (half, pair), rows = units[u], rows_of(n)
                for t in range(BANK // P):
                    tile = chunk * (BANK // P) + t
                    bank = 4 + tile // 2
                    pe = product(c, c.banks[bank][:, (tile % 2) * D:(tile % 2 + 1) * D], [h[0:rows, t * P:(t + 1) * P] for h in hidden_split[n % HR]],
                                 [v[0:rows, GU:] for v in split[u % SPLITS]], pair == 0 and tile % 2 == 0, pair == PAIRS, ready[n], *bank_free[bank])
                down_done[n] = split_free[u % SPLITS] = pe
                if pair == PAIRS:
                    resid_ready[half * HALF + chunk] = []
                    for bank in (4 + 2 * chunk, 5 + 2 * chunk):
                        b = half * NB // 2 + 2 * (bank - 4)
                        bank_free[bank] = [c.on_dve(lambda e: e.scalar_tensor_tensor(
                            resid[:, b:b + 2, :], c.banks[bank][:, :].rearrange("p (b n) -> p b n", b=2), c.gates[:, 1:2], resid[:, b:b + 2, :],
                            ALU.mult, ALU.add), pe, c.gates_ready)]
                        resid_ready[half * HALF + chunk] += bank_free[bank]

            for u in range(RING - 1):
                load_comb(u)
            LAG = 2
            head_mean = s3("e_head_mean", [P, NB, CELLS])
            place, next_norm = [None, bank_free], NormWork(c, w3, "m_first")
            behind = [route(routers[i], HALF + i, place) for i in range(HALF)]
            for n in range(len(steps) + LAG):
                if n == len(units) + LAG + 1:
                    behind += [mlstm_columns(c, next_norm, chunk, place, *resid_ready[chunk]) for chunk in range(HALF)]
                if behind and n >= 2:
                    place[0] = 2 * (n % 2) + 1
                    if next(behind[0], "ended") == "ended":
                        behind.pop(0)
                if n == NB:
                    load_context_columns(c, io)
                if n < NB:
                    c.ctx_centred = centre_context(c, head_mean, n, *c.ctx_in)
                if 1 <= n <= len(steps):
                    split_hidden(n - 1)
                if n < len(steps):
                    gate_and_up(n)
                    u, chunk = steps[n]
                    if chunk == chunks - 1 and u + RING - 1 < len(units):
                        load_weights(u + RING - 1)
                        load_comb(u + RING - 1)
                if n >= LAG:
                    to_out(n - LAG)
                if n < len(steps) and steps[n][1] == 0 and steps[n][0] + 1 < len(units):
                    split_weights(steps[n][0] + 1)
            c.join()


CELLS, CD = 16, 16
CELL_EPS = 1e-6
LOWEST = -3e38
SPAN = 32


def centre_context(c, mean, b, *ready):
    heads = c.ctx[:, b, :].rearrange("p (h d) -> p h d", h=CELLS)
    m = c.on_dve(lambda e: e.tensor_reduce(mean[:, b, :], heads, AX.X, ALU.add), *ready)
    m = c.on_dve(lambda e: e.tensor_scalar(mean[:, b, :], mean[:, b, :], 1.0 / CD, None, ALU.mult), m)
    return c.on_dve(lambda e: e.tensor_tensor(heads, heads, mean[:, b, :].unsqueeze(2).to_broadcast([P, CELLS, CD]), ALU.subtract), m)


def load_context_columns(c, io):
    c.ctxT_in = c.load(c.ctxT[:, :, :], io["m_ctxT"].rearrange("(k p) t -> p k t", p=P), c.tally("m_ctxT_in"))


def mlstm_columns(c, norm, chunk, place, *ready):
    rows, cols = slice(chunk * CHUNK, (chunk + 1) * CHUNK), slice(chunk * BANK, (chunk + 1) * BANK)
    m = yield from norm_pieces(c, norm.work, c.resid[:, rows, :], norm.rows, c.x_in[chunk * CHUNK], *ready, *norm.read)
    yield
    pe, a = yield from column_pieces(c, norm.rows, c.columns[:, :, cols], place, m)
    norm.read, c.columns_ready[chunk] = [pe], a


def layer1_mlstm(c, io):
    resid, ctx, xT = c.resid, c.ctx, c.columns
    with ExitStack() as w:
        sb = lambda name, shape, dtype=F32: c.sbuf(w, name, shape, dtype)
        ctxT = c.ctxT
        small_in = c.tally("m_small_in")
        gate_w = sb("m_gate_w", [P, 3 * DK, 2 * SPAN])
        gate_bias, head_mask, ln_scale = sb("m_gate_bias", [P, 2]), sb("m_head_mask", [P, CELLS // DK]), sb("m_ln_scale", [P, D])
        for dst, src in ((gate_w[:, :, :], io["m_gate_w"]), (gate_bias[:, :], io["m_gate_bias"]), (head_mask[:, :], io["m_head_mask"])):
            c.load(dst, src, small_in)
        small = c.load(ln_scale[:, :], io["m_ln_scale"].broadcast_to([P, D]), small_in)
        vaug = sb("m_vaug", [P, NB, CELLS, CD + 1])
        g_token, e_token = sb("m_g_token", [P, NB, CELLS]), sb("m_e_token", [P, NB, CELLS])
        square_sum, inv_norm = sb("m_square_sum", [P, NB * CELLS]), sb("m_inv_norm", [P, NB * CELLS])
        cell = sb("m_cell", [P, NB, D])

        with ExitStack() as w2:
            s2 = lambda name, shape, dtype=F32: c.sbuf(w2, name, shape, dtype)
            for which, bank in ((0, 5), (1, 4)):
                for n in range(T // BANK):
                    rows = slice(n * SPAN, (n + 1) * SPAN)
                    for k in range(DK, 3 * DK):
                        c.on_pe(lambda e: e.matmul(c.banks[bank][rows, :], gate_w[:, k, which * SPAN:(which + 1) * SPAN],
                                                   ctxT[:, k % DK, n * BANK:(n + 1) * BANK], start=k == DK, stop=False, skip_group_check=True),
                                small, c.ctxT_in)
            with ExitStack() as w3:
                left = [chunk for chunk in range(NCHUNK) if chunk not in c.columns_ready]
                inputs = [mlstm_columns(c, NormWork(c, w3, f"m_norm{chunk}"), chunk, [i, {i: []}]) for i, chunk in enumerate(left)]
                while inputs:
                    inputs = [pieces for pieces in inputs if next(pieces, "ended") != "ended"]
                inputs_done = c.now()
            ig, fg, scratch, keep, drop, peak = (s2(f"m_{n}", [P, BANK]) for n in ("ig", "fg", "scratch", "keep", "drop", "peak"))
            first = lambda t: t[:, :].rearrange("p (b t) -> p b t", t=P)[:, :, 0]
            c.on_pool(lambda e: e.memset(keep[:, :], 1.0), *inputs_done)
            c.on_pool(lambda e: e.memset(drop[:, :], 0.0))
            c.on_pool(lambda e: e.memset(first(keep), 0.0))
            resets = c.on_pool(lambda e: e.memset(first(drop), LOWEST))
            for which, bank in ((0, 5), (1, 4)):
                for n in range(T // BANK):
                    cols, rows = slice(n * BANK, (n + 1) * BANK), slice(n * SPAN, (n + 1) * SPAN)
                    for k in range(DK):
                        pe = c.on_pe(lambda e: e.matmul(c.banks[bank][rows, :], gate_w[:, k, which * SPAN:(which + 1) * SPAN], xT[:, k, cols],
                                                        start=False, stop=k == DK - 1, skip_group_check=True), c.columns_ready[n])
                if which == 0:
                    i_done = pe
            a = c.on_act(lambda e: e.activation(fg[:, :], c.banks[4][:, :], ACT.Identity, bias=gate_bias[:, 1:2]), pe, *inputs_done)
            i_ready = c.on_act(lambda e: e.activation(ig[:, :], c.banks[5][:, :], ACT.Identity, bias=gate_bias[:, 0:1]), i_done)
            c.on_dve(lambda e: e.memset(vaug[:, :, :, CD], 1.0))
            vaug_ready = c.on_dve(lambda e: e.tensor_copy(vaug[:, :, :, 0:CD], ctx[:, :, :].rearrange("p b (h d) -> p b h d", h=CELLS)), c.ctx_centred)
            m = c.on_dve(lambda e: e.scalar_tensor_tensor(scratch[:, :], fg[:, :], -1.0, fg[:, :], ALU.mult, ALU.min), a)
            m = c.on_act(lambda e: e.activation(scratch[:, :], scratch[:, :], ACT.Exp), m)
            m = c.on_act(lambda e: e.activation(scratch[:, :], scratch[:, :], ACT.Ln, bias=1.0), m)
            m = c.on_dve(lambda e: e.scalar_tensor_tensor(scratch[:, :], fg[:, :], 0.0, scratch[:, :], ALU.min, ALU.subtract), m)
            m = c.on_dve(lambda e: e.tensor_tensor_scan(fg[:, :], keep[:, :], scratch[:, :], 0.0, ALU.mult, ALU.add), m, resets)
            g = c.on_dve(lambda e: e.tensor_tensor(ig[:, :], ig[:, :], fg[:, :], ALU.subtract), m, i_ready)
            m = c.on_dve(lambda e: e.tensor_tensor_scan(peak[:, :], drop[:, :], ig[:, :], 0.0, ALU.add, ALU.max), g)
            neg = c.on_dve(lambda e: e.tensor_scalar(scratch[:, :], peak[:, :], -1.0, None, ALU.mult), m)
            peak_stored = c.tally("m_peak_stored")
            for n in range(T // BANK):
                negpeak_in = c.load(io["m_negpeak"][:, n * BANK:(n + 1) * BANK], scratch[n * SPAN:n * SPAN + CELLS, :], peak_stored, neg)
            peak_stored = negpeak_in
            m = c.on_dve(lambda e: e.tensor_tensor(fg[:, :], fg[:, :], peak[:, :], ALU.add), m)
            a = c.on_act(lambda e: e.activation(fg[:, :], fg[:, :], ACT.Exp, scale=-1.0), m)
            for rows, bank, dst, ready in ((ig, 6, g_token, g), (fg, 7, e_token, a)):
                for j in range(BANK // P):
                    pe = c.on_pe(lambda e: e.transpose(c.banks[bank][:, j * P:(j + 1) * P], rows[:, j * P:(j + 1) * P], c.ident[:, :]), ready)
                by_token = c.banks[bank][:, :].rearrange("p (j n h) -> p n j h", j=BANK // P, n=T // BANK)[:, :, :, 0:CELLS]
                a = c.on_act(lambda e: e.copy(dst[:, :, :].rearrange("p (n j) h -> p n j h", n=T // BANK), by_token), pe)
            token_ready = a
            scans_done = c.now() + [peak_stored]

        with ExitStack() as w2:
            s2 = lambda name, shape, dtype=F32: c.sbuf(w2, name, shape, dtype)
            RING = 3
            qblock = [s2(f"m_qblock{i}", [P, DK, CELLS // DK, P]) for i in range(2)]
            decay = [s2(f"m_decay{i}", [P, CELLS, P]) for i in range(RING)]
            product = [s2(f"m_product{i}", [P, CELLS, P]) for i in range(2)]
            sums = [s2(f"m_sums{i}", [P, BANK]) for i in range(2)]
            row_sums = [s2(f"m_row_sums{i}", [P, CELLS]) for i in range(2)]
            square = [s2(f"m_square{i}", [P, D]) for i in range(2)]
            denom = [s2(f"m_denom{i}", [P, CELLS]) for i in range(2)]
            peak_in = [c.tally(f"m_peak_in{i}") for i in range(RING)]
            bank_free = {n: scans_done for n in range(8)}
            for bank in (4, 5):
                bank_free[bank] = [c.on_dve(lambda e: e.memset(c.banks[bank][:, :], 0.0), *scans_done)]
            masked, decayed, multiplied, sums_free, out = {}, {}, {}, {}, {}
            per_half = CELLS // DK

            def decay_of(b):
                d = decay[b % RING]
                arrived = c.load(d[:, :, :], io["m_negpeak"].rearrange("h (b s) -> b h s", b=NB)[b].unsqueeze(0).broadcast_to([P, CELLS, P]),
                                 peak_in[b % RING], peak_stored, *scans_done, multiplied.get(b - RING))
                gt = g_token[:, b, :].unsqueeze(2).to_broadcast([P, CELLS, P])
                m = c.on_dve(lambda e: e.tensor_tensor(d[:, :, :], d[:, :, :], gt, ALU.add), arrived, token_ready)
                m = c.on_pool(lambda e: e.affine_select(out=d[:, :, :], in_=d[:, :, :], compare_op=ALU.is_ge, fill=LOWEST, base=0,
                                                        pattern=[[0, CELLS], [1, P]], channel_multiplier=-1), m)
                masked[b] = m

            def exponential(b):
                d = decay[b % RING]
                decayed[b] = c.on_act(lambda e: e.activation(d[:, :, :], d[:, :, :], ACT.Exp), masked[b])

            def block_queries(b):
                q = xT[:, 0, b * P:(b + 1) * P].unsqueeze(1).to_broadcast([P, per_half, P])
                h = head_mask[:, :].unsqueeze(2).to_broadcast([P, per_half, P])
                m = c.on_pool(lambda e: e.tensor_tensor(qblock[b % 2][:, 0, :, :], q, h, ALU.mult), *scans_done, scored.get(b - 2))
                for h in range(per_half):
                    a = c.on_act(lambda e: e.activation(qblock[b % 2][:, 1, h, :], xT[:, 1, b * P:(b + 1) * P], ACT.Identity,
                                                        scale=head_mask[:, h:h + 1]), *scans_done, scored.get(b - 2))
                blocked[b] = [m, a]

            blocked, scored, copied = {}, {}, {}

            def scores(b):
                for i in range(4):
                    k, q4 = divmod(i, 2)
                    pe = c.on_pe(lambda e: e.matmul(c.banks[i][:, :], ctxT[:, k, b * P:(b + 1) * P],
                                                    qblock[b % 2][:, k, 4 * q4:4 * q4 + 4, :].rearrange("p h s -> p (h s)"),
                                                    start=True, stop=True), *blocked[b], *bank_free[i])
                    m = c.on_dve(lambda e: e.tensor_tensor(product[b % 2][:, 4 * i:4 * i + 4, :].rearrange("p h s -> p (h s)"), c.banks[i][:, :],
                                                           decay[b % RING][:, 4 * i:4 * i + 4, :].rearrange("p h s -> p (h s)"), ALU.mult),
                                 pe, decayed[b], out.get(b - 2))
                    bank_free[i] = [m]
                scored[b], multiplied[b] = pe, m

            def times_v(b):
                bank = 4 + b % 2
                for i in range(4):
                    for tile in range(4):
                        h = 4 * i + tile
                        pe = c.on_pe(lambda e: e.matmul(c.banks[bank][32 * tile:32 * tile + CD + 1, i * P:(i + 1) * P], vaug[:, b, h, :],
                                                        product[b % 2][:, h, :], start=True, stop=True),
                                     multiplied[b], vaug_ready, *bank_free[bank])
                out[b] = pe
                a = c.on_act(lambda e: e.copy(sums[b % 2][:, :], c.banks[bank][:, :]), pe, sums_free.get(b - 2))
                bank_free[bank] = [a]
                return a

            def by_token(b, copied):
                for i in range(4):
                    pe = c.on_pe(lambda e: e.transpose(c.banks[6][:, i * P:(i + 1) * P], sums[b % 2][:, i * P:(i + 1) * P], c.ident[:, :]),
                                 copied, *bank_free[6])
                sums_free[b] = pe
                view, den = c.banks[6][:, :].rearrange("p (h d) -> p h d", h=CELLS), denom[b % 2]
                as_heads = lambda t: t.rearrange("p (h d) -> p h d", h=CELLS)
                row_sum, features = row_sums[b % 2], cell[:, b, :]
                copied = c.on_act(lambda e: e.copy(as_heads(features), view[:, :, 0:CD]), pe)
                m = c.on_act(lambda e: e.copy(row_sum[:, :], view[:, :, CD]), normed_by.get(b - 2))
                bank_free[6] = [m]
                squared[b] = c.on_act(lambda e: e.activation(square[b % 2][:, :], features, ACT.Square), copied, summed.get(b - 2))
                m = c.on_dve(lambda e: e.scalar_tensor_tensor(den[:, :], row_sum[:, :], -1.0, e_token[:, b, :], ALU.mult, ALU.max), m)
                normed_by[b] = m = c.on_dve(lambda e: e.tensor_tensor(den[:, :], row_sum[:, :], den[:, :], ALU.max), m)
                m = c.on_dve(lambda e: e.tensor_scalar(den[:, :], den[:, :], CELL_EPS, None, ALU.add), m)
                c.on_dve(lambda e: e.reciprocal(inv_norm[:, b * CELLS:(b + 1) * CELLS], den[:, :]), m)

            def scale(b):
                c.on_pool(lambda e: e.tensor_tensor(cell[:, b, :], cell[:, b, :], ln_scale[:, :], ALU.mult), squared[b], small)

            def sum_squares(b):
                summed[b] = c.on_dve(lambda e: e.tensor_reduce(square_sum[:, b * CELLS:(b + 1) * CELLS],
                                                               square[b % 2][:, :].rearrange("p (h d) -> p h d", h=CELLS), AX.X, ALU.add), squared[b])

            squared, summed, normed_by = {}, {}, {}
            for n in range(NB + 4):
                if n < NB:
                    block_queries(n)
                    decay_of(n)
                if 1 <= n <= NB:
                    exponential(n - 1)
                    scores(n - 1)
                if 2 <= n <= NB + 1:
                    copied[n - 2] = times_v(n - 2)
                if 3 <= n < NB + 3:
                    by_token(n - 3, copied[n - 3])
                if n >= 4:
                    sum_squares(n - 4)
                    scale(n - 4)
            cells_done = c.now()

        with ExitStack() as w2:
            factor, root = c.sbuf(w2, "m_factor", [P, NB * CELLS]), c.sbuf(w2, "m_root", [P, NB * CELLS])
            m = c.on_dve(lambda e: e.tensor_tensor(root[:, :], inv_norm[:, :], inv_norm[:, :], ALU.mult), *cells_done)
            m = c.on_dve(lambda e: e.tensor_tensor(root[:, :], root[:, :], square_sum[:, :], ALU.mult), m)
            m = c.on_dve(lambda e: e.tensor_scalar(root[:, :], root[:, :], 1.0 / CD, CELL_EPS, ALU.mult, ALU.add), m)
            m = c.on_act(lambda e: e.activation(root[:, :], root[:, :], ACT.Sqrt), m)
            m = c.on_dve(lambda e: e.reciprocal(root[:, :], root[:, :]), m)
            m = c.on_dve(lambda e: e.tensor_tensor(factor[:, :], root[:, :], inv_norm[:, :], ALU.mult), m)
            GROUP = 4
            groups = [slice(g * GROUP, (g + 1) * GROUP) for g in range(NB // GROUP)]
            scaled = [c.on_dve(lambda e: e.tensor_tensor(
                cell[:, g, :].rearrange("p b (h d) -> p (b h) d", d=CD), cell[:, g, :].rearrange("p b (h d) -> p (b h) d", d=CD),
                factor[:, g.start * CELLS:g.stop * CELLS].unsqueeze(2).to_broadcast([P, GROUP * CELLS, CD]), ALU.mult), m) for g in groups]
            for g, ready in zip(groups, scaled):
                c.on_dve(lambda e: e.scalar_tensor_tensor(resid[:, g, :], cell[:, g, :], c.gates[:, 2:3], resid[:, g, :], ALU.mult, ALU.add),
                         ready, c.gates_ready)
            c.join()


RH, RD = 16, 128
MOE, MW = 4, 256
MASKED = -3e38


def layer1_block(c, io):
    with ExitStack() as w:
        sb = lambda name, shape, dtype=F32: c.sbuf(w, name, shape, dtype)
        y = sb("b_y", [P, NB, D])
        small_in = c.tally("b_small_in")
        vectors = sb("b_vectors", [P, 8])
        head_bias = sb("b_head_bias", [P, 3, RH])
        swap_bias = sb("b_swap_bias", [P, 2, RH])
        bo = sb("b_bo", [P, D])
        for dst, src in ((vectors[:, :], io["b_vectors"]), (head_bias[:, :, :], io["b_head_bias"]), (swap_bias[:, :, :], io["b_swap_bias"])):
            c.load(dst, src, small_in)
        small = c.load(bo[:, :], io["b_bo"].broadcast_to([P, D]), small_in)
        x_split = [sb(f"b_x_{n}", [P, DK, T], F32R) for n in ("hi", "lo")]
        experts = ExpertsInput(c, io, w, y, x_split, vectors, small)
        block_attention(c, io, y, x_split, experts, vectors, head_bias, swap_bias, bo, small)
        block_experts(c, io, y, x_split, experts)


class ExpertsInput:

    def __init__(self, c, io, w, y, x_split, vectors, small):
        self.c, self.io, self.y, self.x_split, self.vectors, self.small = c, io, y, x_split, vectors, small
        sb = lambda name, shape: c.sbuf(w, f"b_{name}", shape)
        PAD = 12
        self.norm = NormWork(c, w, "b_second", columns=True)
        self.gate = sb("gate", [P, DK, MOE])
        self.b1, self.b2 = sb("b1", [P, MOE, MW // P]), sb("b2", [MOE, D])
        self.w1, self.w2 = (c.columns[:, i, :] for i in range(2))
        self.probs, self.left, self.lead, self.best = (sb(n, [P, CHUNK, s]) for n, s in (("padded", PAD), ("left", PAD), ("lead", 8), ("best", 8)))
        self.peak, self.total = sb("gate_peak", [P, CHUNK]), sb("gate_total", [P, CHUNK])
        self.comb, self.combT = sb("comb", [P, CHUNK, MOE]), sb("combT", [MOE, T])
        c.on_pool(lambda e: e.memset(self.probs[:, :, :], -1.0))
        self.pad = c.on_pool(lambda e: e.memset(self.lead[:, :, :], -1.0))
        self.x_ready, self.comb_stored, self.comb_used = {}, {}, None

    def load_weights(self):
        c, io, small_in, raw_in = self.c, self.io, self.c.tally("b_gate_in"), self.c.tally("b_experts_in")
        c.load(self.gate[:, :, :], io["b_gate"], small_in)
        c.load(self.b1[:, :, :], io["b_b1"], small_in)
        self.gate_in = c.load(self.b2[:, :], io["b_b2"], small_in)
        c.load(self.w1, io["b_w1"], raw_in)
        self.raw_in = c.load(self.w2, io["b_w2"], raw_in)

    def pieces(self, chunk, place, *ready):
        c, probs, left, lead, best, peak, total, comb, norm = (self.c, self.probs, self.left, self.lead, self.best, self.peak, self.total,
                                                              self.comb, self.norm)
        rows, cols = self.y[:, chunk * CHUNK:(chunk + 1) * CHUNK, :], slice(chunk * BANK, (chunk + 1) * BANK)
        m = yield from norm_pieces(c, norm.work, rows, norm.rows, *ready, *norm.read)
        yield
        pe, a = yield from column_pieces(c, norm.rows, norm.columns, place, m, self.small, scale=self.vectors[:, 4:6], bias=self.vectors[:, 6:8])
        bank, free = c.banks[place[0]], place[1][place[0]]
        for b in range(CHUNK):
            for k in range(DK):
                pe = c.on_pe(lambda e: e.matmul(bank[:, b * MOE:(b + 1) * MOE], norm.columns[:, k, b * P:(b + 1) * P], self.gate[:, k, :],
                                                start=k == 0, stop=k == DK - 1), a, self.gate_in, *free)
        real = probs[:, :, 0:MOE]
        wide = lambda t: t.unsqueeze(2).to_broadcast([P, CHUNK, MOE])
        m = c.on_dve(lambda e: e.tensor_copy(real, bank[:, 0:CHUNK * MOE].rearrange("p (b n) -> p b n", b=CHUNK)), pe, self.pad)
        place[1][place[0]] = [m]
        yield
        hi, lo = (t[:, :, cols] for t in self.x_split)
        a = c.on_act(lambda e: e.copy(hi, norm.columns[:, :, :]))
        self.x_ready[chunk] = c.on_pool(lambda e: e.tensor_tensor(lo, norm.columns[:, :, :], hi.bitcast(F32), ALU.subtract), a)
        norm.read = [pe, self.x_ready[chunk]]
        m = c.on_dve(lambda e: e.tensor_reduce(peak[:, :], real, AX.X, ALU.max), m)
        m = c.on_dve(lambda e: e.tensor_tensor(real, real, wide(peak[:, :]), ALU.subtract), m)
        yield
        a = c.on_act(lambda e: e.activation(real, real, ACT.Exp), m)
        yield
        m = c.on_dve(lambda e: e.tensor_reduce(total[:, :], real, AX.X, ALU.add), a)
        m = c.on_dve(lambda e: e.reciprocal(total[:, :], total[:, :]), m)
        m = c.on_dve(lambda e: e.tensor_tensor(real, real, wide(total[:, :]), ALU.mult), m)
        for b in range(CHUNK):
            m8 = c.on_dve(lambda e: e.max(best[:, b, :], probs[:, b, :]), m)
        m = c.on_dve(lambda e: e.tensor_copy(lead[:, :, 0:2], best[:, :, 0:2]), m8)
        for b in range(CHUNK):
            m8 = c.on_dve(lambda e: e.match_replace(left[:, b, :], lead[:, b, :], probs[:, b, :], -2.0), m)
        m = c.on_dve(lambda e: e.tensor_tensor(comb[:, :, :], real, wide(best[:, :, 0]), ALU.subtract), m8, self.comb_used)
        yield
        a = c.on_act(lambda e: e.activation(comb[:, :, :], comb[:, :, :], ACT.Exp), m)
        yield
        m = c.on_dve(lambda e: e.scalar_tensor_tensor(comb[:, :, :], left[:, :, 0:MOE], -1.5, comb[:, :, :], ALU.is_lt, ALU.mult), a)
        m = c.on_dve(lambda e: e.tensor_reduce(total[:, :], comb[:, :, :], AX.X, ALU.add), m)
        m = c.on_dve(lambda e: e.reciprocal(total[:, :], total[:, :]), m)
        m = c.on_dve(lambda e: e.tensor_tensor(comb[:, :, :], comb[:, :, :], wide(total[:, :]), ALU.mult), m)
        yield
        bank, free = c.banks[place[0]], place[1][place[0]]
        for b in range(CHUNK):
            pe = c.on_pe(lambda e: e.transpose(bank[0:MOE, b * P:(b + 1) * P], comb[:, b, :], c.ident[:, :]), m, *free)
        self.comb_used = pe
        a = c.on_act(lambda e: e.copy(self.combT[:, cols], bank[0:MOE, :]), pe)
        place[1][place[0]] = [a]
        self.comb_stored[chunk] = c.load(self.io["b_comb_rows"][:, cols], self.combT[:, cols], c.tally(f"b_comb_stored{chunk}"), a)


def block_attention(c, io, y, x_split, experts, vectors, head_bias, swap_bias, bo, small):
    resid = c.resid
    SCALE = 1.0 / float(np.sqrt(RD))
    with ExitStack() as w:
        sb = lambda name, shape, dtype=F32: c.sbuf(w, name, shape, dtype)
        GROUP = 4
        NQK, NV = 2 * DK * RD, DK * GROUP * RD
        raw_qk, raw_o = [sb(f"b_raw_qk{i}", [P, NQK]) for i in range(3)], [sb(f"b_raw_o{i}", [P, D]) for i in range(3)]
        raw_v = [sb(f"b_raw_v{i}", [P, NV]) for i in range(2)]
        pair = lambda name, n: [sb(f"b_{name}_{half}", [P, n], F32R) for half in ("hi", "lo")]
        split_qk, split_o, split_v = ([pair(f"{name}{i}", n) for i in range(2)] for name, n in (("qk", NQK), ("o", D), ("vw", NV)))
        rope, mask = sb("b_rope", [P, 2, S]), sb("b_mask", [P, S])
        qk_in, o_in, v_in = ([c.tally(f"b_{n}_in{i}") for i in range(count)] for n, count in (("qk", 3), ("o", 3), ("v", 2)))
        steps = NCHUNK * RH
        loaded, raw_free, split_done, split_free = {}, {}, {}, {}
        kinds = {"qk": (raw_qk, split_qk, qk_in, io["b_wqk"], RH), "o": (raw_o, split_o, o_in, io["b_wo"], RH),
                 "v": (raw_v, split_v, v_in, io["b_wv"], RH // GROUP)}

        def load_weights(kind, n):
            raw, _, tallies, src, period = kinds[kind]
            r = n % len(raw)
            loaded[kind, n] = c.load(raw[r][:, :], src[n % period], tallies[r], raw_free.get((kind, r)))

        def split_weights(kind, n):
            raw, split = kinds[kind][:2]
            r, i = n % len(raw), n % 2
            hi, lo = (t[:, :] for t in split[i])
            m = c.on_dve(lambda e: e.tensor_copy(hi, raw[r][:, :]), loaded[kind, n], split_free.get((kind, i)))
            rest_to_split.append((kind, n, r, hi, lo, m))

        def split_rest():
            for kind, n, r, hi, lo, m in rest_to_split:
                split_done[kind, n] = raw_free[kind, r] = c.on_pool(
                    lambda e: e.tensor_tensor(lo, kinds[kind][0][r][:, :], hi.bitcast(F32), ALU.subtract), m)
            rest_to_split.clear()

        rest_to_split = []

        load_weights("qk", 0)
        load_weights("v", 0)
        tables_in = c.tally("b_tables_in")
        c.load(rope[:, :, :], io["b_rope"], tables_in)
        tables = c.load(mask[:, :], io["b_mask"], tables_in)
        for n in range(3):
            if n >= 1:
                load_weights("qk", n)
            load_weights("o", n)
        load_weights("v", 1)

        first = NormWork(c, w, "b_first", columns=True)
        x_ready, with_bo = {}, {}

        def input_pieces(chunk, place):
            rows, cols = slice(chunk * CHUNK, (chunk + 1) * CHUNK), slice(chunk * BANK, (chunk + 1) * BANK)
            m = yield from norm_pieces(c, first.work, resid[:, rows, :], y[:, rows, :], c.x_in[chunk * CHUNK])
            yield
            m = yield from norm_pieces(c, first.work, y[:, rows, :], first.rows, m, *first.read)
            yield
            pe, a = yield from column_pieces(c, first.rows, first.columns, place, m, small, scale=vectors[:, 0:2], bias=vectors[:, 2:4])
            hi, lo = (t[:, :, cols] for t in x_split)
            a = c.on_act(lambda e: e.copy(hi, first.columns[:, :, :]), a)
            on = c.on_dve if chunk == 0 else c.on_pool
            x_ready[chunk] = on(lambda e: e.tensor_tensor(lo, first.columns[:, :, :], hi.bitcast(F32), ALU.subtract), a)
            yield
            with_bo[chunk] = c.on_pool(lambda e: e.tensor_tensor(y[:, rows, :], y[:, rows, :], bo[:, :].unsqueeze(1).to_broadcast([P, CHUNK, D]),
                                                                 ALU.add), m, small)
            first.read = [pe, x_ready[chunk]]

        with ExitStack() as w2:
            s2 = lambda name, shape, dtype=F32: c.sbuf(w2, name, shape, dtype)
            v = [s2(f"b_v{i}", [P, CHUNK, GROUP * RD]) for i in range(2)]
            turned = [s2(f"b_turned{i}", [P, 2, BANK]) for i in range(2)]
            straight = [s2(f"b_straight{i}", [P, 2, BANK]) for i in range(2)]
            probs = [s2(f"b_probs{i}", [P, CHUNK, S]) for i in range(3)]
            peak, peak_scaled, total, inv = ([s2(f"b_{n}{i}", [P, CHUNK]) for i in range(2)] for n in ("peak", "peak_scaled", "total", "inv"))
            probsT = [s2(f"b_probsT{i}", [P, BANK]) for i in range(2)]
            outT = [[s2(f"b_outT_{n}{i}", [P, BANK], F32R) for n in ("hi", "lo")] for i in range(2)]
            Q, K, V, SC, PT, OT, OUT = 0, 1, 2, 3, 4, 5, 6
            free = {n: [] for n in range(8)}
            v_ready, v_used, rotated, scored, prob_ready, out_ready, done = {}, {}, {}, {}, {}, {}, {}

            def values(n):
                group, tile = divmod(n, CHUNK)
                chunk, g = divmod(group, RH // GROUP)
                b = chunk * CHUNK + tile
                for k in range(DK):
                    pe = product(c, c.banks[V][:, :], [t[:, k, b * P:(b + 1) * P] for t in x_split],
                                 [t[:, k * BANK:(k + 1) * BANK] for t in split_v[group % 2]], k == 0, k == DK - 1,
                                 x_ready[chunk], split_done["v", group], *free[V])
                split_free["v", group % 2] = pe
                v_ready[group] = a = c.on_act(lambda e: e.copy(v[group % 2][:, tile, :], c.banks[V][:, :]), pe, *v_used.get(group - 2, ()))
                free[V] = [a]

            def queries_keys(n):
                chunk, h = divmod(n, RH)
                i = n % 2
                by_batch = lambda t: t.rearrange("p (b s) -> p b s", b=CHUNK)
                wide = lambda which: rope[:, which, :].unsqueeze(1).to_broadcast([P, CHUNK, S])
                both[n] = []
                for which, bank in ((0, Q), (1, K)):
                    for k in range(DK):
                        at = (which * DK + k) * RD
                        pe = product(c, c.banks[bank][:, :], [t[:, at:at + RD] for t in split_qk[i]],
                                     [t[:, k, chunk * BANK:(chunk + 1) * BANK] for t in x_split], k == 0, k == DK - 1,
                                     x_ready[chunk], split_done["qk", n], *free[bank])
                        split_free["qk", i] = pe
                    half = P // 2
                    for dst, src in ((0, half), (half, 0)):
                        a = c.on_act(lambda e: e.activation(turned[i][dst:dst + half, which, :], c.banks[bank][src:src + half, :], ACT.Identity,
                                                            bias=swap_bias[dst:dst + half, which, h:h + 1]), pe, small, scored.get(n - 2))
                    m = c.on_dve(lambda e: e.scalar_tensor_tensor(by_batch(straight[i][:, which, :]), by_batch(c.banks[bank][:, :]),
                                                                  head_bias[:, which, h:h + 1], wide(0), ALU.add, ALU.mult),
                                 pe, a, tables, scored.get(n - 2))
                    free[bank] = [a, m]
                    turned_ready = m, c.on_pool(lambda e: e.tensor_tensor(by_batch(turned[i][:, which, :]), by_batch(turned[i][:, which, :]), wide(1), ALU.mult), a, tables)
                    both[n].append(turned_ready)

            def rotate(n):
                i = n % 2
                for which in range(2):
                    rotated[n] = c.on_dve(lambda e: e.tensor_tensor(straight[i][:, which, :], straight[i][:, which, :], turned[i][:, which, :], ALU.add),
                                          *both[n][which])

            def softmax(n):
                i = n % 2
                for b in range(CHUNK):
                    pe = c.on_pe(lambda e: e.matmul(c.banks[SC][:, b * S:(b + 1) * S], straight[i][:, 0, b * S:(b + 1) * S],
                                                    straight[i][:, 1, b * S:(b + 1) * S], start=True, stop=True), rotated[n], *free[SC])
                scored[n] = pe
                by_batch = c.banks[SC][:, :].rearrange("p (b s) -> p b s", b=CHUNK)
                m = c.on_dve(lambda e: e.tensor_tensor(probs[n % 3][:, :, :], by_batch, mask[:, :].unsqueeze(1).to_broadcast([P, CHUNK, S]), ALU.add),
                             pe, tables, prob_used.get(n - 3))
                free[SC] = [m]
                m = c.on_dve(lambda e: e.tensor_reduce(peak[i][:, :], probs[n % 3][:, :, :], AX.X, ALU.max, negate=True), m)
                peak_ready[n] = c.on_dve(lambda e: e.tensor_scalar(peak_scaled[i][:, :], peak[i][:, :], SCALE, None, ALU.mult), m)

            def exponentials(n):
                i = n % 2
                for b in range(CHUNK):
                    a = c.on_act(lambda e: e.activation(probs[n % 3][:, b, :], probs[n % 3][:, b, :], ACT.Exp, scale=SCALE, bias=peak_scaled[i][:, b:b + 1],
                                                        accum_out=total[i][:, b:b + 1]), peak_ready[n])
                exp_ready[n] = a

            def normalise(n):
                i = n % 2
                m = c.on_dve(lambda e: e.reciprocal(inv[i][:, :], total[i][:, :]), exp_ready[n])
                prob_ready[n] = c.on_pool(lambda e: e.tensor_tensor(probs[n % 3][:, :, :], probs[n % 3][:, :, :],
                                                                    inv[i][:, :].unsqueeze(2).to_broadcast([P, CHUNK, S]), ALU.mult), m)

            y_ready, both = {}, {}
            prob_used, peak_ready, exp_ready = {}, {}, {}

            def transpose_probs(n):
                i = n % 2
                for b in range(CHUNK):
                    pe = c.on_pe(lambda e: e.transpose(c.banks[PT][:, b * S:(b + 1) * S], probs[n % 3][:, b, :], c.ident[:, :]), prob_ready[n], *free[PT])
                prob_used[n] = pe
                if n % 2:
                    a = c.on_act(lambda e: e.copy(probsT[i][:, :], c.banks[PT][:, :]), pe, weighed.get(n - 2))
                else:
                    a = c.on_dve(lambda e: e.tensor_copy(probsT[i][:, :], c.banks[PT][:, :]), pe, weighed.get(n - 2))
                free[PT] = [a]
                transposed[n] = a

            transposed, weighed = {}, {}

            def weigh_values(n):
                chunk, h = divmod(n, RH)
                group, i = n // GROUP, n % 2
                for b in range(CHUNK):
                    pe = c.on_pe(lambda e: e.matmul(c.banks[OT][:, b * S:(b + 1) * S], v[group % 2][:, b, (h % GROUP) * RD:(h % GROUP + 1) * RD],
                                                    probsT[i][:, b * S:(b + 1) * S], start=True, stop=True), transposed[n], v_ready[group], *free[OT])
                v_used[group], weighed[n] = [pe], pe
                hi, lo = outT[i]
                a = c.on_act(lambda e: e.activation(hi[:, :], c.banks[OT][:, :], ACT.Identity, bias=head_bias[:, 2, h:h + 1]), pe, done.get(n - 2))
                m = c.on_dve(lambda e: e.scalar_tensor_tensor(lo[:, :], c.banks[OT][:, :], head_bias[:, 2, h:h + 1], hi[:, :].bitcast(F32),
                                                              ALU.add, ALU.subtract), a)
                free[OT], out_ready[n] = [m], m

            def project(n):
                chunk, h = divmod(n, RH)
                i = n % 2
                for b in range(CHUNK):
                    bank = OUT + b // 2
                    pe = product(c, c.banks[bank][:, (b % 2) * D:(b % 2 + 1) * D], [t[:, b * S:(b + 1) * S] for t in outT[i]],
                                 [t[:, :] for t in split_o[i]], h == 0 and b % 2 == 0, h == RH - 1, out_ready[n], split_done["o", n], *free[bank])
                done[n] = split_free["o", i] = pe
                if h == RH - 1:
                    for bank in (OUT, OUT + 1):
                        rows = y[:, chunk * CHUNK + 2 * (bank - OUT):chunk * CHUNK + 2 * (bank - OUT) + 2, :]
                        free[bank] = [c.on_dve(lambda e: e.tensor_tensor(rows, rows, c.banks[bank][:, :].rearrange("p (b n) -> p b n", b=2), ALU.add),
                                               pe, with_bo[chunk])]
                    y_ready[chunk] = free[OUT] + free[OUT + 1]

            groups = steps // GROUP
            place = (V, free)
            first_input = input_pieces(0, place)
            for _ in range(6):
                next(first_input)
            for kind in ("qk", "v"):
                split_weights(kind, 0)
            split_rest()
            for _ in first_input:
                pass
            behind = []
            for n in range(steps + 5):
                chunk, h = divmod(n, RH)
                if n == RH:
                    experts.load_weights()
                if h == 0 and chunk + 1 < NCHUNK:
                    behind.append(input_pieces(chunk + 1, place))
                if h == 5 and chunk >= 1:
                    behind.append(experts.pieces(chunk - 1, place, *y_ready[chunk - 1], (c.pe, c.pe.count)))
                if n + 1 < steps:
                    split_weights("qk", n + 1)
                split_rest()
                if 4 <= n < steps + 4:
                    split_weights("o", n - 4)
                if n % GROUP == 0 and n // GROUP + 1 < groups:
                    split_weights("v", n // GROUP + 1)
                if 2 <= n <= steps + 1:
                    exponentials(n - 2)
                if n < steps:
                    queries_keys(n)
                if 2 <= n <= steps + 1:
                    normalise(n - 2)
                split_rest()
                if n + 3 < steps:
                    load_weights("qk", n + 3)
                if 4 <= n <= steps:
                    load_weights("o", n - 1)
                if n % GROUP == 0 and n // GROUP + 2 < groups:
                    load_weights("v", n // GROUP + 2)
                if 1 <= n <= steps:
                    softmax(n - 1)
                if n < steps:
                    rotate(n)
                    values(n)
                if 3 <= n < steps + 3:
                    transpose_probs(n - 3)
                if 4 <= n < steps + 4:
                    weigh_values(n - 4)
                behind = [pieces for pieces in behind if next(pieces, "ended") != "ended"]
                if 5 <= n:
                    project(n - 5)
            for pieces in behind:
                for _ in pieces:
                    pass
            experts.y_ready = y_ready[NCHUNK - 1]
            c.join()


def block_experts(c, io, y, x_split, experts):
    resid, b1, b2, combT = c.resid, experts.b1, experts.b2, experts.combT
    with ExitStack() as w:
        sb = lambda name, shape, dtype=F32: c.sbuf(w, name, shape, dtype)
        comb_wide = sb("b_comb_wide", [P, MOE, T])
        w1_split = [sb(f"b_w1_{n}", [P, MOE, DK, MW], F32R) for n in ("hi", "lo")]
        w2_split = [sb(f"b_w2_{n}", [P, MOE, MW // P, D], F32R) for n in ("hi", "lo")]
        w1_ready, w2_ready = {}, {}
        for e_ in range(MOE):
            for raw, dst, marks in ((experts.w1, w1_split, w1_ready), (experts.w2, w2_split, w2_ready)):
                whole = raw.rearrange("p (e k n) -> p e k n", e=MOE, k=DK)[:, e_]
                marks[e_] = split2(c, c.on_act, whole, *(t[:, e_, :, :] for t in dst), experts.raw_in)
        comb_in = {}

        def load_comb(chunk):
            cols, tally = slice(chunk * BANK, (chunk + 1) * BANK), c.tally(f"b_comb_in{chunk}")
            for e_ in range(MOE):
                comb_in[chunk] = c.load(comb_wide[:, e_, cols], io["b_comb_rows"][e_:e_ + 1, cols].broadcast_to([P, BANK]), tally,
                                        experts.comb_stored[chunk])

        for chunk in range(NCHUNK - 1):
            load_comb(chunk)

        with ExitStack() as w3:
            s3 = lambda name, shape, dtype=F32: c.sbuf(w3, name, shape, dtype)
            act = [s3(f"b_act{i}", [P, BANK]) for i in range(2)]
            hidden = [s3(f"b_hidden{i}", [P, BANK]) for i in range(2)]
            hidden_split = [[s3(f"b_hidden_{n}{i}", [P, BANK], F32R) for n in ("hi", "lo")] for i in range(3)]
            MB = MW // P
            steps = [(chunk, e_, mb) for chunk in range(NCHUNK) for e_ in range(MOE) for mb in range(MB)]
            free = {n: [] for n in range(8)}
            ready, used, weighed = {}, {}, {}
            out_stored = c.tally("out_stored")

            def up(n):
                chunk, e_, mb = steps[n]
                i, cols = n % 2, slice(chunk * BANK, (chunk + 1) * BANK)
                for k in range(DK):
                    pe = product(c, c.banks[i][:, :], [t[:, e_, k, mb * P:(mb + 1) * P] for t in w1_split], [t[:, k, cols] for t in x_split],
                                 k == 0, k == DK - 1, experts.x_ready[chunk], w1_ready[e_], *free[i])
                a = c.on_act(lambda e: e.activation(act[i][:, :], c.banks[i][:, :], ACT.Gelu, bias=b1[:, e_, mb:mb + 1]), pe, weighed.get(n - 2))
                free[i] = [a]
                weighed[n] = c.on_dve(lambda e: e.tensor_tensor(hidden[i][:, :], act[i][:, :], comb_wide[:, e_, cols], ALU.mult), a, comb_in[chunk],
                                      ready.get(n - 2))

            def split_hidden(n):
                ready[n] = split2(c, c.on_act, hidden[n % 2][:, :], *(t[:, :] for t in hidden_split[n % 3]), weighed[n], used.get(n - 3))

            def down(n):
                chunk, e_, mb = steps[n]
                i, base = n % 2, 4 + 2 * (chunk % 2)
                for t in range(CHUNK):
                    bank = base + t // 2
                    out = c.banks[bank][:, (t % 2) * D:(t % 2 + 1) * D]
                    tok = slice((chunk * CHUNK + t) * P, (chunk * CHUNK + t + 1) * P)
                    if e_ == 0 and mb == 0:
                        c.on_pe(lambda e: e.matmul(out, combT[:, tok], b2[:, :], start=t % 2 == 0, stop=False, skip_group_check=True), *free[bank])
                    pe = product(c, out, [v[:, t * P:(t + 1) * P] for v in hidden_split[n % 3]], [v[:, e_, mb, :] for v in w2_split],
                                 False, n % (MOE * MB) == MOE * MB - 1, ready[n], w2_ready[e_])
                used[n] = pe
                if n % (MOE * MB) == MOE * MB - 1:
                    for bank in (base, base + 1):
                        b = chunk * CHUNK + 2 * (bank - base)
                        rows, x = y[:, b:b + 2, :], resid[:, b:b + 2, :]
                        m = c.on_dve(lambda e: e.tensor_tensor(rows, rows, c.banks[bank][:, :].rearrange("p (b n) -> p b n", b=2), ALU.add), pe)
                        free[bank] = [m]
                        m = c.on_dve(lambda e: e.scalar_tensor_tensor(x, rows, c.gates[:, 3:4], x, ALU.mult, ALU.add), m, c.gates_ready)
                        c.out_mark = c.load(io["out"][b:b + 2, :, :].rearrange("b p n -> p b n"), x, out_stored, m)

            LAG = 2
            behind = [experts.pieces(NCHUNK - 1, (2, free), *experts.y_ready)]
            for n in range(len(steps) + LAG):
                if n >= 1 and behind and next(behind[0], "ended") == "ended":
                    behind = []
                    load_comb(NCHUNK - 1)
                if 1 <= n <= len(steps):
                    split_hidden(n - 1)
                if n < len(steps):
                    up(n)
                if n >= LAG:
                    down(n - LAG)


def program(nc, io):
    with ExitStack() as stack:
        c = Core(nc, stack)
        sb = lambda name, shape, dtype=F32: c.sbuf(stack, name, shape, dtype)
        c.resid = sb("resid", [P, NB, D])
        c.columns = sb("columns", [P, DK, T])
        c.ident, c.gates = sb("ident", [P, P]), sb("gates", [P, 4])
        context, c.ctxT = ExitStack(), None
        c.ctx = c.sbuf(context, "ctx", [P, NB, D])
        c.x_in, c.ctx_in, c.columns_ready = [], [], {}

        def load_inputs(chunk):
            for name, dst, marks in (("x", c.resid, c.x_in), ("ctx", c.ctx, c.ctx_in)):
                b = slice(chunk * CHUNK, (chunk + 1) * CHUNK)
                marks += [c.load(dst[:, b, :], io[name][b, :, :].rearrange("b p n -> p b n"), c.tally(f"{name}_in{chunk}"))] * CHUNK

        c.load_inputs = load_inputs
        load_inputs(0)
        gates_in = c.load(c.gates[:, :], io["gates"], c.tally("gates_in"))
        c.gates_ready = c.on_act(lambda e: e.activation(c.gates[:, :], c.gates[:, :], ACT.Tanh), gates_in)
        zero = c.on_pool(lambda e: e.memset(c.ident[:, :], 0.0))
        c.ident_ready = c.on_pool(lambda e: e.affine_select(out=c.ident[:, :], in_=c.ident[:, :], compare_op=ALU.not_equal, fill=1.0,
                                                            base=0, pattern=[[-1, P]], channel_multiplier=1), zero)
        for stage in (layer0_attention, layer0_experts, layer1_mlstm):
            if stage is not layer0_attention and c.ctxT is None:
                c.ctxT = c.sbuf(context, "ctxT", [P, DK, T])
            stage(c, io)
        context.close()
        layer1_block(c, io)
        c.need(nc.sync, c.out_mark)


def layouts(a):
    from_name = lambda n: np.asarray(a[n])
    out = {"x": from_name("x"), "ctx": from_name("ctx_2048")}
    gates = np.concatenate([from_name("g_xattn")[:, None], from_name("g_ffn")[:, None]], 1).reshape(4)
    out["gates"] = np.broadcast_to(gates, (P, 4))
    turned = lambda t: t.reshape((HEADS, HD) + t.shape[1:]).swapaxes(0, 1).reshape(t.shape)
    for n in "qkvo":
        wT = from_name(f"L0_xattn_W{n}")
        out[f"a_w{n}T"] = (turned(wT) if n in "qk" else wT).T
    out["a_bias"] = np.stack([turned(from_name(f"L0_xattn_b{n}")) if n in "qk" else from_name(f"L0_xattn_b{n}") for n in "qkvo"], 1)
    gu = from_name("L0_ffn_gate_up_proj").reshape(PAIRS, 2, 2, WIDTH, DK, P)
    gu = gu.transpose(0, 5, 4, 2, 1, 3).reshape(PAIRS, P, DK * 2 * P)
    down = from_name("L0_ffn_down_proj").reshape(PAIRS, 2, D, WIDTH).transpose(0, 1, 3, 2).reshape(PAIRS, P, D)
    out["e_weights"] = np.concatenate([gu, down], 2)
    shared = np.stack([from_name("L0_ffn_shared_gate_w"), from_name("L0_ffn_shared_up_w")]).reshape(2, WIDTH, DK, P)
    out["e_shared_gate_up"] = shared.transpose(3, 2, 0, 1).reshape(P, DK * 2 * WIDTH)
    out["e_shared_down"] = from_name("L0_ffn_shared_down_w").T
    router = np.concatenate([from_name("L0_ffn_router_w"), from_name("L0_ffn_shared_expert_gate_w")])
    out["e_router"] = router.reshape(EXPERTS + 1, DK, P).transpose(2, 1, 0)
    out["m_ctxT"] = out["ctx"].transpose(2, 0, 1).reshape(D, T)
    gate_w, gate_bias = np.zeros((3 * D, 2, SPAN), np.float32), np.zeros((P // SPAN, SPAN, 2), np.float32)
    for i, n in enumerate("if"):
        gate_w[:, i, 0:CELLS], gate_bias[:, 0:CELLS, i] = from_name(f"L1_xattn_W{n}"), from_name(f"L1_xattn_b{n}")
    out["m_gate_w"] = gate_w.reshape(3 * DK, P, 2 * SPAN).transpose(1, 0, 2)
    out["m_gate_bias"] = gate_bias.reshape(P, 2)
    head_of = np.arange(P)[:, None] // CD == np.arange(CELLS // DK)[None, :]
    out["m_head_mask"] = head_of.astype(np.float32) / 4
    out["m_ln_scale"] = from_name("L1_xattn_ln_scale").reshape(1, D)
    by_block = lambda v: v.reshape(DK, P).T
    out["b_vectors"] = np.concatenate([by_block(from_name(f"L1_ffn_{n}")) for n in ("ln1_w", "ln1_b", "ln2_w", "ln2_b")], 1)
    biases = np.stack([from_name(f"L1_ffn_b{n}").reshape(RH, RD) for n in "qkv"])
    out["b_head_bias"] = biases.transpose(2, 0, 1)
    swapped = np.concatenate([biases[:2, :, RD // 2:], biases[:2, :, :RD // 2]], 2)
    out["b_swap_bias"] = swapped.transpose(2, 0, 1)
    out["b_bo"] = from_name("L1_ffn_bo").reshape(1, D)
    qk = np.stack([from_name("L1_ffn_wq"), from_name("L1_ffn_wk")]).reshape(2, DK, P, RH, RD)
    out["b_wqk"] = qk.transpose(3, 2, 0, 1, 4).reshape(RH, P, 2 * DK * RD)
    out["b_wv"] = from_name("L1_ffn_wv").reshape(DK, P, RH // 4, 4 * RD).transpose(2, 1, 0, 3).reshape(RH // 4, P, DK * 4 * RD)
    out["b_wo"] = from_name("L1_ffn_wo").reshape(RH, RD, D)
    f32 = np.float32
    inv_freq = (f32(1.0) / f32(10000.0) ** (np.arange(0, RD, 2, dtype=f32) / f32(RD))).astype(f32)
    angle = np.arange(S, dtype=f32)[None, :] * np.concatenate([inv_freq, inv_freq])[:, None]
    sign = np.where(np.arange(RD) < RD // 2, f32(-1), f32(1))[:, None]
    out["b_rope"] = np.stack([np.cos(angle), np.sin(angle) * sign], 1).astype(f32)
    out["b_mask"] = np.where(np.arange(S)[None, :] > np.arange(S)[:, None], f32(MASKED), f32(0))
    out["b_gate"] = from_name("L1_ffn_w_gate").reshape(DK, P, MOE).transpose(1, 0, 2)
    out["b_w1"] = from_name("L1_ffn_we1").reshape(MOE, DK, P, MW).transpose(2, 0, 1, 3).reshape(P, MOE * DK * MW)
    out["b_w2"] = from_name("L1_ffn_we2").reshape(MOE, MW // P, P, D).transpose(2, 0, 1, 3).reshape(P, MOE * MW // P * D)
    out["b_b1"] = from_name("L1_ffn_be1").reshape(MOE, MW // P, P).transpose(2, 0, 1)
    out["b_b2"] = from_name("L1_ffn_be2")
    return {n: np.ascontiguousarray(v) for n, v in out.items()}


SCRATCH = {
    "b_comb_rows": ((MOE, T), F32),
    "m_negpeak": ((CELLS, T), F32),
    "e_combT": ((EXPERTS + 1, T), F32),
    "a_q_parts": ((NB, 3, P, D), BF16),
    "a_k_parts": ((NB, 3, P, D), BF16),
}


def kernel(**inputs):
    import concourse.bacc as _bacc
    from concourse.bass_utils import run_bass_kernel_spmd as _run

    nc = _bacc.Bacc("TRN2", target_bir_lowering=False, num_devices=1)
    arrays, io = layouts(inputs), {}
    for n, v in arrays.items():
        io[n] = nc.dram_tensor("in_" + n, v.shape, mybir.dt.from_np(v.dtype), kind="ExternalInput").ap()
    io["out"] = nc.dram_tensor("out", (NB, S, D), F32, kind="ExternalOutput").ap()
    for n, (shape, dtype) in SCRATCH.items():
        io[n] = nc.dram_tensor(n, shape, dtype).ap()
    program(nc, io)
    return _run(nc, [{"in_" + n: v for n, v in arrays.items()}], core_ids=[0]).results[0]["out"]
```
